# Optimizing a Trainium2 kernel written in Bass

```python
import numpy as np
import jax
import jax.numpy as jnp

def _softmax(x, axis=-1):
    return jax.nn.softmax(x, axis=axis)

def _gelu(x):
    return jax.nn.gelu(x, approximate=True)

def _silu(x):
    return jax.nn.silu(x)

def _sigmoid(x):
    return jax.nn.sigmoid(x)

def _layernorm(x, axis=-1, eps=1e-05):
    m = jnp.mean(x, axis=axis, keepdims=True)
    v = jnp.var(x, axis=axis, keepdims=True)
    return (x - m) / jnp.sqrt(v + eps)

def _scatter_add(tgt, idx, src, axis=0):
    return tgt.at[idx].add(src)

def _segment_sum(src, seg, n):
    return jax.ops.segment_sum(src, seg, n)
kernel_name = 'mk_hybrid_d2_jaxref_r8_63b5c7'

def setup_inputs(seed: int=0):
    np.random.seed(seed)
    _w = jnp.asarray

    def _L0_attn_a_setup():
        import jax, jax.numpy as jnp
        import numpy as np
        D_MODEL = 256
        NUM_HEADS = 16
        THETA = 10000.0

        def _rope(t, cos, sin):
            x_even = t[..., 0::2]
            x_odd = t[..., 1::2]
            rot = jnp.stack((-x_odd, x_even), axis=-1).reshape(t.shape)
            return t * cos + rot * sin
        key = jax.random.key(seed)
        ks = jax.random.split(key, 5)
        bs, S, d = (4, 256, D_MODEL)
        std = (2.0 / (d + d)) ** 0.5
        x = jax.random.normal(ks[0], (bs, S, d), dtype=jnp.float32)
        wq = jax.random.normal(ks[1], (d, d), dtype=jnp.float32) * std
        wk = jax.random.normal(ks[2], (d, d), dtype=jnp.float32) * std
        wv = jax.random.normal(ks[3], (d, d), dtype=jnp.float32) * std
        wo = jax.random.normal(ks[4], (d, d), dtype=jnp.float32) * std
        return {'x': x, 'wq': wq, 'wk': wk, 'wv': wv, 'wo': wo}
    _L0_attn_a_in = _L0_attn_a_setup()

    def _L0_attn_b_setup():
        import jax, jax.numpy as jnp
        import numpy as np
        DIM = 256
        N_HEADS = 16
        HEAD_DIM = DIM // N_HEADS
        key = jax.random.key(seed)
        kx, kqkv, kout = jax.random.split(key, 3)
        x = jax.random.normal(kx, (2, 256, DIM), dtype=jnp.float32)
        W_qkv = jax.random.normal(kqkv, (3 * DIM, DIM), dtype=jnp.float32) * DIM ** (-0.5)
        W_out = jax.random.normal(kout, (DIM, DIM), dtype=jnp.float32) * DIM ** (-0.5)
        return {'x': x, 'W_qkv': W_qkv, 'W_out': W_out}
    _L0_attn_b_in = _L0_attn_b_setup()

    def _L0_ffn_setup():
        import jax, jax.numpy as jnp
        import numpy as np
        HIDDEN = 256
        INTER = 1024
        SCALE = 64.0

        def fwht(x):
            orig_shape = x.shape
            n = orig_shape[-1]
            x = x.reshape(-1, n)
            h = 1
            while h < n:
                x = x.reshape(-1, n // (2 * h), 2, h)
                a, b = (x[:, :, 0, :], x[:, :, 1, :])
                x = jnp.stack([a + b, a - b], axis=2).reshape(-1, n)
                h *= 2
            return (x / jnp.sqrt(jnp.asarray(n, x.dtype))).reshape(orig_shape)
        key = jax.random.key(seed)
        ks = jax.random.split(key, 8)
        inp = jax.random.normal(ks[0], (4, 256, HIDDEN), dtype=jnp.float32)
        SU_ug = jnp.where(jax.random.bernoulli(ks[1], 0.5, (HIDDEN,)), 1.0, -1.0).astype(jnp.float32)
        SU_dp = jnp.where(jax.random.bernoulli(ks[2], 0.5, (INTER,)), 1.0, -1.0).astype(jnp.float32)
        Wscale_ug = jax.random.uniform(ks[3], (2 * INTER,), jnp.float32, 0.5, 1.5)
        Wscale_dp = jax.random.uniform(ks[4], (HIDDEN,), jnp.float32, 0.5, 1.5)
        W_up = jax.random.normal(ks[5], (INTER, HIDDEN), dtype=jnp.float32) * 0.02
        W_gate = jax.random.normal(ks[6], (INTER, HIDDEN), dtype=jnp.float32) * 0.02
        W_down = jax.random.normal(ks[7], (HIDDEN, INTER), dtype=jnp.float32) * 0.02
        return {'input': inp, 'SU_ug': SU_ug, 'SU_dp': SU_dp, 'Wscale_ug': Wscale_ug, 'Wscale_dp': Wscale_dp, 'W_up': W_up, 'W_gate': W_gate, 'W_down': W_down}
    _L0_ffn_in = _L0_ffn_setup()

    def _L1_attn_a_setup():
        import jax, jax.numpy as jnp
        import numpy as np
        NH = 16
        key = jax.random.key(seed)
        ks = jax.random.split(key, 5)
        B, T, D = (2, 256, 256)
        scale = 0.02
        return {'x': jax.random.normal(ks[0], (B, T, D), dtype=jnp.float32), 'Wq': jax.random.normal(ks[1], (D, D), dtype=jnp.float32) * scale, 'Wk': jax.random.normal(ks[2], (D, D), dtype=jnp.float32) * scale, 'Wv': jax.random.normal(ks[3], (D, D), dtype=jnp.float32) * scale, 'Wo': jax.random.normal(ks[4], (D, D), dtype=jnp.float32) * scale}
    _L1_attn_a_in = _L1_attn_a_setup()

    def _L1_attn_b_setup():
        import jax, jax.numpy as jnp
        import numpy as np
        N_EMBD = 256
        EXPAND = 2
        D_INNER = N_EMBD * EXPAND
        D_STATE = 128
        N_HEADS = D_INNER // D_STATE
        HEAD_DIM = D_INNER // N_HEADS
        N_GROUPS = 1
        D_CONV = 4
        CHUNK = 64
        N_LAYERS = 48
        GS = N_GROUPS * D_STATE
        PROJ = 2 * D_INNER + N_HEADS + 2 * GS
        RMS_EPS = 1e-06

        def _ssd_scan(A, B, C, dt, x, chunk_size=CHUNK):
            batch, seq_len, n_heads, P = x.shape
            G, N = (B.shape[2], B.shape[3])
            Hg = n_heads // G
            Q = chunk_size
            pad_len = -seq_len % Q
            if pad_len:
                A = jnp.pad(A, ((0, 0), (0, pad_len), (0, 0)))
                B = jnp.pad(B, ((0, 0), (0, pad_len), (0, 0), (0, 0)))
                C = jnp.pad(C, ((0, 0), (0, pad_len), (0, 0), (0, 0)))
                dt = jnp.pad(dt, ((0, 0), (0, pad_len), (0, 0)))
                x = jnp.pad(x, ((0, 0), (0, pad_len), (0, 0), (0, 0)))
            T_pad = seq_len + pad_len
            n_chunks = T_pad // Q
            A_c = A.reshape(batch, n_chunks, Q, n_heads)
            B_c = B.reshape(batch, n_chunks, Q, G, N)
            C_c = C.reshape(batch, n_chunks, Q, G, N)
            dt_c = dt.reshape(batch, n_chunks, Q, n_heads)
            x_c = x.reshape(batch, n_chunks, Q, n_heads, P)
            log_a = A_c * dt_c
            cum_log_a = jnp.cumsum(log_a, axis=2)
            chunk_log_decay = cum_log_a[:, :, -1, :]
            log_diff = cum_log_a[:, :, :, None, :] - cum_log_a[:, :, None, :, :]
            causal = jnp.tril(jnp.ones((Q, Q), dtype=jnp.bool_))[None, None, :, :, None]
            L = jnp.exp(jnp.where(causal, log_diff, -jnp.inf))
            CB = jnp.einsum('bcign,bcjgn->bcijg', C_c, B_c)
            L_rs = L.reshape(batch, n_chunks, Q, Q, G, Hg)
            dt_rs = dt_c.reshape(batch, n_chunks, Q, G, Hg)
            x_rs = x_c.reshape(batch, n_chunks, Q, G, Hg, P)
            y_intra = jnp.einsum('bcijGH,bcijG,bcjGH,bcjGHp->bciGHp', L_rs, CB, dt_rs, x_rs)
            decay_to_end = jnp.exp(chunk_log_decay[:, :, None, :] - cum_log_a)
            decay_to_end_rs = decay_to_end.reshape(batch, n_chunks, Q, G, Hg)
            state_local = jnp.einsum('bcjGH,bcjGH,bcjGn,bcjGHp->bcGHnp', decay_to_end_rs, dt_rs, B_c, x_rs)
            chunk_decay = jnp.exp(chunk_log_decay).reshape(batch, n_chunks, G, Hg)

            def scan_op(left, right):
                d_l, s_l = left
                d_r, s_r = right
                return (d_l * d_r, d_r[..., None, None] * s_l + s_r)
            _, state_at_end = jax.lax.associative_scan(scan_op, (chunk_decay, state_local), axis=1)
            state_at_start = jnp.concatenate([jnp.zeros_like(state_at_end[:, :1]), state_at_end[:, :-1]], axis=1)
            decay_from_start = jnp.exp(cum_log_a).reshape(batch, n_chunks, Q, G, Hg)
            y_inter = jnp.einsum('bciGH,bciGn,bcGHnp->bciGHp', decay_from_start, C_c, state_at_start)
            y = (y_intra + y_inter).reshape(batch, T_pad, n_heads, P)
            if pad_len:
                y = y[:, :seq_len]
            return y
        key = jax.random.key(seed)
        ks = jax.random.split(key, 6)
        Bsz, T = (2, 256)
        x = jax.random.normal(ks[0], (Bsz, T, N_EMBD), jnp.float32)
        norm_scale = jnp.ones((N_EMBD,), jnp.float32)
        in_proj_w = 0.02 * jax.random.normal(ks[1], (N_EMBD, PROJ), jnp.float32)
        conv_weight = 0.02 * jax.random.normal(ks[2], (D_CONV, D_INNER), jnp.float32)
        conv_bias = jnp.zeros((D_INNER,), jnp.float32)
        A_log = jnp.log(jnp.arange(1, N_HEADS + 1, dtype=jnp.float32))
        dt_bias = 0.1 * jax.random.normal(ks[3], (N_HEADS,), jnp.float32)
        D = jnp.ones((D_INNER,), jnp.float32)
        out_proj_w = 0.02 / np.sqrt(2 * N_LAYERS) * jax.random.normal(ks[4], (D_INNER, N_EMBD), jnp.float32)
        return dict(x=x, norm_scale=norm_scale, in_proj_w=in_proj_w, conv_weight=conv_weight, conv_bias=conv_bias, A_log=A_log, dt_bias=dt_bias, D=D, out_proj_w=out_proj_w)
    _L1_attn_b_in = _L1_attn_b_setup()

    def _L1_ffn_setup():
        import jax, jax.numpy as jnp
        import numpy as np
        TOP_K = 8
        CAPACITY = 128
        key = jax.random.key(seed)
        k1, k2, k3, k4 = jax.random.split(key, 4)
        B, S, H, E, I = (2, 128, 256, 64, 96)
        hidden_states = jax.random.normal(k1, (B, S, H), dtype=jnp.float32)
        router_weight = jax.random.normal(k2, (E, H), dtype=jnp.float32) * 0.02
        gate_up_proj = jax.random.normal(k3, (E, H, 2 * I), dtype=jnp.float32) * 0.02
        down_proj = jax.random.normal(k4, (E, I, H), dtype=jnp.float32) * 0.02
        return {'hidden_states': hidden_states, 'router_weight': router_weight, 'gate_up_proj': gate_up_proj, 'down_proj': down_proj}
    _L1_ffn_in = _L1_ffn_setup()
    _d = {'L0_attn_a_x': _L0_attn_a_in['x'], 'L0_attn_a_wq': _L0_attn_a_in['wq'], 'L0_attn_a_wk': _L0_attn_a_in['wk'], 'L0_attn_a_wv': _L0_attn_a_in['wv'], 'L0_attn_a_wo': _L0_attn_a_in['wo'], 'L0_attn_b_W_qkv': _L0_attn_b_in['W_qkv'], 'L0_attn_b_W_out': _L0_attn_b_in['W_out'], 'L0_ffn_SU_ug': _L0_ffn_in['SU_ug'], 'L0_ffn_SU_dp': _L0_ffn_in['SU_dp'], 'L0_ffn_Wscale_ug': _L0_ffn_in['Wscale_ug'], 'L0_ffn_Wscale_dp': _L0_ffn_in['Wscale_dp'], 'L0_ffn_W_up': _L0_ffn_in['W_up'], 'L0_ffn_W_gate': _L0_ffn_in['W_gate'], 'L0_ffn_W_down': _L0_ffn_in['W_down'], 'L1_attn_a_Wq': _L1_attn_a_in['Wq'], 'L1_attn_a_Wk': _L1_attn_a_in['Wk'], 'L1_attn_a_Wv': _L1_attn_a_in['Wv'], 'L1_attn_a_Wo': _L1_attn_a_in['Wo'], 'L1_attn_b_norm_scale': _L1_attn_b_in['norm_scale'], 'L1_attn_b_in_proj_w': _L1_attn_b_in['in_proj_w'], 'L1_attn_b_conv_weight': _L1_attn_b_in['conv_weight'], 'L1_attn_b_conv_bias': _L1_attn_b_in['conv_bias'], 'L1_attn_b_A_log': _L1_attn_b_in['A_log'], 'L1_attn_b_dt_bias': _L1_attn_b_in['dt_bias'], 'L1_attn_b_D': _L1_attn_b_in['D'], 'L1_attn_b_out_proj_w': _L1_attn_b_in['out_proj_w'], 'L1_ffn_router_weight': _L1_ffn_in['router_weight'], 'L1_ffn_gate_up_proj': _L1_ffn_in['gate_up_proj'], 'L1_ffn_down_proj': _L1_ffn_in['down_proj']}
    _x0 = _d['L0_attn_a_x']
    _d['L0_attn_a_x'] = jax.random.normal(jax.random.fold_in(jax.random.key(seed), 1), (4, 1024, 256), dtype=_x0.dtype)
    del _x0
    return _d

def reference(L0_attn_a_x, L0_attn_a_wq, L0_attn_a_wk, L0_attn_a_wv, L0_attn_a_wo, L0_attn_b_W_qkv, L0_attn_b_W_out, L0_ffn_SU_ug, L0_ffn_SU_dp, L0_ffn_Wscale_ug, L0_ffn_Wscale_dp, L0_ffn_W_up, L0_ffn_W_gate, L0_ffn_W_down, L1_attn_a_Wq, L1_attn_a_Wk, L1_attn_a_Wv, L1_attn_a_Wo, L1_attn_b_norm_scale, L1_attn_b_in_proj_w, L1_attn_b_conv_weight, L1_attn_b_conv_bias, L1_attn_b_A_log, L1_attn_b_dt_bias, L1_attn_b_D, L1_attn_b_out_proj_w, L1_ffn_router_weight, L1_ffn_gate_up_proj, L1_ffn_down_proj):

    def _L0_attn_a_ref(x, wq, wk, wv, wo):
        import jax, jax.numpy as jnp
        import numpy as np
        D_MODEL = 256
        NUM_HEADS = 16
        THETA = 10000.0

        def _rope(t, cos, sin):
            x_even = t[..., 0::2]
            x_odd = t[..., 1::2]
            rot = jnp.stack((-x_odd, x_even), axis=-1).reshape(t.shape)
            return t * cos + rot * sin
        bs, S, d = x.shape
        H = NUM_HEADS
        dk = d // H
        q = (x @ wq.T).reshape(bs, S, H, dk).transpose(0, 2, 1, 3)
        k = (x @ wk.T).reshape(bs, S, H, dk).transpose(0, 2, 1, 3)
        v = (x @ wv.T).reshape(bs, S, H, dk).transpose(0, 2, 1, 3)
        half = dk // 2
        inv_freq = THETA ** (-2.0 * jnp.arange(half, dtype=jnp.float32) / dk)
        pos = jnp.arange(S, dtype=jnp.float32)
        ang = pos[:, None] * inv_freq[None, :]
        cos = jnp.repeat(jnp.cos(ang), 2, axis=-1)
        sin = jnp.repeat(jnp.sin(ang), 2, axis=-1)
        q = _rope(q, cos, sin)
        k = _rope(k, cos, sin)
        scale = 1.0 / jnp.sqrt(jnp.asarray(dk, dtype=x.dtype))
        attn = jnp.einsum('bhqd,bhkd->bhqk', q, k) * scale
        causal = jnp.tril(jnp.ones((S, S), dtype=bool))
        attn = jnp.where(causal, attn, -jnp.inf)
        probs = jax.nn.softmax(attn, axis=-1)
        out = jnp.einsum('bhqk,bhkd->bhqd', probs, v)
        out = out.transpose(0, 2, 1, 3).reshape(bs, S, d)
        return out @ wo.T

    def _L0_attn_b_ref(x, W_qkv, W_out):
        import jax, jax.numpy as jnp
        import numpy as np
        DIM = 256
        N_HEADS = 16
        HEAD_DIM = DIM // N_HEADS
        B, T, D = x.shape
        qkv = jnp.einsum('btd,ed->bte', x, W_qkv)
        q, k, v = jnp.split(qkv, 3, axis=-1)

        def heads(t):
            return t.reshape(B, T, N_HEADS, HEAD_DIM).transpose(0, 2, 1, 3)
        q, k, v = (heads(q), heads(k), heads(v))
        att = jnp.einsum('bhid,bhjd->bhij', q, k) / HEAD_DIM ** 0.5
        causal = jnp.tril(jnp.ones((T, T), dtype=bool))
        att = jnp.where(causal, att, -jnp.inf)
        att = jax.nn.softmax(att, axis=-1)
        out = jnp.einsum('bhij,bhjd->bhid', att, v)
        out = out.transpose(0, 2, 1, 3).reshape(B, T, D)
        return jnp.einsum('btd,ed->bte', out, W_out)

    def _L0_ffn_ref(input, SU_ug, SU_dp, Wscale_ug, Wscale_dp, W_up, W_gate, W_down):
        import jax, jax.numpy as jnp
        import numpy as np
        HIDDEN = 256
        INTER = 1024
        SCALE = 64.0

        def fwht(x):
            orig_shape = x.shape
            n = orig_shape[-1]
            x = x.reshape(-1, n)
            h = 1
            while h < n:
                x = x.reshape(-1, n // (2 * h), 2, h)
                a, b = (x[:, :, 0, :], x[:, :, 1, :])
                x = jnp.stack([a + b, a - b], axis=2).reshape(-1, n)
                h *= 2
            return (x / jnp.sqrt(jnp.asarray(n, x.dtype))).reshape(orig_shape)
        n = SU_ug.shape[0]
        x = input.reshape(-1, n)
        x = fwht(x * SU_ug) / SCALE
        x_up = x @ W_up.T * (Wscale_ug[:INTER] * SCALE)
        x_gate = x @ W_gate.T * (Wscale_ug[INTER:] * SCALE)
        x = jax.nn.silu(x_gate) * x_up
        x = fwht(x * SU_dp) / SCALE
        x = x @ W_down.T * (Wscale_dp * SCALE)
        return x.reshape(input.shape)

    def _L1_attn_a_ref(x, Wq, Wk, Wv, Wo):
        import jax, jax.numpy as jnp
        import numpy as np
        NH = 16
        B, T, D = x.shape
        hd = D // NH
        q = (x @ Wq.T).reshape(B, T, NH, hd).transpose(0, 2, 1, 3)
        k = (x @ Wk.T).reshape(B, T, NH, hd).transpose(0, 2, 1, 3)
        v = (x @ Wv.T).reshape(B, T, NH, hd).transpose(0, 2, 1, 3)
        att = jnp.einsum('bhtd,bhsd->bhts', q, k) / jnp.sqrt(jnp.asarray(hd, x.dtype))
        neg = jnp.finfo(att.dtype).min
        mask = jnp.triu(jnp.full((T, T), neg, dtype=att.dtype), k=1)
        att = att + mask
        w = jax.nn.softmax(att, axis=-1)
        z = jnp.einsum('bhts,bhsd->bhtd', w, v)
        z = z.transpose(0, 2, 1, 3).reshape(B, T, D)
        return z @ Wo.T

    def _L1_attn_b_ref(x, norm_scale, in_proj_w, conv_weight, conv_bias, A_log, dt_bias, D, out_proj_w):
        import jax, jax.numpy as jnp
        import numpy as np
        N_EMBD = 256
        EXPAND = 2
        D_INNER = N_EMBD * EXPAND
        D_STATE = 128
        N_HEADS = D_INNER // D_STATE
        HEAD_DIM = D_INNER // N_HEADS
        N_GROUPS = 1
        D_CONV = 4
        CHUNK = 64
        N_LAYERS = 48
        GS = N_GROUPS * D_STATE
        PROJ = 2 * D_INNER + N_HEADS + 2 * GS
        RMS_EPS = 1e-06

        def _ssd_scan(A, B, C, dt, x, chunk_size=CHUNK):
            batch, seq_len, n_heads, P = x.shape
            G, N = (B.shape[2], B.shape[3])
            Hg = n_heads // G
            Q = chunk_size
            pad_len = -seq_len % Q
            if pad_len:
                A = jnp.pad(A, ((0, 0), (0, pad_len), (0, 0)))
                B = jnp.pad(B, ((0, 0), (0, pad_len), (0, 0), (0, 0)))
                C = jnp.pad(C, ((0, 0), (0, pad_len), (0, 0), (0, 0)))
                dt = jnp.pad(dt, ((0, 0), (0, pad_len), (0, 0)))
                x = jnp.pad(x, ((0, 0), (0, pad_len), (0, 0), (0, 0)))
            T_pad = seq_len + pad_len
            n_chunks = T_pad // Q
            A_c = A.reshape(batch, n_chunks, Q, n_heads)
            B_c = B.reshape(batch, n_chunks, Q, G, N)
            C_c = C.reshape(batch, n_chunks, Q, G, N)
            dt_c = dt.reshape(batch, n_chunks, Q, n_heads)
            x_c = x.reshape(batch, n_chunks, Q, n_heads, P)
            log_a = A_c * dt_c
            cum_log_a = jnp.cumsum(log_a, axis=2)
            chunk_log_decay = cum_log_a[:, :, -1, :]
            log_diff = cum_log_a[:, :, :, None, :] - cum_log_a[:, :, None, :, :]
            causal = jnp.tril(jnp.ones((Q, Q), dtype=jnp.bool_))[None, None, :, :, None]
            L = jnp.exp(jnp.where(causal, log_diff, -jnp.inf))
            CB = jnp.einsum('bcign,bcjgn->bcijg', C_c, B_c)
            L_rs = L.reshape(batch, n_chunks, Q, Q, G, Hg)
            dt_rs = dt_c.reshape(batch, n_chunks, Q, G, Hg)
            x_rs = x_c.reshape(batch, n_chunks, Q, G, Hg, P)
            y_intra = jnp.einsum('bcijGH,bcijG,bcjGH,bcjGHp->bciGHp', L_rs, CB, dt_rs, x_rs)
            decay_to_end = jnp.exp(chunk_log_decay[:, :, None, :] - cum_log_a)
            decay_to_end_rs = decay_to_end.reshape(batch, n_chunks, Q, G, Hg)
            state_local = jnp.einsum('bcjGH,bcjGH,bcjGn,bcjGHp->bcGHnp', decay_to_end_rs, dt_rs, B_c, x_rs)
            chunk_decay = jnp.exp(chunk_log_decay).reshape(batch, n_chunks, G, Hg)

            def scan_op(left, right):
                d_l, s_l = left
                d_r, s_r = right
                return (d_l * d_r, d_r[..., None, None] * s_l + s_r)
            _, state_at_end = jax.lax.associative_scan(scan_op, (chunk_decay, state_local), axis=1)
            state_at_start = jnp.concatenate([jnp.zeros_like(state_at_end[:, :1]), state_at_end[:, :-1]], axis=1)
            decay_from_start = jnp.exp(cum_log_a).reshape(batch, n_chunks, Q, G, Hg)
            y_inter = jnp.einsum('bciGH,bciGn,bcGHnp->bciGHp', decay_from_start, C_c, state_at_start)
            y = (y_intra + y_inter).reshape(batch, T_pad, n_heads, P)
            if pad_len:
                y = y[:, :seq_len]
            return y
        residual = x
        b, t = (x.shape[0], x.shape[1])
        h = x * jax.lax.rsqrt(jnp.mean(x * x, axis=-1, keepdims=True) + RMS_EPS) * norm_scale
        proj = h @ in_proj_w
        gate = proj[..., :D_INNER]
        ssm_in = proj[..., D_INNER:2 * D_INNER]
        dt_raw = proj[..., 2 * D_INNER:2 * D_INNER + N_HEADS]
        Bm = proj[..., 2 * D_INNER + N_HEADS:2 * D_INNER + N_HEADS + GS].reshape(b, t, N_GROUPS, D_STATE)
        Cm = proj[..., 2 * D_INNER + N_HEADS + GS:].reshape(b, t, N_GROUPS, D_STATE)
        xp = jnp.pad(ssm_in, ((0, 0), (D_CONV - 1, 0), (0, 0)))
        w_t = conv_weight.T[:, None, :]
        y = jax.lax.conv_general_dilated(jnp.transpose(xp, (0, 2, 1)), w_t, window_strides=(1,), padding='VALID', feature_group_count=D_INNER)
        ssm_in = jnp.transpose(y, (0, 2, 1)) + conv_bias
        ssm_in = jax.nn.silu(ssm_in)
        dt = jax.nn.softplus(dt_raw + dt_bias)
        A = -jnp.exp(A_log)
        A_f = jnp.broadcast_to(A[None, None, :], (b, t, N_HEADS))
        x_h = ssm_in.reshape(b, t, N_HEADS, HEAD_DIM)
        y_ssd = _ssd_scan(A_f, Bm, Cm, dt, x_h).reshape(b, t, D_INNER)
        y_ssd = y_ssd + D * ssm_in
        y_ssd = y_ssd * jax.nn.silu(gate)
        return residual + y_ssd @ out_proj_w

    def _L1_ffn_ref(hidden_states, router_weight, gate_up_proj, down_proj):
        import jax, jax.numpy as jnp
        import numpy as np
        TOP_K = 8
        CAPACITY = 128
        B, S, H = hidden_states.shape
        E = router_weight.shape[0]
        K, C = (TOP_K, CAPACITY)
        x = hidden_states.reshape(-1, H)
        logits = x @ router_weight.T
        probs = jax.nn.softmax(logits, axis=-1)
        topw, topi = jax.lax.top_k(probs, K)
        topw = topw / jnp.sum(topw, axis=-1, keepdims=True)
        flat_e = topi.reshape(-1)
        oh = jax.nn.one_hot(flat_e, E, dtype=jnp.int32)
        pos = jnp.take_along_axis(jnp.cumsum(oh, axis=0), flat_e[:, None], axis=1)[:, 0] - 1
        x_rep = jnp.repeat(x, K, axis=0)
        xe = jnp.zeros((E, C, H), x.dtype).at[flat_e, pos].set(x_rep, mode='drop')
        gu = jnp.einsum('ech,ehf->ecf', xe, gate_up_proj)
        g, u = jnp.split(gu, 2, axis=-1)
        h = jax.nn.silu(g) * u
        ye = jnp.einsum('eci,eih->ech', h, down_proj)
        valid = pos < C
        y_flat = jnp.where(valid[:, None], ye[flat_e, jnp.minimum(pos, C - 1)], 0.0)
        y = jnp.sum(y_flat.reshape(-1, K, H) * topw.reshape(-1, K)[..., None], axis=1)
        return y.reshape(B, S, H)
    x = L0_attn_a_x
    x = x + _L0_attn_a_ref(_layernorm(x, axis=-1), L0_attn_a_wq, L0_attn_a_wk, L0_attn_a_wv, L0_attn_a_wo)
    x = x + _L0_ffn_ref(_layernorm(x, axis=-1), L0_ffn_SU_ug, L0_ffn_SU_dp, L0_ffn_Wscale_ug, L0_ffn_Wscale_dp, L0_ffn_W_up, L0_ffn_W_gate, L0_ffn_W_down)
    x = x + _L0_attn_b_ref(_layernorm(x, axis=-1), L0_attn_b_W_qkv, L0_attn_b_W_out)
    x = x + _L0_ffn_ref(_layernorm(x, axis=-1), L0_ffn_SU_ug, L0_ffn_SU_dp, L0_ffn_Wscale_ug, L0_ffn_Wscale_dp, L0_ffn_W_up, L0_ffn_W_gate, L0_ffn_W_down)
    x = x + _L1_attn_a_ref(_layernorm(x, axis=-1), L1_attn_a_Wq, L1_attn_a_Wk, L1_attn_a_Wv, L1_attn_a_Wo)
    x = x + _L1_ffn_ref(_layernorm(x, axis=-1), L1_ffn_router_weight, L1_ffn_gate_up_proj, L1_ffn_down_proj)
    x = x + _L1_attn_b_ref(_layernorm(x, axis=-1), L1_attn_b_norm_scale, L1_attn_b_in_proj_w, L1_attn_b_conv_weight, L1_attn_b_conv_bias, L1_attn_b_A_log, L1_attn_b_dt_bias, L1_attn_b_D, L1_attn_b_out_proj_w)
    x = x + _L1_ffn_ref(_layernorm(x, axis=-1), L1_ffn_router_weight, L1_ffn_gate_up_proj, L1_ffn_down_proj)
    return x

_drawn_inputs = setup_inputs


def setup_inputs(seed=0):
    import zlib

    import numpy as np

    out = dict(_drawn_inputs(seed))
    spreads = {'L1_attn_b_norm_scale': (1.0, 0.6),
     'L1_attn_b_conv_bias': (0.0, 0.8),
     'L1_attn_b_D': (1.0, 0.6)}
    factors = {'L0_ffn_Wscale_dp': 2.838,
     'L1_attn_a_Wq': 8.0,
     'L1_attn_a_Wk': 8.0,
     'L1_attn_a_Wv': 3.112,
     'L1_attn_a_Wo': 3.145,
     'L1_attn_b_in_proj_w': 8.0,
     'L1_attn_b_conv_weight': 8.0,
     'L1_attn_b_A_log': 8.0,
     'L1_attn_b_dt_bias': 8.0,
     'L1_attn_b_out_proj_w': 8.0,
     'L1_ffn_router_weight': 8.0,
     'L1_ffn_gate_up_proj': 8.0,
     'L1_ffn_down_proj': 8.0}
    for name, (base, spread) in spreads.items():
        noise = np.random.default_rng([zlib.crc32(name.encode()), seed]).standard_normal(out[name].shape)
        drawn = base * np.exp(spread * noise) if base else spread * noise
        out[name] = jnp.asarray(drawn.astype(out[name].dtype))
    for name, factor in factors.items():
        out[name] = (out[name] * factor).astype(out[name].dtype)
    return out
```

```python
from contextlib import ExitStack

import numpy as np
import concourse.bass as bass
from concourse import mybir

F32 = mybir.dt.float32
BF16 = mybir.dt.bfloat16
I32 = mybir.dt.int32
U32 = mybir.dt.uint32
ALU = mybir.AluOpType
ACT = mybir.ActivationFunctionType
AX = mybir.AxisListType

P = 128
B, S, D = 4, 1024, 256
T = B * S
NT = T // P
TS = S // P
KD = D // P
LN_EPS = 1e-5

HEADS, DH = 16, 16
HG = 4
NG = HEADS // HG
GW = 3 * HG * DH
GQ = 2 * HG * DH
Q_PARTS = (0, 0, 1, 0, 2, 1)
K_PARTS = (0, 1, 0, 2, 0, 1)
NS = len(Q_PARTS)
MASKED = -1e30

INTER = 1024
E, FE, TOPK, CAP = 64, 96, 8, 128


class Steps:

    def __init__(self, engine, sem):
        self.engine, self.sem = engine, sem

    def begin(self, base):
        self.base, self.n = base, 0

    def done(self, instruction):
        instruction.then_inc(self.sem, 1)
        self.n += 1

    def wait(self):
        self.engine.wait_ge(self.sem, self.base + self.n)

    def end(self, planned):
        assert self.n == planned, (self.n, planned)


def carry(nc, tile):
    nc.vector.memset(tile[:, 0:1], 0.0)


def carry_on_pool(nc, tile, column, carried, before):
    nc.gpsimd.wait_ge(carried, before)
    nc.gpsimd.tensor_tensor(tile[:, column:column + 1], tile[:, 0:1], tile[:, 0:1], ALU.mult).then_inc(carried, 1)


def allocators(nc, ctx, name):
    def sb(what, shape, dt):
        return ctx.enter_context(nc.sbuf_tensor(f"{name}_{what}", shape, dt))

    def pb(what, shape, dt):
        return ctx.enter_context(nc.psum_tensor(f"{name}_{what}", shape, dt))

    used = []

    def sem(what):
        used.append(nc.alloc_semaphore(f"{name}_{what}"))
        return used[-1]

    def release():
        if used:
            nc.clear_and_free_semaphores(used)
            nc.all_engine_barrier()

    ctx.callback(release)
    return sb, pb, sem


def attention_layer(nc, name, x_res, consts, wqkv_dram, wout_dram, rope_dram):
    ident, ident_b, causal_q, causal_k = (consts[k] for k in ("ident", "ident_b", "causal_q", "causal_k"))
    with ExitStack() as ctx:
        sb, pb, sem = allocators(nc, ctx, name)
        w_qkv = sb("w_qkv", [P, KD, NG * GW], F32)
        w_out = sb("w_out", [P, KD, D], F32)
        if rope_dram is not None:
            cos_t = sb("cos_t", [P, TS, GQ], F32)
            sin_t = sb("sin_t", [P, TS, GQ], F32)
            rot_a = sb("rot_a", [P, TS, GQ], F32)
            rot_b = sb("rot_b", [P, TS, GQ], F32)
        waits_v, waits_p = sb("waits_v", [P, 2], F32), sb("waits_p", [P, 2], F32)
        h_tok = sb("h_tok", [P, TS, D], F32)
        hT = sb("hT", [P, KD, S], F32)
        stats = sb("stats", [P, TS, 6], F32)
        mv = sb("mv", [P, TS, 2], F32)
        rstd = sb("rstd", [P, 3, TS], F32)
        qkv = sb("qkv", [P, TS, GW], F32)
        qk = sb("qk", [P, TS, GQ], F32)
        part = sb("part", [P, 3, TS, GQ], BF16)
        rest = sb("rest", [P, 2, TS, GQ], F32)
        q_stack = sb("q_stack", [P, TS, HG, NS, DH], BF16)
        k_stack = sb("k_stack", [P, TS, HG, NS, DH], BF16)
        qsT = sb("qsT", [P, HG, S], BF16)
        ksT = sb("ksT", [P, HG, S], BF16)
        v_aug = sb("v_aug", [P, TS, HG, 32], F32)
        m_part = sb("m_part", [P, HG, TS, 2], F32)
        m_all = sb("m_all", [P, HG, TS], F32)
        m_rest = sb("m_rest", [P, 2, HG, TS], F32)
        m_split = sb("m_split", [P, HG, TS, 3], BF16)
        probs = sb("probs", [P, 2, HG, S], F32)
        oT = sb("oT", [P, S], F32)
        rsum = sb("rsum", [P, TS, HG], F32)
        attn = sb("attn", [P, TS, D], F32)
        ps_s = [pb(f"ps_s{i}", [P, 1024], F32) for i in range(2)]
        ps_o = pb("ps_o", [P, 1024], F32)
        ps_a = [pb(f"ps_a{i}", [P, 512], F32) for i in range(2)]

        carried = sem("carried")
        w_in = sem("w_in")
        ready0 = sem("ready0")
        dve = sem("dve")
        var_ready = sem("var_ready")
        std_ready = sem("std_ready")
        h_ready = sem("h_ready")
        hT_psum = sem("hT_psum")
        hT_ready = sem("hT_ready")
        qkv_psum = sem("qkv_psum")
        qkv_ready = sem("qkv_ready")
        v_ready = sem("v_ready")
        rot_ready = sem("rot_ready")
        stack_ready = sem("stack_ready")
        st_psum = sem("st_psum")
        st_ready_a = sem("st_ready_a")
        st_ready_v = sem("st_ready_v")
        max_psum = sem("max_psum")
        max_done = sem("max_done")
        nm_ready = sem("nm_ready")
        nm_psum = sem("nm_psum")
        nm_ready_a = sem("nm_ready_a")
        nm_ready_v = sem("nm_ready_v")
        s_psum = sem("s_psum")
        p_ready = sem("p_ready")
        pv_done = sem("pv_done")
        oT_ready = sem("oT_ready")
        o_psum = sem("o_psum")
        attn_ready = sem("attn_ready")
        aT_psum = sem("aT_psum")
        aT_ready = sem("aT_ready")
        y_psum = sem("y_psum")
        x_done = sem("x_done")

        DVE_LN = 2 * TS + 1
        DVE_IT = 13 if rope_dram is None else 16
        block = ctx.enter_context(nc.Block())

        CHUNKS = [(qt, c, 512 * c, min(512, 128 * (qt + 1) - 512 * c), 128 * (qt + 1) <= 512 * (c + 1))
                  for qt in range(TS) for c in range(2) if 512 * c < 128 * (qt + 1)]
        NMAX = HG * len(CHUNKS)

        @block.sync
        def _(sp):
            sp.dma_start(w_qkv[:], wqkv_dram.rearrange("(k p) n -> p k n", p=P)).then_inc(w_in, 16)
            sp.dma_start(w_out[:], wout_dram.rearrange("(k p) n -> p k n", p=P)).then_inc(w_in, 16)
            if rope_dram is not None:
                sp.dma_start(cos_t[:], rope_dram[0].rearrange("(t p) n -> p t n", p=P)).then_inc(w_in, 16)
                sp.dma_start(sin_t[:], rope_dram[1].rearrange("(t p) n -> p t n", p=P)).then_inc(w_in, 16)

        @block.gpsimd
        def _(pool):
            nc.gpsimd.memset(v_aug[:], 1.0).then_inc(ready0, 1)
            nc.gpsimd.memset(waits_p[:], 0.0).then_inc(ready0, 1)
            pool.wait_ge(ready0, 3)
            pool.wait_ge(w_in, 32 if rope_dram is None else 64)
            with pool.Fori(0, B) as b:
                with pool.Fori(0, NG) as g:
                    it = b * NG + g
                    pool.wait_ge(qkv_ready, 4 * it + 4)
                    pool.wait_ge(pv_done, TS * it)
                    carry_on_pool(nc, waits_p, 1, carried, it)
                    nc.gpsimd.tensor_copy(v_aug[:, :, :, 0:DH],
                                          qkv[:, :, GQ:GW].rearrange("p t (h d) -> p t h d", h=HG)).then_inc(v_ready, 1)
                    if rope_dram is not None:
                        pool.wait_ge(stack_ready, it)
                        src = qkv[:, :, 0:GQ].rearrange("p t (n two) -> p t n two", two=2)
                        dst = rot_b[:].rearrange("p t (n two) -> p t n two", two=2)
                        sn = sin_t[:].rearrange("p t (n two) -> p t n two", two=2)
                        nc.gpsimd.tensor_tensor(dst[:, :, :, 0], src[:, :, :, 1], sn[:, :, :, 0], ALU.mult).then_inc(rot_ready, 1)
                        nc.gpsimd.tensor_tensor(dst[:, :, :, 1], src[:, :, :, 0], sn[:, :, :, 1], ALU.mult).then_inc(rot_ready, 1)

        @block.tensor
        def _(pe):
            pe.wait_ge(w_in, 32 if rope_dram is None else 64)
            pe.wait_ge(ready0, 3)
            with pe.Fori(0, B) as b:
                for r in range(4):
                    pe.wait_ge(h_ready, 4 * b + r + 1)
                    if r >= 2:
                        pe.wait_ge(hT_ready, 4 * b + r - 1)
                    else:
                        pe.wait_ge(x_done, 4 * b)
                    for k in range(KD):
                        for tl in range(2):
                            mm = nc.tensor.transpose(ps_a[r % 2][:, 256 * k + 128 * tl:256 * k + 128 * tl + 128],
                                                     h_tok[:, 2 * r + tl, 128 * k:128 * k + 128], ident[:])
                    mm.then_inc(hT_psum, 1)
                with pe.Fori(0, NG) as g:
                    it = b * NG + g
                    for r in range(4):
                        if r == 0:
                            pe.wait_ge(hT_ready, 4 * b + 4)
                            pe.wait_ge(nm_ready_a, 2 * it)
                        elif r == 1:
                            pe.wait_ge(nm_ready_v, 2 * it)
                        else:
                            pe.wait_ge(qkv_ready, 4 * it + r - 1)
                        for tl in range(2):
                            t = 2 * r + tl
                            for k in range(KD):
                                mm = nc.tensor.matmul(ps_a[r % 2][:, GW * tl:GW * tl + GW], hT[:, k, 128 * t:128 * t + 128],
                                                      w_qkv[:, k, bass.ds(g * GW, GW)], start=(k == 0), stop=(k == KD - 1))
                        mm.then_inc(qkv_psum, 1)
                    pe.wait_ge(stack_ready, it + 1)
                    for u in range(2 * HG):
                        src = (q_stack if u < HG else k_stack)[:, :, u % HG, :, :]
                        if u < 2:
                            pe.wait_ge(qkv_ready, 4 * it + 3 + u)
                        elif u % 2 == 0:
                            pe.wait_ge(st_ready_a, 4 * it + u // 2)
                        else:
                            pe.wait_ge(st_ready_v, 4 * it + u // 2)
                        for t in range(TS):
                            mm = nc.tensor.transpose(ps_a[u % 2][:].bitcast(BF16)[0:96, 128 * t:128 * t + 128],
                                                     src[:, t].rearrange("p s d -> p (s d)"), ident_b[:])
                        mm.then_inc(st_psum, 1)
                    for v in range(NMAX):
                        h, (qt, c, k0, kn, diag) = v // len(CHUNKS), CHUNKS[v % len(CHUNKS)]
                        if v == 0:
                            pe.wait_ge(st_ready_a, 4 * it + 4)
                            pe.wait_ge(st_ready_v, 4 * it + 4)
                        elif v >= 2:
                            pe.wait_ge(max_done, NMAX * it + v - 1)
                        bank = ps_a[v % 2]
                        mm = nc.tensor.matmul(bank[:, 0:kn], qsT[0:96, h, 128 * qt:128 * qt + 128],
                                              ksT[0:96, h, k0:k0 + kn], start=True, stop=not diag)
                        if diag:
                            mm = nc.tensor.matmul(bank[:, kn - 128:kn], ident_b[:], causal_q[:], start=False, stop=True)
                        mm.then_inc(max_psum, 1)
                    pe.wait_ge(nm_ready, it + 1)
                    for h in range(HG):
                        if h >= 2:
                            pe.wait_ge(nm_ready_a if h % 2 == 0 else nm_ready_v, 2 * it + 1)
                        for t in range(TS):
                            mm = nc.tensor.transpose(ps_a[h % 2][:].bitcast(BF16)[96:99, 128 * t:128 * t + 128],
                                                     m_split[:, h, t, :], ident_b[:])
                        mm.then_inc(nm_psum, 1)
                    pe.wait_ge(nm_ready_a, 2 * it + 2)
                    pe.wait_ge(nm_ready_v, 2 * it + 2)
                    for kt in range(TS + 1):
                        if kt < TS:
                            for h in range(HG):
                                w = kt * HG + h
                                if w >= 2:
                                    pe.wait_ge(p_ready, HG * TS * it + w - 1)
                                else:
                                    pe.wait_ge(attn_ready, it)
                                for c in range(2):
                                    q0, q1 = max(512 * c, 128 * kt), 512 * (c + 1)
                                    if q0 >= q1:
                                        continue
                                    diag = q0 == 128 * kt
                                    mm = nc.tensor.matmul(ps_s[w % 2][:, q0:q1], ksT[0:99, h, 128 * kt:128 * kt + 128],
                                                          qsT[0:99, h, q0:q1], start=True, stop=not diag)
                                    if diag:
                                        mm = nc.tensor.matmul(ps_s[w % 2][:, q0:q0 + 128], ident_b[:], causal_k[:],
                                                              start=False, stop=True)
                                mm.then_inc(s_psum, 1)
                        if kt >= 1:
                            kp = kt - 1
                            pe.wait_ge(p_ready, HG * TS * it + HG * kp + HG)
                            if kp == 0:
                                pe.wait_ge(v_ready, it + 1)
                                pe.wait_ge(oT_ready, it)
                            for c in range(2):
                                q0, q1 = max(512 * c, 128 * kp), 512 * (c + 1)
                                if q0 >= q1:
                                    continue
                                for h in range(HG):
                                    mm = nc.tensor.matmul(ps_o[32 * h:32 * h + 32, q0:q1], v_aug[:, kp, h, :],
                                                          probs[:, kp % 2, h, q0:q1], start=(kp == 0),
                                                          stop=(kp == 4 * c + 3))
                            mm.then_inc(pv_done, 1)
                    pe.wait_ge(oT_ready, it + 1)
                    for t in range(TS):
                        mm = nc.tensor.transpose(ps_s[0][:, 128 * t:128 * t + 128], oT[:, 128 * t:128 * t + 128], ident[:])
                    mm.then_inc(o_psum, 1)
                pe.wait_ge(attn_ready, NG * b + NG)
                for r in range(4):
                    if r < 2:
                        pass
                    else:
                        pe.wait_ge(aT_ready, 4 * b + r - 1)
                    for k in range(KD):
                        for tl in range(2):
                            mm = nc.tensor.transpose(ps_a[r % 2][:, 256 * k + 128 * tl:256 * k + 128 * tl + 128],
                                                     attn[:, 2 * r + tl, 128 * k:128 * k + 128], ident[:])
                    mm.then_inc(aT_psum, 1)
                for r in range(4):
                    if r == 0:
                        pe.wait_ge(aT_ready, 4 * b + 4)
                    elif r >= 2:
                        pe.wait_ge(x_done, 4 * b + r - 1)
                    for tl in range(2):
                        t = 2 * r + tl
                        for k in range(KD):
                            mm = nc.tensor.matmul(ps_a[r % 2][:, D * tl:D * tl + D], hT[:, k, 128 * t:128 * t + 128],
                                                  w_out[:, k, :], start=(k == 0), stop=(k == KD - 1))
                    mm.then_inc(y_psum, 1)

        @block.scalar
        def _(act):
            with act.Fori(0, B) as b:
                act.wait_ge(var_ready, b + 1)
                nc.scalar.activation(rstd[:, 1], rstd[:, 0], ACT.Sqrt).then_inc(std_ready, 1)
                act.wait_ge(y_psum, 4 * b)
                for r in range(4):
                    act.wait_ge(hT_psum, 4 * b + r + 1)
                    nc.scalar.copy(hT[:, :, 256 * r:256 * r + 256],
                                   ps_a[r % 2][:].rearrange("p (k n) -> p k n", k=KD)).then_inc(hT_ready, 1)
                with act.Fori(0, NG) as g:
                    it = b * NG + g
                    for r in range(4):
                        act.wait_ge(qkv_psum, 4 * it + r + 1)
                        if r == 0:
                            act.wait_ge(v_ready, it)
                            act.wait_ge(stack_ready, it)
                        nc.scalar.copy(qkv[:, 2 * r:2 * r + 2, :],
                                       ps_a[r % 2][:, 0:2 * GW].rearrange("p (t n) -> p t n", t=2)).then_inc(qkv_ready, 1)
                    for u in range(0, 2 * HG, 2):
                        act.wait_ge(st_psum, 8 * it + u + 1)
                        if u == 0:
                            act.wait_ge(pv_done, TS * it)
                        nc.scalar.copy((qsT if u < HG else ksT)[0:96, u % HG, :], ps_a[0][:].bitcast(BF16)[0:96, :])\
                          .then_inc(st_ready_a, 1)
                    for h in range(0, HG, 2):
                        act.wait_ge(nm_psum, HG * it + h + 1)
                        nc.scalar.copy(qsT[96:99, h, :], ps_a[0][:].bitcast(BF16)[96:99, :]).then_inc(nm_ready_a, 1)
                    for w in range(HG * TS):
                        kt, h = w // HG, w % HG
                        act.wait_ge(s_psum, HG * TS * it + w + 1)
                        if h == 0:
                            if kt >= 2:
                                act.wait_ge(pv_done, TS * it + kt - 1)
                            else:
                                act.wait_ge(pv_done, TS * it)
                        nc.scalar.activation(probs[:, kt % 2, h, 128 * kt:S], ps_s[w % 2][:, 128 * kt:S], ACT.Exp,
                                             scale=DH ** -0.5).then_inc(p_ready, 1)
                    act.wait_ge(pv_done, TS * it + TS)
                    act.wait_ge(o_psum, it)
                    nc.scalar.copy(oT[:], ps_o[:]).then_inc(oT_ready, 1)
                for r in range(4):
                    act.wait_ge(aT_psum, 4 * b + r + 1)
                    nc.scalar.copy(hT[:, :, 256 * r:256 * r + 256],
                                   ps_a[r % 2][:].rearrange("p (k n) -> p k n", k=KD)).then_inc(aT_ready, 1)

        @block.vector
        def _(v):
            step = Steps(v, dve)
            nc.vector.memset(ksT[96:99, :, :], 1.0).then_inc(ready0, 1)
            if rope_dram is not None:
                v.wait_ge(w_in, 64)
            with v.Fori(0, B) as b:
                step.begin((DVE_LN + NG * DVE_IT) * b)
                for t in range(TS):
                    step.done(nc.vector.bn_stats(stats[:, t, :], x_res[:, bass.ds(b * TS + t, 1), :].rearrange("p o d -> p (o d)")))
                step.wait()
                carry(nc, waits_v)
                for t in range(TS):
                    step.done(nc.vector.bn_aggr(mv[:, t, :], stats[:, t, :]))
                step.wait()
                nc.vector.tensor_scalar(rstd[:, 0], mv[:, :, 1], LN_EPS, None, ALU.add).then_inc(var_ready, 1)
                v.wait_ge(std_ready, b + 1)
                step.done(nc.vector.reciprocal(rstd[:, 2], rstd[:, 1]))
                step.wait()
                v.wait_ge(hT_psum, 4 * b)
                for t in range(TS):
                    ins = nc.vector.tensor_scalar(h_tok[:, t, :], x_res[:, bass.ds(b * TS + t, 1), :].rearrange("p o d -> p (o d)"),
                                                  mv[:, t, 0:1], rstd[:, 2, t:t + 1], ALU.subtract, ALU.mult)
                    if t % 2 == 1:
                        ins.then_inc(h_ready, 1)
                step.end(DVE_LN)
                with v.Fori(0, NG) as g:
                    it = b * NG + g
                    step.begin((DVE_LN + NG * DVE_IT) * b + DVE_LN + DVE_IT * g)
                    v.wait_ge(qkv_ready, 4 * it + 4)
                    if rope_dram is None:
                        src = qkv[:, :, 0:GQ]
                    else:
                        src = qk[:]
                        step.done(nc.vector.tensor_tensor(rot_a[:], qkv[:, :, 0:GQ], cos_t[:], ALU.mult))
                        v.wait_ge(rot_ready, 2 * it + 2)
                        step.wait()
                        ra = rot_a[:].rearrange("p t (n two) -> p t n two", two=2)
                        rb = rot_b[:].rearrange("p t (n two) -> p t n two", two=2)
                        qq = qk[:].rearrange("p t (n two) -> p t n two", two=2)
                        step.done(nc.vector.tensor_tensor(qq[:, :, :, 0], ra[:, :, :, 0], rb[:, :, :, 0], ALU.subtract))
                        step.done(nc.vector.tensor_tensor(qq[:, :, :, 1], ra[:, :, :, 1], rb[:, :, :, 1], ALU.add))
                        step.wait()
                    step.done(nc.vector.tensor_copy(part[:, 0], src))
                    step.wait()
                    step.done(nc.vector.tensor_tensor(rest[:, 0], src, part[:, 0], ALU.subtract))
                    step.wait()
                    step.done(nc.vector.tensor_copy(part[:, 1], rest[:, 0]))
                    step.wait()
                    step.done(nc.vector.tensor_tensor(rest[:, 1], rest[:, 0], part[:, 1], ALU.subtract))
                    step.wait()
                    step.done(nc.vector.tensor_copy(part[:, 2], rest[:, 1]))
                    step.wait()
                    v.wait_ge(st_psum, 8 * it)
                    for stack, order, o in ((q_stack, Q_PARTS, 0), (k_stack, K_PARTS, HG * DH)):
                        for s in range(NS):
                            ins = nc.vector.tensor_copy(stack[:, :, :, s, :],
                                                        part[:, order[s], :, o:o + HG * DH].rearrange("p t (h d) -> p t h d", h=HG))
                    ins.then_inc(stack_ready, 1)
                    for u in range(1, 2 * HG, 2):
                        v.wait_ge(st_psum, 8 * it + u + 1)
                        if u == 1:
                            v.wait_ge(pv_done, TS * it)
                        nc.vector.tensor_copy((qsT if u < HG else ksT)[0:96, u % HG, :], ps_a[1][:].bitcast(BF16)[0:96, :])\
                          .then_inc(st_ready_v, 1)
                    for i in range(NMAX):
                        h, (qt, c, k0, kn, diag) = i // len(CHUNKS), CHUNKS[i % len(CHUNKS)]
                        v.wait_ge(max_psum, NMAX * it + i + 1)
                        nc.vector.tensor_reduce(m_part[:, h, qt, c:c + 1], ps_a[i % 2][:, 0:kn], AX.X, ALU.max)\
                          .then_inc(max_done, 1)
                    v.wait_ge(max_done, NMAX * it + NMAX)
                    v.wait_ge(nm_psum, HG * it)
                    step.done(nc.vector.tensor_scalar(m_all[:, :, 0:4], m_part[:, :, 0:4, 0], -1.0, None, ALU.mult))
                    step.done(nc.vector.tensor_tensor(m_rest[:, 0, :, 4:8], m_part[:, :, 4:8, 0], m_part[:, :, 4:8, 1], ALU.max))
                    step.wait()
                    step.done(nc.vector.tensor_scalar(m_all[:, :, 4:8], m_rest[:, 0, :, 4:8], -1.0, None, ALU.mult))
                    step.wait()
                    step.done(nc.vector.tensor_copy(m_split[:, :, :, 0], m_all[:]))
                    step.wait()
                    step.done(nc.vector.tensor_tensor(m_rest[:, 0], m_all[:], m_split[:, :, :, 0], ALU.subtract))
                    step.wait()
                    step.done(nc.vector.tensor_copy(m_split[:, :, :, 1], m_rest[:, 0]))
                    step.wait()
                    step.done(nc.vector.tensor_tensor(m_rest[:, 1], m_rest[:, 0], m_split[:, :, :, 1], ALU.subtract))
                    step.wait()
                    nc.vector.tensor_copy(m_split[:, :, :, 2], m_rest[:, 1]).then_inc(nm_ready, 1)
                    for h in range(1, HG, 2):
                        v.wait_ge(nm_psum, HG * it + h + 1)
                        nc.vector.tensor_copy(qsT[96:99, h, :], ps_a[1][:].bitcast(BF16)[96:99, :]).then_inc(nm_ready_v, 1)
                    v.wait_ge(o_psum, it + 1)
                    o_tok = ps_s[0][:].rearrange("p (t h e) -> p t h e", t=TS, h=HG)
                    step.done(nc.vector.reciprocal(rsum[:], o_tok[:, :, :, DH]))
                    step.wait()
                    v.wait_ge(aT_psum, 4 * b)
                    nc.vector.tensor_tensor(attn[:, :, bass.ds(g * (HG * DH), HG * DH)].rearrange("p t (h d) -> p t h d", h=HG),
                                            o_tok[:, :, :, 0:DH], rsum[:].unsqueeze(3).to_broadcast([P, TS, HG, DH]),
                                            ALU.mult).then_inc(attn_ready, 1)
                    step.end(DVE_IT)
                for r in range(4):
                    v.wait_ge(y_psum, 4 * b + r + 1)
                    xs = x_res[:, bass.ds(b * TS + 2 * r, 2), :]
                    nc.vector.tensor_tensor(xs, xs, ps_a[r % 2][:].rearrange("p (t n) -> p t n", t=2), ALU.add).then_inc(x_done, 1)


def mlp_weights(nc, w_ug, w_dn, wug_dram, wdn_dram, had_dram, su_dram, scale_ug, su_dp, scale_dp):
    KI = INTER // P
    with ExitStack() as ctx:
        sb, pb, sem = allocators(nc, ctx, "fold")
        raw_ug = sb("raw_ug", [P, KD, 2 * INTER], F32)
        raw_dn = sb("raw_dn", [P, KI, D], F32)
        had = sb("had", [P, 4, P], F32)
        su_u = sb("su_u", [P, KD], F32)
        su_d = sb("su_d", [P, KI], F32)
        sc_u = sb("sc_u", [P, 2 * INTER], F32)
        sc_d = sb("sc_d", [P, D], F32)
        ps = [pb(f"ps{i}", [P, 512], F32) for i in range(2)]
        landed, folded, scaled = sem("landed"), sem("folded"), sem("scaled")
        block = ctx.enter_context(nc.Block())
        NLOAD = 7
        jobs = []
        for a1 in range(KD):
            for c in range(4):
                jobs.append((w_ug[:, a1, 512 * c:512 * c + 512], su_u[:, a1:a1 + 1], sc_u[:, 512 * c:512 * c + 512],
                             [((a0 & a1) % 2, raw_ug[:, a0, 512 * c:512 * c + 512]) for a0 in range(KD)]))
        for c1 in range(KI):
            jobs.append((w_dn[:, c1, :], su_d[:, c1:c1 + 1], sc_d[:],
                         [(2 + bin(c0 & c1).count("1") % 2, raw_dn[:, c0, :]) for c0 in range(KI)]))

        @block.sync
        def _(sp):
            sp.dma_start(had[:], had_dram.rearrange("m p n -> p m n")).then_inc(landed, 16)
            sp.dma_start(raw_ug[:], wug_dram.rearrange("(k p) n -> p k n", p=P)).then_inc(landed, 16)
            sp.dma_start(su_u[:], su_dram).then_inc(landed, 16)
            sp.dma_start(sc_u[:], scale_ug.partition_broadcast(P)).then_inc(landed, 16)
            sp.dma_start(raw_dn[:], wdn_dram.rearrange("(k p) n -> p k n", p=P)).then_inc(landed, 16)
            sp.dma_start(su_d[:], su_dp).then_inc(landed, 16)
            sp.dma_start(sc_d[:], scale_dp.partition_broadcast(P)).then_inc(landed, 16)

        @block.tensor
        def _(pe):
            pe.wait_ge(landed, 16 * NLOAD)
            for n, (dst, _, _, products) in enumerate(jobs):
                if n >= 2:
                    pe.wait_ge(scaled, n - 1)
                width = dst.shape[-1]
                for i, (which, moving) in enumerate(products):
                    mm = nc.tensor.matmul(ps[n % 2][:, 0:width], had[:, which, :], moving, start=(i == 0),
                                          stop=(i == len(products) - 1))
                mm.then_inc(folded, 1)

        @block.vector
        def _(v):
            v.wait_ge(landed, 16 * NLOAD)
            for n, (dst, sign, scale, _) in enumerate(jobs):
                v.wait_ge(folded, n + 1)
                nc.vector.scalar_tensor_tensor(dst, ps[n % 2][:, 0:dst.shape[-1]], sign, scale, ALU.mult, ALU.mult)\
                  .then_inc(scaled, 1)
            v.wait_ge(scaled, len(jobs))


def mlp_layer(nc, name, x_res, consts, w_ug, w_dn):
    ident = consts["ident"]
    CT = 4
    NC = NT // CT
    CW = CT * P
    KI = INTER // P
    with ExitStack() as ctx:
        sb, pb, sem = allocators(nc, ctx, name)
        stats = sb("stats", [P, NT, 6], F32)
        mv = sb("mv", [P, NT, 2], F32)
        rstd = sb("rstd", [P, 3, NT], F32)
        h_tok = sb("h_tok", [P, CT, D], F32)
        hT = sb("hT", [P, KD, CW], F32)
        gated = sb("gated", [P, 2, CW], F32)
        mid = sb("mid", [P, KI, CW], F32)
        ps_t = [pb(f"ps_t{i}", [P, 512], F32) for i in range(2)]
        ps_g = [pb(f"ps_g{i}", [P, 512], F32) for i in range(2)]
        ps_u = [pb(f"ps_u{i}", [P, 512], F32) for i in range(2)]
        ps_y = [pb(f"ps_y{i}", [P, 512], F32) for i in range(2)]
        dve = sem("dve")
        var_ready, std_ready = sem("var_ready"), sem("std_ready")
        h_ready, hT_psum, hT_ready = sem("h_ready"), sem("hT_psum"), sem("hT_ready")
        gu_psum, silu_ready, mid_ready = sem("gu_psum"), sem("silu_ready"), sem("mid_ready")
        y_psum, x_done = sem("y_psum"), sem("x_done")
        block = ctx.enter_context(nc.Block())

        @block.tensor
        def _(pe):
            def to_features(c):
                for r in range(2):
                    pe.wait_ge(h_ready, 2 * c + r + 1)
                    for k in range(KD):
                        for tl in range(2):
                            mm = nc.tensor.transpose(ps_t[r][:, 256 * k + 128 * tl:256 * k + 128 * tl + 128],
                                                     h_tok[:, 2 * r + tl, 128 * k:128 * k + 128], ident[:])
                    mm.then_inc(hT_psum, 1)

            def chunk(c, last):
                pe.wait_ge(hT_ready, 2 * c + 2)
                for j in range(KI):
                    if j >= 2:
                        pe.wait_ge(mid_ready, KI * c + j - 1)
                    for base, ps in ((0, ps_u), (INTER, ps_g)):
                        for k in range(KD):
                            mm = nc.tensor.matmul(ps[j % 2][:], w_ug[:, k, base + P * j:base + P * j + P], hT[:, k, :],
                                                  start=(k == 0), stop=(k == KD - 1))
                    mm.then_inc(gu_psum, 1)
                if not last:
                    to_features(c + 1)
                for t in range(CT):
                    if t == 0:
                        pe.wait_ge(x_done, 2 * c)
                    for j in range(KI):
                        if t == 0:
                            pe.wait_ge(mid_ready, KI * c + j + 1)
                        mm = nc.tensor.matmul(ps_y[t // 2][:, D * (t % 2):D * (t % 2) + D], mid[:, j, P * t:P * t + P],
                                              w_dn[:, j, :], start=(j == 0), stop=(j == KI - 1))
                    if t % 2 == 1:
                        mm.then_inc(y_psum, 1)

            to_features(0)
            with pe.Fori(0, NC - 1) as c:
                chunk(c, False)
            chunk(NC - 1, True)

        @block.scalar
        def _(act):
            def to_features(c):
                for r in range(2):
                    act.wait_ge(hT_psum, 2 * c + r + 1)
                    if r == 0:
                        act.wait_ge(gu_psum, KI * c)
                    nc.scalar.copy(hT[:, :, 256 * r:256 * r + 256],
                                   ps_t[r][:].rearrange("p (k n) -> p k n", k=KD)).then_inc(hT_ready, 1)

            def chunk(c, last):
                for j in range(KI):
                    act.wait_ge(gu_psum, KI * c + j + 1)
                    if j >= 2:
                        act.wait_ge(mid_ready, KI * c + j - 1)
                    else:
                        act.wait_ge(mid_ready, KI * c)
                    nc.scalar.activation(gated[:, j % 2, :], ps_g[j % 2][:], ACT.Silu).then_inc(silu_ready, 1)
                if not last:
                    to_features(c + 1)

            act.wait_ge(var_ready, 1)
            nc.scalar.activation(rstd[:, 1], rstd[:, 0], ACT.Sqrt).then_inc(std_ready, 1)
            to_features(0)
            with act.Fori(0, NC - 1) as c:
                chunk(c, False)
            chunk(NC - 1, True)

        @block.vector
        def _(v):
            layer_norm_statistics(nc, v, x_res, stats, mv, rstd, dve, var_ready, std_ready)

            def normalize(c):
                v.wait_ge(hT_psum, 2 * c)
                for t in range(CT):
                    tile = c * CT + t
                    ins = nc.vector.tensor_scalar(h_tok[:, t, :], one_tile(x_res, tile), mean_of(mv, tile), rstd_of(rstd, tile),
                                                  ALU.subtract, ALU.mult)
                    if t % 2 == 1:
                        ins.then_inc(h_ready, 1)

            def chunk(c, last):
                if not last:
                    normalize(c + 1)
                for j in range(KI):
                    v.wait_ge(silu_ready, KI * c + j + 1)
                    if j == 0:
                        v.wait_ge(y_psum, 2 * c)
                    nc.vector.tensor_tensor(mid[:, j, :], gated[:, j % 2, :], ps_u[j % 2][:], ALU.mult).then_inc(mid_ready, 1)
                for r in range(2):
                    v.wait_ge(y_psum, 2 * c + r + 1)
                    xs = x_res[:, bass.ds(c * CT + 2 * r, 2), :]
                    nc.vector.tensor_tensor(xs, xs, ps_y[r][:].rearrange("p (t n) -> p t n", t=2), ALU.add).then_inc(x_done, 1)

            normalize(0)
            with v.Fori(0, NC - 1) as c:
                chunk(c, False)
            chunk(NC - 1, True)


def one_tile(x, t):
    return x[:, bass.ds(t, 1), :].rearrange("p o d -> p (o d)")


def mean_of(mv, t):
    return mv[:, bass.ds(t, 1), 0:1].rearrange("p o d -> p (o d)")


def rstd_of(rstd, t):
    return rstd[:, 2, bass.ds(t, 1)]


def layer_norm_statistics(nc, v, x_res, stats, mv, rstd, dve, var_ready, std_ready):
    step = Steps(v, dve)
    PER = 8
    with v.Fori(0, NT // PER) as i:
        step.begin(PER * i)
        for t in range(PER):
            step.done(nc.vector.bn_stats(stats[:, bass.ds(PER * i + t, 1), :].rearrange("p o d -> p (o d)"), one_tile(x_res, PER * i + t)))
    step.begin(NT)
    step.wait()
    for t in range(NT):
        step.done(nc.vector.bn_aggr(mv[:, t, :], stats[:, t, :]))
    step.wait()
    nc.vector.tensor_scalar(rstd[:, 0], mv[:, :, 1], LN_EPS, None, ALU.add).then_inc(var_ready, 1)
    v.wait_ge(std_ready, 1)
    step.done(nc.vector.reciprocal(rstd[:, 2], rstd[:, 1]))
    step.wait()
    return step


def moe_layer(nc, name, x_res, consts, router_dram, gate_up_dram, down_dram, keyval_dram, slot_no_dram, rows_dram, x_dram):
    ident = consts["ident"]
    NI = NT // 2
    ROW = D + E
    with ExitStack() as outer:
        _, _, osem = allocators(nc, outer, name)
        slot_token = outer.enter_context(nc.sbuf_tensor(f"{name}_slot_token", [P, E], I32))

        with ExitStack() as ctx:
            sb, pb, sem = allocators(nc, ctx, name)
            stats = sb("stats", [P, NT, 6], F32)
            mv = sb("mv", [P, NT, 2], F32)
            rstd = sb("rstd", [P, 3, NT], F32)
            waits_v = sb("waits_v", [P, 2], F32)
            w_r = sb("w_r", [P, KD, E], F32)
            zeros = sb("zeros", [P, ROW], F32)
            rows = sb("rows", [P, 2, 2, ROW], F32)
            hT = sb("hT", [P, 2, KD, P], F32)
            nmax = sb("nmax", [P, 2], F32)
            ex = sb("ex", [P, 2, E], F32)
            esum = sb("esum", [P, 2], F32)
            einv = sb("einv", [P, 2], F32)
            probs = sb("probs", [P, 2, E], F32)
            best = sb("best", [P, 2, TOPK], F32)
            left = sb("left", [P, 2, E], F32)
            mask = sb("mask", [P, 2, E], F32)
            wraw = sb("wraw", [P, 2, E], F32)
            wsum = sb("wsum", [P, 2], F32)
            winv = sb("winv", [P, 2], F32)
            keyval = sb("keyval", [P, T // 2], F32)
            keys = sb("keys", [P, T // 2], F32)
            first = sb("first", [P, CAP], F32)
            firstT = sb("firstT", [P, P], F32)
            both = sb("both", [E, 2 * CAP], F32)
            picked = sb("picked", [E, CAP], F32)
            empty = sb("empty", [P, E], F32)
            token_f = sb("token_f", [P, E], F32)
            slot_no = sb("slot_no", [P, 1], F32)
            ps_t = [pb(f"ps_t{i}", [P, 512], F32) for i in range(2)]
            ps_l = [pb(f"ps_l{i}", [P, 512], F32) for i in range(2)]
            ps_m = pb("ps_m", [P, 512], F32)
            landed, stored, rows_out, zeroed = sem("landed"), sem("stored"), sem("rows_out"), sem("zeroed")
            dve = sem("dve")
            var_ready, std_ready = sem("var_ready"), sem("std_ready")
            h_ready, hT_psum, hT_ready = sem("h_ready"), sem("hT_psum"), sem("hT_ready")
            logit_psum, nmax_ready, ex_ready = sem("logit_psum"), sem("nmax_ready"), sem("ex_ready")
            maskT_psum, key_done, w_ready = sem("maskT_psum"), sem("key_done"), sem("w_ready")
            first_ready, firstT_psum, firstT_ready, both_psum = sem("first_ready"), sem("firstT_psum"), sem("firstT_ready"), sem("both_psum")
            picked_ready, picked_psum, slots_ready = sem("picked_ready"), sem("picked_psum"), sem("slots_ready")
            block = ctx.enter_context(nc.Block())
            PAIR = 8

            @block.sync
            def _(sp):
                sp.dma_start(w_r[:], router_dram.rearrange("(k p) e -> p k e", p=P)).then_inc(landed, 16)
                sp.dma_start(keyval[:], keyval_dram).then_inc(landed, 16)
                sp.dma_start(slot_no[:], slot_no_dram).then_inc(landed, 16)
                sp.dma_start(x_dram[0:T, :].rearrange("(t p) d -> p t d", p=P), x_res[:]).then_inc(stored, 16)
                sp.wait_ge(zeroed, 1)
                sp.dma_start(rows_dram[T:T + P, :], zeros[:]).then_inc(stored, 16)
                sp.dma_start(x_dram[T:T + P, :], zeros[:, 0:D]).then_inc(stored, 16)
                with sp.Fori(0, NI) as i:
                    for half in range(2):
                        sp.wait_ge(w_ready, 2 * i + half + 1)
                        sp.dma_start(rows_dram[bass.ds((i + NI * half) * P, P), :], rows[:, 0, half, :]).then_inc(rows_out, 16)
                sp.wait_ge(rows_out, 32 * NI)
                sp.wait_ge(stored, 48)

            @block.tensor
            def _(pe):
                pe.wait_ge(landed, 48)
                with pe.Fori(0, NI) as i:
                    for half in range(2):
                        n = 2 * i + half
                        pe.wait_ge(h_ready, n + 1)
                        for k in range(KD):
                            mm = nc.tensor.transpose(ps_t[half][:, P * k:P * k + P], rows[:, 0, half, P * k:P * k + P], ident[:])
                        mm.then_inc(hT_psum, 1)
                    for half in range(2):
                        n = 2 * i + half
                        pe.wait_ge(hT_ready, n + 1)
                        for k in range(KD):
                            mm = nc.tensor.matmul(ps_l[half][:, 0:E], hT[:, half, k, :], w_r[:, k, :], start=(k == 0), stop=(k == KD - 1))
                        mm.then_inc(logit_psum, 1)
                    pe.wait_ge(w_ready, 2 * i + 2)
                    nc.tensor.transpose(ps_m[:, 0:P], mask[:].rearrange("p a e -> p (a e)"), ident[:]).then_inc(maskT_psum, 1)
                pe.wait_ge(first_ready, 1)
                nc.tensor.transpose(ps_t[0][:, 0:P], first[:], ident[:]).then_inc(firstT_psum, 1)
                pe.wait_ge(firstT_ready, 1)
                for half in range(2):
                    mm = nc.tensor.transpose(ps_t[1][0:E, CAP * half:CAP * half + CAP], firstT[:, E * half:E * half + E], ident[:])
                mm.then_inc(both_psum, 1)
                pe.wait_ge(picked_ready, 1)
                nc.tensor.transpose(ps_l[0][:, 0:E], picked[:], ident[0:E, 0:E]).then_inc(picked_psum, 1)

            @block.scalar
            def _(act):
                act.wait_ge(var_ready, 1)
                nc.scalar.activation(rstd[:, 1], rstd[:, 0], ACT.Sqrt).then_inc(std_ready, 1)
                with act.Fori(0, NI) as i:
                    for half in range(2):
                        n = 2 * i + half
                        act.wait_ge(hT_psum, n + 1)
                        act.wait_ge(logit_psum, 2 * i)
                        nc.scalar.copy(hT[:, half, :, :], ps_t[half][:, 0:KD * P].rearrange("p (k n) -> p k n", k=KD))\
                          .then_inc(hT_ready, 1)
                    for half in range(2):
                        n = 2 * i + half
                        act.wait_ge(nmax_ready, n + 1)
                        nc.scalar.activation(ex[:, half, :], ps_l[half][:, 0:E], ACT.Exp, bias=nmax[:, half:half + 1],
                                             accum_out=esum[:, half:half + 1]).then_inc(ex_ready, 1)

            @block.gpsimd
            def _(pool):
                nc.gpsimd.memset(zeros[:], 0.0).then_inc(zeroed, 1)

            @block.vector
            def _(v):
                v.wait_ge(landed, 48)
                layer_norm_statistics(nc, v, x_res, stats, mv, rstd, dve, var_ready, std_ready)
                step = Steps(v, dve)
                with v.Fori(0, NI) as i:
                    step.begin(2 * NT + 1 + 2 * PAIR * i)
                    v.wait_ge(rows_out, 32 * i)
                    for half in range(2):
                        tile = i + NI * half
                        nc.vector.tensor_scalar(rows[:, 0, half, 0:D], one_tile(x_res, tile), mean_of(mv, tile), rstd_of(rstd, tile),
                                                ALU.subtract, ALU.mult).then_inc(h_ready, 1)
                    for half in range(2):
                        n = 2 * i + half
                        v.wait_ge(logit_psum, n + 1)
                        nc.vector.tensor_reduce(nmax[:, half:half + 1], ps_l[half][:, 0:E], AX.X, ALU.max, negate=True)\
                          .then_inc(nmax_ready, 1)
                    for half in range(2):
                        n = 2 * i + half
                        v.wait_ge(ex_ready, n + 1)
                        step.done(nc.vector.reciprocal(einv[:, half:half + 1], esum[:, half:half + 1]))
                        step.wait()
                        step.done(nc.vector.tensor_scalar(probs[:, half, :], ex[:, half, :], einv[:, half:half + 1], None, ALU.mult))
                        step.wait()
                        carry(nc, waits_v)
                        step.done(nc.vector.max(best[:, half, :], probs[:, half, :]))
                        step.wait()
                        carry(nc, waits_v)
                        step.done(nc.vector.match_replace(left[:, half, :], best[:, half, :], probs[:, half, :], -1.0))
                        step.wait()
                        v.wait_ge(maskT_psum, i)
                        step.done(nc.vector.tensor_scalar(mask[:, half, :], left[:, half, :], 0.0, None, ALU.is_lt))
                        step.wait()
                        step.done(nc.vector.tensor_tensor(wraw[:, half, :], mask[:, half, :], probs[:, half, :], ALU.mult))
                        step.wait()
                        step.done(nc.vector.tensor_reduce(wsum[:, half:half + 1], wraw[:, half, :], AX.X, ALU.add))
                        step.wait()
                        step.done(nc.vector.reciprocal(winv[:, half:half + 1], wsum[:, half:half + 1]))
                        step.wait()
                        nc.vector.tensor_scalar(rows[:, 0, half, D:ROW], wraw[:, half, :], winv[:, half:half + 1], None,
                                                ALU.mult).then_inc(w_ready, 1)
                    v.wait_ge(maskT_psum, i + 1)
                    nc.vector.tensor_tensor(keys[:, bass.ds(i * P, P)], ps_m[:, 0:P], keyval[:, bass.ds(i * P, P)], ALU.mult)\
                      .then_inc(key_done, 1)
                    step.end(2 * PAIR)
                step.begin(2 * NT + 1 + 2 * PAIR * NI)
                v.wait_ge(key_done, NI)
                for source, dest in ((keys, first), (both, picked)):
                    if source is both:
                        v.wait_ge(first_ready, 1)
                        v.wait_ge(firstT_psum, 1)
                        nc.vector.tensor_copy(firstT[:], ps_t[0][:, 0:P]).then_inc(firstT_ready, 1)
                        v.wait_ge(both_psum, 1)
                        step.done(nc.vector.tensor_copy(both[:], ps_t[1][0:E, 0:2 * CAP]))
                        step.wait()
                    for r in range(CAP // TOPK):
                        ins = nc.vector.max(dest[:, TOPK * r:TOPK * r + TOPK], source[:])
                        if r == CAP // TOPK - 1:
                            ins.then_inc(first_ready if source is keys else picked_ready, 1)
                            continue
                        step.done(ins)
                        step.wait()
                        step.done(nc.vector.match_replace(source[:], dest[:, TOPK * r:TOPK * r + TOPK], source[:], 0.0))
                        step.wait()
                v.wait_ge(picked_psum, 1)
                step.done(nc.vector.tensor_scalar(empty[:], ps_l[0][:, 0:E], 0.0, slot_no[:, 0:1], ALU.is_equal, ALU.mult))
                step.wait()
                step.done(nc.vector.tensor_tensor(token_f[:], empty[:], ps_l[0][:, 0:E], ALU.subtract))
                step.wait()
                nc.vector.tensor_scalar(slot_token[:], token_f[:], float(T), None, ALU.add).then_inc(slots_ready, 1)
                v.wait_ge(slots_ready, 1)

        experts(nc, name + "e", consts, slot_token, gate_up_dram, down_dram, rows_dram, x_dram, x_res)


def experts(nc, name, consts, slot_token, gate_up_dram, down_dram, rows_dram, x_dram, x_res):
    ident = consts["ident"]
    R = 4
    ROW = D + E
    with ExitStack() as ctx:
        sb, pb, sem = allocators(nc, ctx, name)
        waits_p = sb("waits_p", [P, 2 + R], F32)
        slot = [sb(f"slot{j}", [P, 1], I32) for j in range(R)]
        rows = [sb(f"rows{j}", [P, ROW], F32) for j in range(R)]
        w_gu = [sb(f"w_gu{j}", [P, KD, 2 * FE], F32) for j in range(R)]
        w_dn = [sb(f"w_dn{j}", [FE, D], F32) for j in range(R)]
        hT = [sb(f"hT{j}", [P, KD * P], F32) for j in range(2)]
        gated = [sb(f"gated{j}", [FE, P], F32) for j in range(2)]
        mid = [sb(f"mid{j}", [FE, P], F32) for j in range(2)]
        weight = [sb(f"weight{j}", [P, 1], F32) for j in range(R)]
        y = [sb(f"y{j}", [P, D], F32) for j in range(R)]
        ps_t = [pb(f"ps_t{i}", [P, 512], F32) for i in range(2)]
        ps_g = [pb(f"ps_g{i}", [P, 512], F32) for i in range(2)]
        ps_u = [pb(f"ps_u{i}", [P, 512], F32) for i in range(2)]
        ps_y = [pb(f"ps_y{i}", [P, 512], F32) for i in range(2)]
        gathered = [sem(f"gathered{j}") for j in range(R)]
        w_landed = [sem(f"w_landed{j}") for j in range(R)]
        added = sem("added")
        waits_set, carried = sem("waits_set"), sem("carried")
        slot_ready, hT_psum, hT_ready = sem("slot_ready"), sem("hT_psum"), sem("hT_ready")
        gu_psum, silu_ready, mid_ready, y_psum, y_ready = sem("gu_psum"), sem("silu_ready"), sem("mid_ready"), sem("y_psum"), sem("y_ready")
        weight_ready = sem("weight_ready")
        back = sem("back")
        block = ctx.enter_context(nc.Block())

        @block.sync
        def _(sp):
            with sp.Fori(0, E // R) as i:
                for j in range(R):
                    e = R * i + j
                    sp.wait_ge(y_psum, R * i)
                    sp.dma_start(w_gu[j][:], gate_up_dram[bass.ds(e, 1)].rearrange("o (k p) f -> p (o k) f", p=P)).then_inc(w_landed[j], 16)
                    sp.dma_start(w_dn[j][:], down_dram[bass.ds(e, 1)].rearrange("o f d -> f (o d)")).then_inc(w_landed[j], 16)
            sp.wait_ge(added, 16 * E)
            sp.dma_start(x_res[:], x_dram[0:T, :].rearrange("(t p) d -> p t d", p=P)).then_inc(back, 16)
            sp.wait_ge(back, 16)

        @block.gpsimd
        def _(pool):

            def gather(e, j):
                nc.gpsimd.indirect_dma_start(rows[j][:], None, rows_dram, bass.IndirectOffsetOnAxis(slot[j][:, 0:1], 0))\
                  .then_inc(gathered[j], 16)

            nc.gpsimd.memset(waits_p[:], 0.0).then_inc(waits_set, 1)
            pool.wait_ge(waits_set, 1)
            with pool.Fori(0, E // R) as i:
                pool.wait_ge(slot_ready, R * i + R)
                carry_on_pool(nc, waits_p, 1, carried, (R + 1) * i)
                for j in range(R):
                    gather(R * i + j, j)
                for j in range(R):
                    e = R * i + j
                    pool.wait_ge(y_ready, e + 1)
                    pool.wait_ge(added, 16 * e)
                    carry_on_pool(nc, waits_p, 2 + j, carried, (R + 1) * i)
                    nc.gpsimd.indirect_dma_start(x_dram, bass.IndirectOffsetOnAxis(slot[j][:, 0:1], 0), y[j][:], None,
                                                 bounds_check=T + P - 1, oob_is_err=True, compute_op=ALU.add).then_inc(added, 16)
            pool.wait_ge(added, 16 * E)

        @block.tensor
        def _(pe):
            with pe.Fori(0, E // R) as i:
                for j in range(R):
                    e = R * i + j
                    pe.wait_ge(gathered[j], 16 * i + 16)
                    if j >= 2:
                        pe.wait_ge(hT_ready, e - 1)
                    else:
                        pe.wait_ge(hT_ready, R * i)
                    for k in range(KD):
                        mm = nc.tensor.transpose(ps_t[j % 2][:, P * k:P * k + P], rows[j][:, P * k:P * k + P], ident[:])
                    mm.then_inc(hT_psum, 1)
                    pe.wait_ge(w_landed[j], 32 * i + 32)
                    pe.wait_ge(hT_ready, e + 1)
                    if j >= 2:
                        pe.wait_ge(mid_ready, e - 1)
                    else:
                        pe.wait_ge(mid_ready, R * i)
                    for base, ps in ((FE, ps_u), (0, ps_g)):
                        for k in range(KD):
                            mm = nc.tensor.matmul(ps[j % 2][0:FE, 0:P], w_gu[j][:, k, base:base + FE], hT[j % 2][:, P * k:P * k + P],
                                                  start=(k == 0), stop=(k == KD - 1))
                    mm.then_inc(gu_psum, 1)
                    pe.wait_ge(mid_ready, e + 1)
                    if j >= 2:
                        pe.wait_ge(y_ready, e - 1)
                    else:
                        pe.wait_ge(y_ready, R * i)
                    nc.tensor.matmul(ps_y[j % 2][:, 0:D], mid[j % 2][:], w_dn[j][:], start=True, stop=True).then_inc(y_psum, 1)

        @block.scalar
        def _(act):
            with act.Fori(0, E // R) as i:
                for j in range(R):
                    e = R * i + j
                    act.wait_ge(hT_psum, e + 1)
                    nc.scalar.copy(hT[j % 2][:], ps_t[j % 2][:, 0:KD * P]).then_inc(hT_ready, 1)
                    act.wait_ge(gu_psum, e + 1)
                    nc.scalar.activation(gated[j % 2][:], ps_g[j % 2][0:FE, 0:P], ACT.Silu).then_inc(silu_ready, 1)

        @block.vector
        def _(v):
            with v.Fori(0, E // R) as i:
                for j in range(R):
                    e = R * i + j
                    v.wait_ge(added, 16 * R * i)
                    nc.vector.tensor_copy(slot[j][:], slot_token[:, bass.ds(e, 1)]).then_inc(slot_ready, 1)
                for j in range(R):
                    e = R * i + j
                    v.wait_ge(gathered[j], 16 * i + 16)
                    nc.vector.tensor_copy(weight[j][:], rows[j][:, bass.ds(D + e, 1)]).then_inc(weight_ready, 1)
                    v.wait_ge(silu_ready, e + 1)
                    nc.vector.tensor_tensor(mid[j % 2][:], gated[j % 2][:], ps_u[j % 2][0:FE, 0:P], ALU.mult).then_inc(mid_ready, 1)
                    v.wait_ge(y_psum, e + 1)
                    v.wait_ge(weight_ready, e + 1)
                    nc.vector.tensor_scalar(y[j][:], ps_y[j % 2][:, 0:D], weight[j][:, 0:1], None, ALU.mult).then_inc(y_ready, 1)


def state_space_layer(nc, x_res, consts, w_in_dram, w_out_dram, vec, mats):
    ident = consts["ident"]
    NH, NP_, DI, TAPS = 4, 128, 512, 4
    KI = DI // P
    PROJ = 2 * DI + NH + 2 * P
    DT0, B0, C0 = 2 * DI, 2 * DI + NH, 2 * DI + NH + P
    RMS_EPS = 1e-6
    with ExitStack() as ctx:
        sb, pb, sem = allocators(nc, ctx, "ssm")
        w_in = sb("w_in", [P, KD, PROJ], F32)
        w_out = sb("w_out", [P, KI, D], F32)
        cols = sb("cols", [P, KD + 2 * KI + KI * TAPS], F32)
        norm_c = cols[:, 0:KD]
        conv_b = cols[:, KD:KD + KI]
        skip_c = cols[:, KD + KI:KD + 2 * KI]
        conv_w = cols[:, KD + 2 * KI:].rearrange("p (c k) -> p c k", k=TAPS)
        heads = sb("heads", [P, 2, NH], F32)
        upper = sb("upper", [P, P], F32)
        last = sb("last", [P, P], F32)
        waits_p = sb("waits_p", [P, 2], F32)
        h_all = sb("h_all", [P, NT, D], F32)
        hT_all = sb("hT_all", [P, KD, T], F32)
        stats = sb("stats", [P, NT, 6], F32)
        mv = sb("mv", [P, NT, 2], F32)
        rstd = sb("rstd", [P, 3, NT], F32)
        rms = sb("rms", [P, 4, NT], F32)
        z = sb("z", [P, NT, NH], F32)
        spl = sb("spl", [P, 3, NT * NH], F32)
        dt = sb("dt", [P, NT, NH], F32)
        a_neg = sb("a_neg", [P, NH], F32)
        log_a = sb("log_a", [P, NT, NH], F32)
        cum = sb("cum", [P, NT, NH], F32)
        to_end = sb("to_end", [P, NT, NH], F32)
        dec_end = sb("dec_end", [P, NT, NH], F32)
        dec_in = sb("dec_in", [P, NT, NH], F32)
        dec_chunk = sb("dec_chunk", [P, NT, NH], F32)

        with ExitStack() as ctx1:
            sb1, pb1, sem1 = allocators(nc, ctx1, "ssm_a")
            square = sb1("square", [P, 2, D], F32)
            hn = sb1("hn", [P, 2, D], F32)
            hT = sb1("hT", [P, 2, KD, P], F32)
            ps_t = [pb1(f"ps_t{i}", [P, 512], F32) for i in range(2)]
            ps_d = [pb1(f"ps_d{i}", [P, 512], F32) for i in range(2)]
            landed, scaled = sem1("landed"), sem1("scaled")
            dve = sem1("dve")
            var_ready, std_ready = sem1("var_ready"), sem1("std_ready")
            h_ready, squared, ms_ready, root_ready = sem1("h_ready"), sem1("squared"), sem1("ms_ready"), sem1("root_ready")
            hn_ready, hT_psum, hT_ready, dt_psum, z_done = sem1("hn_ready"), sem1("hT_psum"), sem1("hT_ready"), sem1("dt_psum"), sem1("z_done")
            carried = sem1("carried")
            kept, added = sem1("kept"), sem1("added")
            z_parts, exp_ready, log_ready = sem1("z_parts"), sem1("exp_ready"), sem1("log_ready")
            la_ready, cum_psum, cum_ready, end_psum, ends_ready, decays = (sem1(n) for n in (
                "la_ready", "cum_psum", "cum_ready", "end_psum", "ends_ready", "decays"))
            block = ctx1.enter_context(nc.Block())
            LOADS = 6

            @block.sync
            def _(sp):
                sp.dma_start(w_in[:], w_in_dram.rearrange("(k p) n -> p k n", p=P)).then_inc(landed, 16)
                sp.dma_start(w_out[:], w_out_dram.rearrange("(k p) n -> p k n", p=P)).then_inc(landed, 16)
                sp.dma_start(cols[:], vec[0]).then_inc(landed, 16)
                sp.dma_start(heads[:].rearrange("p a h -> p (a h)"), vec[1].partition_broadcast(P)).then_inc(landed, 16)
                sp.dma_start(upper[:], mats[0]).then_inc(landed, 16)
                sp.dma_start(last[:], mats[1]).then_inc(landed, 16)

            @block.tensor
            def _(pe):
                pe.wait_ge(scaled, KD)
                with pe.Fori(0, NT // 2) as i:
                    for par in range(2):
                        n = 2 * i + par
                        pe.wait_ge(hn_ready, n + 1)
                        for k in range(KD):
                            mm = nc.tensor.transpose(ps_t[par][:, P * k:P * k + P], hn[:, par, P * k:P * k + P], ident[:])
                        mm.then_inc(hT_psum, 1)
                    for par in range(2):
                        n = 2 * i + par
                        pe.wait_ge(hT_ready, n + 1)
                        for k in range(KD):
                            mm = nc.tensor.matmul(ps_d[par][:, 0:NH], hT[:, par, k, :], w_in[:, k, DT0:DT0 + NH],
                                                  start=(k == 0), stop=(k == KD - 1))
                        mm.then_inc(dt_psum, 1)
                pe.wait_ge(la_ready, 1)
                nc.tensor.matmul(ps_t[0][:, 0:NT * NH], upper[:], log_a[:].rearrange("p t h -> p (t h)"), start=True, stop=True)\
                  .then_inc(cum_psum, 1)
                pe.wait_ge(cum_ready, 1)
                nc.tensor.matmul(ps_t[1][:, 0:NT * NH], last[:], cum[:].rearrange("p t h -> p (t h)"), start=True, stop=True)\
                  .then_inc(end_psum, 1)

            @block.scalar
            def _(act):
                act.wait_ge(var_ready, 1)
                nc.scalar.activation(rstd[:, 1], rstd[:, 0], ACT.Sqrt).then_inc(std_ready, 1)
                with act.Fori(0, NT // 2) as i:
                    for par in range(2):
                        n = 2 * i + par
                        act.wait_ge(h_ready, n + 1)
                        act.wait_ge(squared, n)
                        nc.scalar.activation(square[:, 0, :], one_tile(h_all, n), ACT.Square,
                                             accum_out=rms[:, 0, bass.ds(n, 1)]).then_inc(squared, 1)
                act.wait_ge(ms_ready, 1)
                nc.scalar.activation(rms[:, 2], rms[:, 1], ACT.Sqrt).then_inc(root_ready, 1)
                with act.Fori(0, NT // 2) as i:
                    for par in range(2):
                        n = 2 * i + par
                        act.wait_ge(hT_psum, n + 1)
                        act.wait_ge(dt_psum, 2 * i)
                        act.wait_ge(kept, 2 * i + 1)
                        nc.scalar.copy(hT[:, par, :, :], ps_t[par][:, 0:KD * P].rearrange("p (k n) -> p k n", k=KD))\
                          .then_inc(hT_ready, 1)
                act.wait_ge(z_parts, 1)
                nc.scalar.activation(spl[:, 1], spl[:, 0], ACT.Exp).then_inc(exp_ready, 1)
                nc.scalar.activation(a_neg[:], heads[:, 0, :], ACT.Exp).then_inc(exp_ready, 1)
                act.wait_ge(exp_ready, 1)
                nc.scalar.activation(spl[:, 2], spl[:, 1], ACT.Ln, bias=1.0).then_inc(log_ready, 1)
                act.wait_ge(ends_ready, 1)
                for out, in_ in ((dec_end, to_end), (dec_in, cum), (dec_chunk, dec_chunk)):
                    nc.scalar.activation(out[:], in_[:], ACT.Exp).then_inc(decays, 1)

            @block.gpsimd
            def _(pool):
                nc.gpsimd.memset(waits_p[:], 0.0).then_inc(kept, 1)
                pool.wait_ge(kept, 1)
                with pool.Fori(0, NT // 2) as i:
                    for par in range(2):
                        n = 2 * i + par
                        pool.wait_ge(hT_ready, n + 1)
                        carry_on_pool(nc, waits_p, 1, carried, n)
                        nc.gpsimd.tensor_copy(hT_all[:, :, bass.ds(n * P, P)], hT[:, par, :, :]).then_inc(kept, 1)
                        nc.gpsimd.tensor_tensor(one_tile(x_res, n), one_tile(x_res, n), one_tile(h_all, n), ALU.add).then_inc(added, 1)

            @block.vector
            def _(v):
                v.wait_ge(landed, 16 * LOADS)
                for k in range(KD):
                    nc.vector.tensor_scalar(w_in[:, k, :], w_in[:, k, :], norm_c[:, k:k + 1], None, ALU.mult).then_inc(scaled, 1)
                layer_norm_statistics(nc, v, x_res, stats, mv, rstd, dve, var_ready, std_ready)
                step = Steps(v, dve)
                with v.Fori(0, NT // 4) as i:
                    for j in range(4):
                        n = 4 * i + j
                        nc.vector.tensor_scalar(one_tile(h_all, n), one_tile(x_res, n), mean_of(mv, n), rstd_of(rstd, n),
                                                ALU.subtract, ALU.mult).then_inc(h_ready, 1)
                v.wait_ge(squared, NT)
                v.wait_ge(h_ready, NT)
                nc.vector.tensor_scalar(rms[:, 1], rms[:, 0], 1.0 / D, RMS_EPS, ALU.mult, ALU.add).then_inc(ms_ready, 1)
                v.wait_ge(root_ready, 1)
                step.begin(2 * NT + 1)
                step.done(nc.vector.reciprocal(rms[:, 3], rms[:, 2]))
                step.wait()
                with v.Fori(0, NT // 2) as i:
                    for par in range(2):
                        n = 2 * i + par
                        v.wait_ge(hT_psum, 2 * i)
                        nc.vector.tensor_scalar(hn[:, par, :], one_tile(h_all, n), rms[:, 3, bass.ds(n, 1)], None, ALU.mult)\
                          .then_inc(hn_ready, 1)
                    for par in range(2):
                        n = 2 * i + par
                        v.wait_ge(dt_psum, n + 1)
                        nc.vector.tensor_tensor(z[:, bass.ds(n, 1), :].rearrange("p o h -> p (o h)"), ps_d[par][:, 0:NH],
                                                heads[:, 1, :], ALU.add).then_inc(z_done, 1)
                v.wait_ge(z_done, NT)
                zf = z[:].rearrange("p t h -> p (t h)")
                step.done(nc.vector.tensor_scalar(spl[:, 1], zf, -1.0, None, ALU.mult))
                step.wait()
                nc.vector.tensor_tensor(spl[:, 0], zf, spl[:, 1], ALU.min).then_inc(z_parts, 1)
                v.wait_ge(log_ready, 1)
                dtf, laf = dt[:].rearrange("p t h -> p (t h)"), log_a[:]
                step.done(nc.vector.scalar_tensor_tensor(dtf, zf, 0.0, spl[:, 2], ALU.max, ALU.add))
                step.wait()
                v.wait_ge(exp_ready, 2)
                nc.vector.scalar_tensor_tensor(laf, dt[:], -1.0, a_neg[:].unsqueeze(1).to_broadcast([P, NT, NH]), ALU.mult, ALU.mult)\
                  .then_inc(la_ready, 1)
                v.wait_ge(cum_psum, 1)
                nc.vector.tensor_copy(cum[:].rearrange("p t h -> p (t h)"), ps_t[0][:, 0:NT * NH]).then_inc(cum_ready, 1)
                v.wait_ge(end_psum, 1)
                v.wait_ge(cum_ready, 1)
                end = ps_t[1][:, 0:NT * NH]
                step.done(nc.vector.tensor_tensor(to_end[:].rearrange("p t h -> p (t h)"), end, cum[:].rearrange("p t h -> p (t h)"),
                                                  ALU.subtract))
                nc.vector.tensor_copy(dec_chunk[:].rearrange("p t h -> p (t h)"), end).then_inc(ends_ready, 1)
                v.wait_ge(decays, 3)

        with ExitStack() as ctx2:
            sb2, pb2, sem2 = allocators(nc, ctx2, "ssm_b")
            gate = sb2("gate", [P, KI, S], F32)
            HIST = TAPS - 1
            u = sb2("u", [P, KI, HIST + S], F32)
            acc = sb2("acc", [P, 2, S], F32)
            xs = u
            bT = sb2("bT", [P, S], F32)
            cT = sb2("cT", [P, S], F32)
            state = sb2("state", [P, NH, NP_], F32)
            b_tok = sb2("b_tok", [P, P], F32)
            x_dt = sb2("x_dt", [P, NH, NP_], F32)
            x_end = sb2("x_end", [P, NH, NP_], F32)
            diff = sb2("diff", [P, NH, P], F32)
            decay = sb2("decay", [P, NH, P], F32)
            cb = sb2("cb", [P, P], F32)
            cum_c = sb2("cum_c", [P, NH], F32)
            mix = sb2("mix", [P, NH, P], F32)
            y_in = sb2("y_in", [P, NH, NP_], F32)
            y_tok = sb2("y_tok", [P, NH, NP_], F32)
            yT = sb2("yT", [P, NH, P], F32)
            zT = sb2("zT", [P, NH, P], F32)
            ps_x, ps_b, ps_r, ps_y, ps_i, ps_s, ps_z, ps_o = (pb2(f"ps{i}", [P, 512], F32) for i in range(8))
            proj_banks = (ps_y, ps_i, ps_s, ps_z)
            dve = sem2("dve")
            proj_psum, gate_done, other_done = sem2("proj_psum"), sem2("gate_done"), sem2("other_done")
            conv_ready, conv_done = sem2("conv_ready"), sem2("conv_done")
            x_psum, bc_psum, row_psum, diff_ready, decay_ready = (sem2(n) for n in ("x_psum", "bc_psum", "row_psum", "diff_ready", "decay_ready"))
            cum_c_ready, carried = sem2("cum_c_ready"), sem2("carried")
            cb_ready, mix_ready, xdt_ready, xend_ready, state_ready = (sem2(n) for n in ("cb_ready", "mix_ready", "xdt_ready", "xend_ready", "state_ready"))
            intra_psum, inter_psum, local_psum, y_ready = (sem2(n) for n in ("intra_psum", "inter_psum", "local_psum", "y_ready"))
            yT_psum, zT_ready, out_psum, x_done = (sem2(n) for n in ("yT_psum", "zT_ready", "out_psum", "x_done"))
            block = ctx2.enter_context(nc.Block())
            HALF = 512
            UNITS = []
            for half in range(S // HALF):
                for c in range(KI):
                    UNITS += [(c * P, "gate", c, half), (DI + c * P, "u", c, half)]
                UNITS += [(B0, "b", 0, half), (C0, "c", 0, half)]
            NG_ = sum(kind == "gate" for _, kind, _, _ in UNITS)
            NO_ = len(UNITS) - NG_

            def done_before(n):
                g = sum(kind == "gate" for _, kind, _, _ in UNITS[:n])
                return g, n - g

            DVE_B = KI * (TAPS - 1)
            DVE_C = 2

            def of_heads(values, n):
                return values[:, bass.ds(n, 1), :].rearrange("p o h -> p (o h)").unsqueeze(2).to_broadcast([P, NH, NP_])

            @block.tensor
            def _(pe):
                def spread(n, c):
                    tok = slice(P * c, P * c + P)
                    pe.wait_ge(xdt_ready, n)
                    for h in range(NH):
                        mm = nc.tensor.transpose(ps_x[:, P * h:P * h + P], xs[:, h, HIST + P * c:HIST + P * c + P], ident[:])
                    mm.then_inc(x_psum, 1)
                    pe.wait_ge(cb_ready, n)
                    nc.tensor.transpose(ps_b[:, 0:P], bT[:, tok], ident[:])
                    nc.tensor.matmul(ps_b[:, P:2 * P], bT[:, tok], cT[:, tok], start=True, stop=True).then_inc(bc_psum, 1)
                    pe.wait_ge(diff_ready, n)
                    pe.wait_ge(cum_c_ready, n + 1)
                    for h in range(NH):
                        mm = nc.tensor.transpose(ps_r[:, P * h:P * h + P], cum_c[:, h:h + 1].to_broadcast([P, P]), ident[:])
                    mm.then_inc(row_psum, 1)

                def scan(b, c):
                    n = TS * b + c
                    pe.wait_ge(y_ready, n)
                    pe.wait_ge(state_ready, (TS + 1) * b + c + 1)
                    nc.tensor.matmul(ps_i[:], cT[:, P * c:P * c + P], state[:].rearrange("p h d -> p (h d)"), start=True, stop=True)\
                      .then_inc(inter_psum, 1)
                    pe.wait_ge(mix_ready, n + 1)
                    pe.wait_ge(xdt_ready, n + 1)
                    for h in range(NH):
                        mm = nc.tensor.matmul(ps_y[:, P * h:P * h + P], mix[:, h, :], x_dt[:, h, :], start=True, stop=True)
                    mm.then_inc(intra_psum, 1)
                    pe.wait_ge(xend_ready, n + 1)
                    pe.wait_ge(cb_ready, n + 1)
                    nc.tensor.matmul(ps_s[:], b_tok[:], x_end[:].rearrange("p h d -> p (h d)"), start=True, stop=True).then_inc(local_psum, 1)

                def finish(n):
                    pe.wait_ge(y_ready, n + 1)
                    pe.wait_ge(zT_ready, n)
                    for h in range(NH):
                        mm = nc.tensor.transpose(ps_z[:, P * h:P * h + P], y_tok[:, h, :], ident[:])
                    mm.then_inc(yT_psum, 1)
                    pe.wait_ge(zT_ready, n + 1)
                    pe.wait_ge(x_done, n)
                    for h in range(NH):
                        mm = nc.tensor.matmul(ps_o[:, 0:D], zT[:, h, :], w_out[:, h, :], start=(h == 0), stop=(h == NH - 1))
                    mm.then_inc(out_psum, 1)

                with pe.Fori(0, B) as b:
                    for n, (col, kind, c, half) in enumerate(UNITS):
                        if n >= 4:
                            g, o = done_before(n - 3)
                            if UNITS[n - 4][1] == "gate":
                                pe.wait_ge(gate_done, NG_ * b + g)
                            else:
                                pe.wait_ge(other_done, NO_ * b + o)
                        elif n == 0:
                            pe.wait_ge(x_done, TS * b)
                        for k in range(KD):
                            mm = nc.tensor.matmul(proj_banks[n % 4][:], w_in[:, k, col:col + P],
                                                  hT_all[:, k, bass.ds(b * S + half * HALF, HALF)], start=(k == 0), stop=(k == KD - 1))
                        mm.then_inc(proj_psum, 1)
                    pe.wait_ge(conv_done, KI * b + KI)
                    pe.wait_ge(other_done, NO_ * b + NO_)
                    pe.wait_ge(gate_done, NG_ * b + NG_)
                    spread(TS * b, 0)
                    for c in range(TS):
                        scan(b, c)
                        if c < TS - 1:
                            spread(TS * b + c + 1, c + 1)
                        finish(TS * b + c)

            @block.scalar
            def _(act):
                with act.Fori(0, B) as b:
                    act.wait_ge(zT_ready, TS * b)
                    g = 0
                    for n, (col, kind, c, half) in enumerate(UNITS):
                        if kind == "gate":
                            act.wait_ge(proj_psum, len(UNITS) * b + n + 1)
                            nc.scalar.activation(gate[:, c, HALF * half:HALF * half + HALF], proj_banks[n % 4][:], ACT.Silu).then_inc(gate_done, 1)
                    for c in range(KI):
                        act.wait_ge(conv_ready, KI * b + c + 1)
                        nc.scalar.activation(xs[:, c, HIST:], acc[:, c % 2, :], ACT.Silu).then_inc(conv_done, 1)
                    for c in range(TS):
                        n = TS * b + c
                        act.wait_ge(diff_ready, n + 1)
                        act.wait_ge(mix_ready, n)
                        nc.scalar.activation(decay[:], diff[:], ACT.Exp).then_inc(decay_ready, 1)

            @block.gpsimd
            def _(pool):
                with pool.Fori(0, B) as b:
                    for c in range(TS):
                        n = TS * b + c
                        pool.wait_ge(row_psum, n)
                        carry_on_pool(nc, waits_p, 1, carried, n)
                        nc.gpsimd.tensor_copy(cum_c[:], cum[:, bass.ds(n, 1), :].rearrange("p o h -> p (o h)")).then_inc(cum_c_ready, 1)
                        pool.wait_ge(xdt_ready, n + 1)
                        pool.wait_ge(local_psum, n)
                        nc.gpsimd.tensor_tensor(x_end[:], x_dt[:], of_heads(dec_end, n), ALU.mult).then_inc(xend_ready, 1)

            @block.vector
            def _(v):
                step = Steps(v, dve)
                nc.vector.memset(u[:, :, 0:HIST], 0.0).then_inc(dve, 1)
                v.wait_ge(dve, 1)

                def inputs(n):
                    v.wait_ge(x_psum, n + 1)
                    v.wait_ge(intra_psum, n)
                    v.wait_ge(xend_ready, n)
                    nc.vector.tensor_tensor(x_dt[:], ps_x[:].rearrange("p (h d) -> p h d", h=NH), of_heads(dt, n), ALU.mult)\
                      .then_inc(xdt_ready, 1)
                    v.wait_ge(bc_psum, n + 1)
                    v.wait_ge(local_psum, n)
                    nc.vector.tensor_copy(b_tok[:], ps_b[:, 0:P])
                    nc.vector.tensor_tensor(cb[:], ps_b[:, P:2 * P], upper[:], ALU.mult).then_inc(cb_ready, 1)
                    v.wait_ge(row_psum, n + 1)
                    v.wait_ge(decay_ready, n)
                    for h in range(NH):
                        ins = nc.vector.tensor_scalar(diff[:, h, :], ps_r[:, P * h:P * h + P], cum[:, bass.ds(n, 1), h:h + 1].rearrange("p o h -> p (o h)"),
                                                      0.0, ALU.subtract, ALU.min)
                    ins.then_inc(diff_ready, 1)

                with v.Fori(0, B) as b:
                    step.begin(1 + (DVE_B + DVE_C * TS) * b)
                    v.wait_ge(x_psum, TS * b)
                    v.wait_ge(inter_psum, TS * b)
                    for n, (col, kind, c, half) in enumerate(UNITS):
                        if kind == "gate":
                            continue
                        v.wait_ge(proj_psum, len(UNITS) * b + n + 1)
                        dst = {"u": u[:, c, HIST + HALF * half:HIST + HALF * half + HALF], "b": bT[:, HALF * half:HALF * half + HALF],
                               "c": cT[:, HALF * half:HALF * half + HALF]}[kind]
                        nc.vector.tensor_copy(dst, proj_banks[n % 4][:]).then_inc(other_done, 1)
                    nc.vector.memset(state[:], 0.0).then_inc(state_ready, 1)
                    v.wait_ge(other_done, NO_ * b + NO_)
                    for c in range(KI):
                        v.wait_ge(conv_done, KI * b + max(c - 1, 0))
                        for k in range(TAPS):
                            tap = u[:, c, k:k + S]
                            if k == 0:
                                step.done(nc.vector.tensor_scalar(acc[:, c % 2, :], tap, conv_w[:, c, 0:1], conv_b[:, c:c + 1], ALU.mult, ALU.add))
                                step.wait()
                                continue
                            ins = nc.vector.scalar_tensor_tensor(acc[:, c % 2, :], tap, conv_w[:, c, k:k + 1], acc[:, c % 2, :], ALU.mult, ALU.add)
                            if k < TAPS - 1:
                                step.done(ins)
                                step.wait()
                            else:
                                ins.then_inc(conv_ready, 1)
                    inputs(TS * b)
                    for c in range(TS):
                        n = TS * b + c
                        v.wait_ge(decay_ready, n + 1)
                        v.wait_ge(cb_ready, n + 1)
                        v.wait_ge(intra_psum, n)
                        nc.vector.tensor_tensor(mix[:], decay[:], cb[:].unsqueeze(1).to_broadcast([P, NH, P]), ALU.mult).then_inc(mix_ready, 1)
                        v.wait_ge(inter_psum, n + 1)
                        step.done(nc.vector.tensor_tensor(y_in[:], ps_i[:].rearrange("p (h d) -> p h d", h=NH), of_heads(dec_in, n), ALU.mult))
                        step.wait()
                        v.wait_ge(intra_psum, n + 1)
                        v.wait_ge(yT_psum, n)
                        nc.vector.tensor_tensor(y_tok[:], y_in[:], ps_y[:].rearrange("p (h d) -> p h d", h=NH), ALU.add).then_inc(y_ready, 1)
                        v.wait_ge(local_psum, n + 1)
                        v.wait_ge(state_ready, (TS + 1) * b + c + 1)
                        for h in range(NH):
                            ins = nc.vector.scalar_tensor_tensor(state[:, h, :], state[:, h, :], dec_chunk[:, bass.ds(n, 1), h:h + 1].rearrange("p o h -> p (o h)"),
                                                                 ps_s[:, P * h:P * h + P], ALU.mult, ALU.add)
                        ins.then_inc(state_ready, 1)
                        if c < TS - 1:
                            inputs(n + 1)
                        v.wait_ge(yT_psum, n + 1)
                        for h in range(NH):
                            ins = nc.vector.scalar_tensor_tensor(yT[:, h, :], xs[:, h, HIST + P * c:HIST + P * c + P], skip_c[:, h:h + 1],
                                                                 ps_z[:, P * h:P * h + P], ALU.mult, ALU.add)
                        step.done(ins)
                        step.wait()
                        v.wait_ge(out_psum, n)
                        nc.vector.tensor_tensor(zT[:], yT[:], gate[:, :, P * c:P * c + P], ALU.mult).then_inc(zT_ready, 1)
                        v.wait_ge(out_psum, n + 1)
                        nc.vector.tensor_tensor(one_tile(x_res, n), one_tile(x_res, n), ps_o[:, 0:D], ALU.add).then_inc(x_done, 1)
                    step.end(DVE_B + DVE_C * TS)

def load_phase(nc, x_dram, const_dram, x_res, consts):
    with ExitStack() as ctx:
        sb, pb, sem = allocators(nc, ctx, "load")
        masks = sb("masks", [P, 3, P], F32)
        landed, copied = sem("landed"), sem("copied")
        block = ctx.enter_context(nc.Block())

        @block.sync
        def _(sp):
            sp.dma_start(consts["ident"][:], const_dram[0]).then_inc(landed, 16)
            sp.dma_start(masks[:], const_dram[0:3].rearrange("m p n -> p m n")).then_inc(landed, 16)
            sp.dma_start(x_res[:], x_dram.rearrange("(t p) d -> p t d", p=P)).then_inc(landed, 16)
            sp.wait_ge(landed, 48)

        @block.vector
        def _(v):
            v.wait_ge(landed, 48)
            for i, what in enumerate(("ident_b", "causal_q", "causal_k")):
                nc.vector.tensor_copy(consts[what][:], masks[:, i, :]).then_inc(copied, 1)
            v.wait_ge(copied, 3)


def store_phase(nc, x_res, out_dram):
    with ExitStack() as ctx:
        sb, pb, sem = allocators(nc, ctx, "store")
        stored = sem("stored")
        block = ctx.enter_context(nc.Block())

        @block.sync
        def _(sp):
            sp.dma_start(out_dram.rearrange("(t p) d -> p t d", p=P), x_res[:]).then_inc(stored, 16)
            sp.wait_ge(stored, 16)


def program(nc, a, out):
    moe_rows = nc.dram_tensor("moe_rows", [T + P, D + E], F32).ap()
    moe_x = nc.dram_tensor("moe_x", [T + P, D], F32).ap()
    with ExitStack() as ctx:
        def sb(what, shape, dt):
            return ctx.enter_context(nc.sbuf_tensor(what, shape, dt))

        x_res = sb("x_res", [P, NT, D], F32)
        consts = {"ident": sb("ident", [P, P], F32), "ident_b": sb("ident_b", [P, P], BF16),
                  "causal_q": sb("causal_q", [P, P], BF16), "causal_k": sb("causal_k", [P, P], BF16)}
        load_phase(nc, a["x"], a["masks"], x_res, consts)
        attention_layer(nc, "attn1", x_res, consts, a["wqkv1"], a["wo1"], a["rope"])
        with ExitStack() as mlp:
            w_ug = mlp.enter_context(nc.sbuf_tensor("w_ug", [P, KD, 2 * INTER], F32))
            w_dn = mlp.enter_context(nc.sbuf_tensor("w_dn", [P, INTER // P, D], F32))
            mlp_weights(nc, w_ug, w_dn, a["wug"], a["wdn"], a["had"], a["su_ug"], a["scale_ug"], a["su_dp"], a["scale_dp"])
            mlp_layer(nc, "mlp1", x_res, consts, w_ug, w_dn)
            attention_layer(nc, "attn2", x_res, consts, a["wqkv2"], a["wo2"], None)
            mlp_layer(nc, "mlp2", x_res, consts, w_ug, w_dn)
        attention_layer(nc, "attn3", x_res, consts, a["wqkv3"], a["wo3"], None)
        moe_layer(nc, "moe1", x_res, consts, a["router"], a["gate_up"], a["down"], a["keyval"], a["slot_no"], moe_rows, moe_x)
        state_space_layer(nc, x_res, consts, a["ssm_in"], a["ssm_out"], (a["ssm_cols"], a["ssm_heads"]), a["ssm_mats"])
        moe_layer(nc, "moe2", x_res, consts, a["router"], a["gate_up"], a["down"], a["keyval"], a["slot_no"], moe_rows, moe_x)
        store_phase(nc, x_res, out)


def layouts(i):
    def grouped(wq, wk, wv):
        w = np.stack([wq.T, wk.T, wv.T], axis=1).reshape(D, 3, NG, HG * DH)
        return w.transpose(0, 2, 1, 3).reshape(D, NG * GW)

    row, col = np.arange(P)[:, None], np.arange(P)[None, :]
    masks = np.stack([row == col, np.where(col > row, MASKED, 0.0), np.where(row > col, MASKED, 0.0)])
    freq = (10000.0 ** (-2.0 * np.arange(DH // 2, dtype=np.float32) / DH)).astype(np.float32)
    ang = np.arange(S, dtype=np.float32)[:, None] * freq[None, :]
    rope = np.stack([np.tile(np.repeat(f(ang), 2, axis=-1), (1, 2 * HG)) for f in (np.cos, np.sin)])
    def columns(v):
        return v.reshape(-1, P).T

    had = np.array([[1.0]])
    while had.shape[0] < P:
        had = np.block([[had, had], [had, -had]])
    had = np.stack([had / 16, -had / 16, had / 32, -had / 32])
    x = i["L0_attn_a_x"].reshape(T, D)
    token = np.arange(T).reshape(2, 1, T // 2) + np.zeros((1, E, 1), np.int64)
    qkv2 = np.split(i["L0_attn_b_W_qkv"], 3, axis=0)
    d = {
        "x": x, "masks": masks.astype(np.float32), "rope": rope.astype(np.float32),
        "wqkv1": grouped(i["L0_attn_a_wq"], i["L0_attn_a_wk"], i["L0_attn_a_wv"]), "wo1": i["L0_attn_a_wo"].T,
        "keyval": (T - token).reshape(P, T // 2).astype(np.float32), "slot_no": np.arange(P, dtype=np.float32)[:, None], "router": i["L1_ffn_router_weight"].T,
        "gate_up": i["L1_ffn_gate_up_proj"], "down": i["L1_ffn_down_proj"],
        "ssm_in": i["L1_attn_b_in_proj_w"], "ssm_out": i["L1_attn_b_out_proj_w"],
        "ssm_cols": np.concatenate([columns(i["L1_attn_b_norm_scale"]), columns(i["L1_attn_b_conv_bias"]), columns(i["L1_attn_b_D"]),
                                    i["L1_attn_b_conv_weight"].reshape(4, 4, P).transpose(2, 1, 0).reshape(P, 16)], axis=1),
        "ssm_heads": np.concatenate([i["L1_attn_b_A_log"], i["L1_attn_b_dt_bias"]]),
        "ssm_mats": np.stack([row <= col, row + 0 * col == P - 1]).astype(np.float32),
        "wqkv2": grouped(*qkv2), "wo2": i["L0_attn_b_W_out"].T,
        "wqkv3": grouped(i["L1_attn_a_Wq"], i["L1_attn_a_Wk"], i["L1_attn_a_Wv"]), "wo3": i["L1_attn_a_Wo"].T,
        "had": had.astype(np.float32), "wug": np.concatenate([i["L0_ffn_W_up"].T, i["L0_ffn_W_gate"].T], axis=1),
        "wdn": i["L0_ffn_W_down"].T, "su_ug": columns(i["L0_ffn_SU_ug"]), "su_dp": columns(i["L0_ffn_SU_dp"]),
        "scale_ug": i["L0_ffn_Wscale_ug"], "scale_dp": i["L0_ffn_Wscale_dp"],
    }
    return {k: np.ascontiguousarray(v) for k, v in d.items()}


def kernel(**inputs):
    import concourse.bacc as bacc
    from concourse.bass_utils import run_bass_kernel_spmd

    arrays = layouts({name: np.asarray(a) for name, a in inputs.items()})
    nc = bacc.Bacc("TRN2", target_bir_lowering=False, num_devices=1)
    a = {name: nc.dram_tensor(f"in_{name}", v.shape, mybir.dt.from_np(v.dtype), kind="ExternalInput").ap()
         for name, v in arrays.items()}
    out = nc.dram_tensor("out", (T, D), F32, kind="ExternalOutput").ap()
    program(nc, a, out)
    r = run_bass_kernel_spmd(nc, [{f"in_{name}": v for name, v in arrays.items()}], core_ids=[0])
    return r.results[0]["out"].reshape(B, S, D)
```

```python
from contextlib import ExitStack

import numpy as np
import concourse.bass as bass
from concourse import mybir

F32 = mybir.dt.float32
BF16 = mybir.dt.bfloat16
I32 = mybir.dt.int32
U32 = mybir.dt.uint32
ALU = mybir.AluOpType
ACT = mybir.ActivationFunctionType
AX = mybir.AxisListType

P = 128
B, S, D = 4, 1024, 256
T = B * S
NT = T // P
TS = S // P
KD = D // P
LN_EPS = 1e-5

HEADS, DH = 16, 16
HG = 4
NG = HEADS // HG
GW = 3 * HG * DH
GQ = 2 * HG * DH
Q_PARTS = (0, 0, 1, 0, 2, 1)
K_PARTS = (0, 1, 0, 2, 0, 1)
NS = len(Q_PARTS)
MASKED = -1e30

INTER = 1024
E, FE, TOPK, CAP = 64, 96, 8, 128


START = 1


class Steps:

    def __init__(self, engine, sem):
        self.engine, self.sem = engine, sem

    def begin(self, base):
        self.base, self.n = base, 0

    def done(self, instruction):
        instruction.then_inc(self.sem, 1)
        self.n += 1

    def wait(self):
        self.engine.wait_ge(self.sem, START + self.base + self.n)

    def end(self, planned):
        assert self.n == planned, (self.n, planned)


def carry(nc, tile):
    nc.vector.memset(tile[:, 0:1], 0.0)


def carry_on_pool(nc, tile, column, carried, before):
    nc.gpsimd.wait_ge(carried, START + before)
    nc.gpsimd.tensor_tensor(tile[:, column:column + 1], tile[:, 0:1], tile[:, 0:1], ALU.mult).then_inc(carried, 1)


def allocators(nc, ctx, name):
    def sb(what, shape, dt):
        return ctx.enter_context(nc.sbuf_tensor(f"{name}_{what}", shape, dt))

    def pb(what, shape, dt):
        return ctx.enter_context(nc.psum_tensor(f"{name}_{what}", shape, dt))

    used, at_zero = [], []

    def sem(what, from_zero=False):
        used.append(nc.alloc_semaphore(f"{name}_{what}"))
        if from_zero:
            at_zero.append(used[-1])
        return used[-1]

    def release():
        if used:
            nc.clear_and_free_semaphores(used)
            nc.all_engine_barrier()

    ctx.callback(release)

    def start():
        engines = (nc.gpsimd, nc.scalar, nc.vector, nc.sync, nc.tensor)
        for n, s in enumerate(s for s in used if s not in at_zero):
            engines[n % len(engines)].sem_inc(s, START)
        nc.all_engine_barrier()
        return ctx.enter_context(nc.Block())

    return sb, pb, sem, start


HEAD_CHUNKS = [(qt, c, 512 * c, min(512, 128 * (qt + 1) - 512 * c), 128 * (qt + 1) <= 512 * (c + 1))
               for qt in range(TS) for c in range(2) if 512 * c < 128 * (qt + 1)]
NCH = len(HEAD_CHUNKS)
STEPS = [(kt, h, c) for kt in range(TS) for h in range(HG) for c in range(kt // 4, 2)]
NSTEPS = len(STEPS)
ENDS = [1 + max(n for n, s in enumerate(STEPS) if s[0] == kt) for kt in range(TS)]
PRODUCTS = {ENDS[kp] + 2 + c: (kp, c) for kp in range(TS - 1) for c in range(kp // 4, 2)}
SIDE = 4


def side_units(g, first, last):
    steps = [[] for _ in range(NSTEPS)]
    if not (last and g == NG - 1):
        for j in range(2 * HG):
            steps[j].append(("ST", j))
    if g == 2 and not last:
        for r in range(4):
            steps[1 + 2 * r].append(("HT", r))
    for r in range(2):
        steps[5 + r].append(("PAD" if first and g == 0 else "O", r))
    if g == 0 and not first:
        for r in range(4):
            steps[8 + 2 * r].append(("AT", r))
            steps[20 + 3 * r].append(("Y", r))
    if not (last and g >= 2):
        for r in range(4):
            steps[QKV_AT + 2 * r].append(("QKV", r))
    if not (last and g == NG - 1):
        for i in range(HG * NCH):
            at = MX_FROM + i * (MX_TO - MX_FROM) // (HG * NCH)
            steps[at].append(("MX", i))
            if i % NCH == NCH - 1:
                steps[at + 3].insert(0, ("NM", i // NCH))
    return steps


QKV_AT, MX_FROM, MX_TO = 9, 8, 44


PROLOGUE = [("HT", r) for r in range(4)] + [("QKV", r) for r in range(4)] + [("ST", j) for j in range(2 * HG)] + \
           [("QKV", r) for r in range(4)] + [u for h in range(HG) for u in [("MX", NCH * h + i) for i in range(NCH)] + [("NM", h)]]
EPILOGUE = [("O", 0), ("O", 1)] + [("AT", r) for r in range(4)] + [("Y", r) for r in range(4)]
READ_BY_SCALAR = lambda kind, index: kind in ("HT", "QKV", "ST", "AT", "PAD") or (kind == "NM" and index % 2 == 0)


def units_of(first, last):
    return sum(len(s) for g in range(NG) for s in side_units(g, first, last))


class Side:

    def __init__(self, filled, read):
        self.filled, self.read = filled, read

    def begin(self, turns):
        self.turns, self.k = turns, 0

    def bank_free(self, engine):
        engine.wait_ge(self.read[self.k % SIDE], START + self.turns + self.k // SIDE)

    def is_filled(self, engine):
        engine.wait_ge(self.filled, START + self.turns * SIDE + self.k + 1)

    def all_read(self, engine):
        for i in range(SIDE):
            engine.wait_ge(self.read[i], START + self.turns + (self.k + SIDE - 1 - i) // SIDE)


def attention_layer(nc, name, x_res, consts, wqkv_dram, wout_dram, rope_dram):
    ident, ident_b, causal_q, causal_k = (consts[k] for k in ("ident", "ident_b", "causal_q", "causal_k"))
    rope = rope_dram is not None
    with ExitStack() as ctx:
        sb, pb, sem, start = allocators(nc, ctx, name)
        w_qkv = sb("w_qkv", [P, KD, NG * GW], F32)
        w_out = sb("w_out", [P, KD, D], F32)
        if rope:
            cos_t = sb("cos_t", [P, TS, GQ], F32)
            sin_t = sb("sin_t", [P, TS, GQ], F32)
            rot_a = sb("rot_a", [P, TS, GQ], F32)
            rot_b = sb("rot_b", [P, TS, GQ], F32)
            qk = sb("qk", [P, TS, GQ], F32)
        waits_v = sb("waits_v", [P, 2], F32)
        ones = sb("ones", [P, 1], F32)
        pad = sb("pad", [P, 2], F32)
        h_tok = sb("h_tok", [P, TS, D], F32)
        hT = sb("hT", [P, KD, S], F32)
        aT = sb("aT", [P, KD, S], F32)
        stats = sb("stats", [P, TS, 6], F32)
        mv = sb("mv", [P, TS, 2], F32)
        rstd = sb("rstd", [P, 3, TS], F32)
        qkv = sb("qkv", [P, TS, GW], F32)
        part = sb("part", [P, 3, TS, GQ], BF16)
        rest = sb("rest", [P, TS, GQ], F32)
        q_stack = sb("q_stack", [P, TS, HG, NS, DH], BF16)
        k_stack = sb("k_stack", [P, TS, HG, NS, DH], BF16)
        qsT = sb("qsT", [P, 2, HG, S], BF16)
        ksT = sb("ksT", [P, 2, HG, S], BF16)
        v_aug = sb("v_aug", [P, 2, TS, HG, 32], F32)
        m_part = sb("m_part", [P, TS, 2], F32)
        m_neg = sb("m_neg", [P, 2, TS], F32)
        m_split = sb("m_split", [P, HG, TS, 3], BF16)
        probs = sb("probs", [P, 2, HG, S], F32)
        oT = sb("oT", [P, S], F32)
        rsum = sb("rsum", [P, TS, HG], F32)
        attn = sb("attn", [P, TS, D], F32)
        ps_s = [pb(f"ps_s{i}", [P, 512], F32) for i in range(2)]
        ps_o = pb("ps_o", [P, 1024], F32)
        ps_a = [pb(f"ps_a{i}", [P, 512], F32) for i in range(SIDE)]

        w_in = sem("w_in")
        ones_set = sem("ones_set")
        dve, pool_steps = sem("dve"), sem("pool_steps")
        side_filled = sem("side_filled")
        side_read = [sem(f"side_read{i}") for i in range(SIDE)]
        var_ready, std_ready, h_ready = sem("var_ready"), sem("std_ready"), sem("h_ready")
        v_ready, stack_ready, nm_ready = sem("v_ready"), sem("stack_ready"), sem("nm_ready")
        s_psum, p_ready, pv_done, oT_ready = sem("s_psum"), sem("p_ready"), sem("pv_done"), sem("oT_ready")
        NIT = B * NG

        DVE_LN, DVE_MAX, DVE_O = 2 * TS + 1, 6 * HG, 2
        POOL_IT = 5 + (5 if rope else 0)
        n_pro, n_first, n_mid = len(PROLOGUE), units_of(True, False), units_of(False, False)
        n_last = units_of(False, True)
        dve_pro, dve_first, dve_mid = DVE_LN + DVE_MAX, DVE_LN + NG * DVE_MAX + (NG - 1) * DVE_O, DVE_LN + NG * (DVE_MAX + DVE_O)
        dve_last = (NG - 1) * DVE_MAX + NG * DVE_O
        assert not (n_pro % SIDE or n_first % SIDE or n_mid % SIDE or n_last % SIDE), (n_pro, n_first, n_mid, n_last)
        block = start()

        def sequences(engine, side, prologue, iteration, epilogue, before=lambda b, first, last: None):
            side.begin(0)
            prologue()
            for first, last in ((True, False), (False, False), (False, True)):
                if first or last:
                    b = 0 if first else B - 1
                    side.begin((n_pro + (0 if first else n_first + n_mid * (B - 2))) // SIDE)
                    before(b, first, last)
                    for g in range(NG):
                        iteration(b, g, first, last)
                else:
                    with engine.Fori(1, B - 1) as b:
                        side.begin((n_pro + n_first - n_mid) // SIDE + b * (n_mid // SIDE))
                        before(b, first, last)
                        for g in range(NG):
                            iteration(b, g, first, last)
            side.begin((n_pro + n_first + n_mid * (B - 2) + n_last) // SIDE)
            epilogue()

        @block.sync
        def _(sp):
            sp.dma_start(w_qkv[:], wqkv_dram.rearrange("(k p) n -> p k n", p=P)).then_inc(w_in, 16)
            sp.dma_start(w_out[:], wout_dram.rearrange("(k p) n -> p k n", p=P)).then_inc(w_in, 16)
            if rope:
                sp.dma_start(cos_t[:], rope_dram[0].rearrange("(t p) n -> p t n", p=P)).then_inc(w_in, 16)
                sp.dma_start(sin_t[:], rope_dram[1].rearrange("(t p) n -> p t n", p=P)).then_inc(w_in, 16)
        LOADED = 64 if rope else 32

        @block.gpsimd
        def _(pool):
            side, step = Side(side_filled, side_read), Steps(pool, pool_steps)

            def copy(out, in_):
                one = ones[:, 0:1]
                for _ in range(len(in_.shape) - 2):
                    one = one.unsqueeze(1)
                return nc.gpsimd.tensor_tensor(out, in_, one.to_broadcast(list(in_.shape)), ALU.mult)

            def take_v(it):
                par = it_parity[0]
                pool.wait_ge(pv_done, START + TS * (it - 1) if not isinstance(it, int) else START + TS * max(it - 1, 0))
                copy(v_aug[:, par, :, :, 0:DH], qkv[:, :, GQ:GW].rearrange("p t (h d) -> p t h d", h=HG)).then_inc(v_ready, 1)

            it_parity = [0]

            def prepare(it):
                step.begin(POOL_IT * it)
                if rope:
                    two = lambda ap: ap.rearrange("p t (n two) -> p t n two", two=2)
                    src, sn, ra, rb, qq = two(qkv[:, :, 0:GQ]), two(sin_t[:]), two(rot_a[:]), two(rot_b[:]), two(qk[:])
                    step.done(nc.gpsimd.tensor_tensor(rot_a[:], qkv[:, :, 0:GQ], cos_t[:], ALU.mult))
                    step.done(nc.gpsimd.tensor_tensor(rb[:, :, :, 0], src[:, :, :, 1], sn[:, :, :, 0], ALU.mult))
                    step.done(nc.gpsimd.tensor_tensor(rb[:, :, :, 1], src[:, :, :, 0], sn[:, :, :, 1], ALU.mult))
                    step.wait()
                    step.done(nc.gpsimd.tensor_tensor(qq[:, :, :, 0], ra[:, :, :, 0], rb[:, :, :, 0], ALU.subtract))
                    step.done(nc.gpsimd.tensor_tensor(qq[:, :, :, 1], ra[:, :, :, 1], rb[:, :, :, 1], ALU.add))
                    step.wait()
                src = qk[:] if rope else qkv[:, :, 0:GQ]
                step.done(copy(part[:, 0], src))
                step.wait()
                step.done(nc.gpsimd.tensor_tensor(rest[:], src, part[:, 0], ALU.subtract))
                step.wait()
                step.done(copy(part[:, 1], rest[:]))
                step.wait()
                step.done(nc.gpsimd.tensor_tensor(rest[:], rest[:], part[:, 1], ALU.subtract))
                step.wait()
                step.done(copy(part[:, 2], rest[:]))
                step.wait()
                for stack, order, o in ((q_stack, Q_PARTS, 0), (k_stack, K_PARTS, HG * DH)):
                    for s in range(NS):
                        to = stack[:, :, :, s, :]
                        of = part[:, order[s], :, o:o + HG * DH].rearrange("p t (h d) -> p t h d", h=HG)
                        ins = copy(to, of)
                ins.then_inc(stack_ready, 1)
                step.end(POOL_IT)

            def prologue():
                for kind, index in PROLOGUE:
                    side.k += 1
                    if (kind, index) == ("QKV", 3):
                        side.all_read(pool)
                        if side.k == 8:
                            take_v(0)
                            prepare(0)
                        else:
                            pool.wait_ge(side_filled, START + 16)
                            prepare(1)

            def iteration(b, g, first, last):
                it = b * NG + g
                units = [u for s in side_units(g, first, last) for u in s]
                if not (last and g == NG - 1):
                    it_parity[0] = (g + 1) % 2
                    take_v(it + 1)
                k0 = side.k
                if ("QKV", 3) in units:
                    side.k = k0 + units.index(("ST", 2 * HG - 1))
                    side.is_filled(pool)
                    side.k = k0 + units.index(("QKV", 3)) + 1
                    side.all_read(pool)
                    prepare(it + 2)
                side.k = k0 + len(units)

            nc.gpsimd.memset(v_aug[:], 1.0).then_inc(ones_set, 1)
            nc.gpsimd.memset(ones[:], 1.0).then_inc(ones_set, 1)
            pool.wait_ge(ones_set, START + 3)
            pool.wait_ge(w_in, START + LOADED)
            sequences(pool, side, prologue, iteration, lambda: None)

        @block.tensor
        def _(pe):
            side = Side(side_filled, side_read)

            def unit(kind, index, it, b, par, at_start=None):
                bank = ps_a[side.k % SIDE]
                r = index
                if kind == "HT" and r >= 0:
                    pe.wait_ge(h_ready, START + 4 * b + r + 1)
                elif kind == "ST" and index == 0:
                    pe.wait_ge(stack_ready, START + it + 1)
                elif kind == "NM":
                    pe.wait_ge(nm_ready, START + HG * it + index + 1)
                elif kind == "O":
                    pe.wait_ge(oT_ready, START + it)
                elif (kind in ("QKV", "AT") and r == 0) or (kind == "Y" and r == 0) or (kind == "MX" and index % NCH == 0):
                    side.all_read(pe)
                side.bank_free(pe)
                if kind in ("HT", "AT"):
                    src = h_tok if kind == "HT" else attn
                    for k in range(KD):
                        for tl in range(2):
                            mm = nc.tensor.transpose(bank[:, 256 * k + 128 * tl:256 * k + 128 * tl + 128],
                                                     src[:, 2 * r + tl, 128 * k:128 * k + 128], ident[:])
                elif kind == "QKV":
                    for tl in range(2):
                        t = 2 * r + tl
                        for k in range(KD):
                            mm = nc.tensor.matmul(bank[:, GW * tl:GW * tl + GW], hT[:, k, 128 * t:128 * t + 128],
                                                  w_qkv[:, k, qkv_columns[0]], start=(k == 0), stop=(k == KD - 1))
                elif kind == "ST":
                    stack, h = (q_stack, k_stack)[index % 2], index // 2
                    for t in range(TS):
                        mm = nc.tensor.transpose(bank[:].bitcast(BF16)[0:96, 128 * t:128 * t + 128],
                                                 stack[:, t, h].rearrange("p s d -> p (s d)"), ident_b[:])
                elif kind == "MX":
                    h, (qt, c, k0, kn, diag) = index // NCH, HEAD_CHUNKS[index % NCH]
                    mm = nc.tensor.matmul(bank[:, 0:kn], qsT[0:96, par, h, 128 * qt:128 * qt + 128],
                                          ksT[0:96, par, h, k0:k0 + kn], start=True, stop=not diag)
                    if diag:
                        mm = nc.tensor.matmul(bank[:, kn - 128:kn], ident_b[:], causal_q[:], start=False, stop=True)
                elif kind == "NM":
                    for t in range(TS):
                        mm = nc.tensor.transpose(bank[:].bitcast(BF16)[96:99, 128 * t:128 * t + 128],
                                                 m_split[:, index, t, :], ident_b[:])
                elif kind == "O":
                    for t in range(4):
                        q0 = 512 * r + 128 * t
                        mm = nc.tensor.transpose(bank[:, 128 * t:128 * t + 128], oT[:, q0:q0 + 128], ident[:])
                elif kind == "Y":
                    for tl in range(2):
                        t = 2 * r + tl
                        for k in range(KD):
                            mm = nc.tensor.matmul(bank[:, D * tl:D * tl + D], aT[:, k, 128 * t:128 * t + 128],
                                                  w_out[:, k, :], start=(k == 0), stop=(k == KD - 1))
                else:
                    mm = nc.tensor.matmul(bank[:, 0:128], ident_b[:], ident_b[:], start=True, stop=True)
                mm.then_inc(side_filled, 1)
                side.k += 1

            qkv_columns = [None]

            def prologue():
                for n, (kind, index) in enumerate(PROLOGUE):
                    qkv_columns[0] = slice(0, GW) if n < 8 else slice(GW, 2 * GW)
                    unit(kind, index, 0 if kind != "NM" else 0, 0, 0)

            def scores(it, par, n):
                kt, h, c = STEPS[n]
                if n >= 2:
                    pe.wait_ge(p_ready, START + NSTEPS * it + n - 1)
                q0, q1 = max(512 * c, 128 * kt), 512 * (c + 1)
                diag, bank = q0 == 128 * kt, ps_s[n % 2]
                mm = nc.tensor.matmul(bank[:, q0 - 512 * c:512], ksT[0:99, par, h, 128 * kt:128 * kt + 128],
                                      qsT[0:99, par, h, q0:q1], start=True, stop=not diag)
                if diag:
                    mm = nc.tensor.matmul(bank[:, q0 - 512 * c:q0 - 512 * c + 128], ident_b[:], causal_k[:], start=False, stop=True)
                mm.then_inc(s_psum, 1)

            def products(it, par, kp, c):
                pe.wait_ge(p_ready, START + NSTEPS * it + ENDS[kp])
                if kp == 0:
                    pe.wait_ge(v_ready, START + it + 1)
                    pe.wait_ge(oT_ready, START + it)
                q0, q1 = max(512 * c, 128 * kp), 512 * (c + 1)
                for h in range(HG):
                    mm = nc.tensor.matmul(ps_o[32 * h:32 * h + 32, q0:q1], v_aug[:, par, kp, h, :],
                                          probs[:, kp % 2, h, q0:q1], start=(kp == 0), stop=(kp == 4 * c + 3))
                if c == 1:
                    mm.then_inc(pv_done, 1)

            def iteration(b, g, first, last):
                it = b * NG + g
                steps = side_units(g, first, last)
                g2 = (g + 2) % NG
                qkv_columns[0] = slice(g2 * GW, g2 * GW + GW)
                side.all_read(pe)
                scores(it, g % 2, 0)
                for n in range(NSTEPS):
                    if n + 1 < NSTEPS:
                        scores(it, g % 2, n + 1)
                    for kind, index in steps[n]:
                        if kind in ("ST", "NM"):
                            unit(kind, index, it + 1, b, (g + 1) % 2)
                        elif kind == "HT":
                            unit(kind, index, it, b + 1, None)
                        else:
                            unit(kind, index, it, b, (g + 1) % 2)
                    if n in PRODUCTS:
                        products(it, g % 2, *PRODUCTS[n])
                products(it, g % 2, TS - 1, 1)

            pe.wait_ge(w_in, START + LOADED)
            pe.wait_ge(ones_set, START + 3)
            sequences(pe, side, prologue, iteration,
                      lambda: [unit(kind, index, NIT, B, None) for kind, index in EPILOGUE])

        @block.scalar
        def _(act):
            side = Side(side_filled, side_read)

            def read(kind, index, par):
                bank = ps_a[side.k % SIDE]
                if READ_BY_SCALAR(kind, index):
                    side.is_filled(act)
                    if kind in ("HT", "AT"):
                        ins = nc.scalar.copy((hT if kind == "HT" else aT)[:, :, 256 * index:256 * index + 256],
                                             bank[:].rearrange("p (k n) -> p k n", k=KD))
                    elif kind == "QKV":
                        ins = nc.scalar.copy(qkv[:, 2 * index:2 * index + 2, :], bank[:, 0:2 * GW].rearrange("p (t n) -> p t n", t=2))
                    elif kind == "ST":
                        ins = nc.scalar.copy((qsT, ksT)[index % 2][0:96, par, index // 2, :], bank[:].bitcast(BF16)[0:96, :])
                    elif kind == "PAD":
                        ins = nc.scalar.copy(pad[:, index:index + 1], bank[:, 0:1])
                    else:
                        ins = nc.scalar.copy(qsT[96:99, par, index, :], bank[:].bitcast(BF16)[96:99, :])
                    ins.then_inc(side_read[side.k % SIDE], 1)
                side.k += 1

            def root():
                nc.scalar.activation(rstd[:, 1], rstd[:, 0], ACT.Sqrt).then_inc(std_ready, 1)

            def prologue():
                act.wait_ge(var_ready, START + 1)
                root()
                for n, (kind, index) in enumerate(PROLOGUE):
                    if (kind, index) == ("QKV", 0) and n > 8:
                        act.wait_ge(v_ready, START + 1)
                        act.wait_ge(stack_ready, START + 1)
                    read(kind, index, 0)

            def iteration(b, g, first, last):
                it = b * NG + g
                steps = side_units(g, first, last)
                for n, (kt, h, c) in enumerate(STEPS):
                    act.wait_ge(s_psum, START + NSTEPS * it + n + 1)
                    if h == 0:
                        act.wait_ge(pv_done, START + TS * it + (kt - 1 if kt >= 2 else 0))
                    q0, q1 = max(512 * c, 128 * kt), 512 * (c + 1)
                    nc.scalar.activation(probs[:, kt % 2, h, q0:q1], ps_s[n % 2][:, q0 - 512 * c:512], ACT.Exp,
                                         scale=DH ** -0.5).then_inc(p_ready, 1)
                    if n == 2 and not (first and g == 0):
                        act.wait_ge(pv_done, START + TS * it)
                        nc.scalar.copy(oT[:], ps_o[:]).then_inc(oT_ready, 1)
                    if n == 12 and g == 1 and not last:
                        act.wait_ge(var_ready, START + b + 2)
                        root()
                    for kind, index in steps[n]:
                        if (kind, index) == ("QKV", 0):
                            act.wait_ge(v_ready, START + it + 2)
                            act.wait_ge(stack_ready, START + it + 2)
                        read(kind, index, (g + 1) % 2)

            def epilogue():
                act.wait_ge(pv_done, START + TS * NIT)
                nc.scalar.copy(oT[:], ps_o[:]).then_inc(oT_ready, 1)
                for kind, index in EPILOGUE:
                    read(kind, index, None)

            sequences(act, side, prologue, iteration, epilogue)

        @block.vector
        def _(v):
            side, step = Side(side_filled, side_read), Steps(v, dve)

            def statistics(b):
                for t in range(TS):
                    step.done(nc.vector.bn_stats(stats[:, t, :], one_tile(x_res, b * TS + t)))
                step.wait()
                carry(nc, waits_v)
                for t in range(TS):
                    step.done(nc.vector.bn_aggr(mv[:, t, :], stats[:, t, :]))
                step.wait()
                nc.vector.tensor_scalar(rstd[:, 0], mv[:, :, 1], LN_EPS, None, ALU.add).then_inc(var_ready, 1)

            def normalize(b):
                v.wait_ge(std_ready, START + b + 1)
                step.done(nc.vector.reciprocal(rstd[:, 2], rstd[:, 1]))
                step.wait()
                for t in range(TS):
                    ins = nc.vector.tensor_scalar(h_tok[:, t, :], one_tile(x_res, b * TS + t), mv[:, t, 0:1], rstd[:, 2, t:t + 1],
                                                  ALU.subtract, ALU.mult)
                    if t % 2 == 1:
                        ins.then_inc(h_ready, 1)

            def read(kind, index, b, g):
                bank = ps_a[side.k % SIDE]
                mine = side_read[side.k % SIDE]
                if not READ_BY_SCALAR(kind, index):
                    side.is_filled(v)
                    if kind == "MX":
                        qt, c, k0, kn, diag = HEAD_CHUNKS[index % NCH]
                        nc.vector.tensor_reduce(m_part[:, qt, c:c + 1], bank[:, 0:kn], AX.X, ALU.max, negate=False).then_inc(mine, 1)
                    elif kind == "NM":
                        nc.vector.tensor_copy(qsT[96:99, (g + 1) % 2, index, :], bank[:].bitcast(BF16)[96:99, :]).then_inc(mine, 1)
                    elif kind == "O":
                        o_tok = bank[:].rearrange("p (t h e) -> p t h e", t=4, h=HG)
                        rs = rsum[:, 4 * index:4 * index + 4, :]
                        step.done(nc.vector.reciprocal(rs, o_tok[:, :, :, DH]))
                        step.wait()
                        gp = (g - 1) % NG
                        nc.vector.tensor_tensor(attn[:, 4 * index:4 * index + 4, gp * HG * DH:(gp + 1) * HG * DH]
                                                .rearrange("p t (h d) -> p t h d", h=HG), o_tok[:, :, :, 0:DH],
                                                rs.unsqueeze(3).to_broadcast([P, 4, HG, DH]), ALU.mult).then_inc(mine, 1)
                    else:
                        xs = x_res[:, bass.ds((b - 1) * TS + 2 * index, 2), :]
                        nc.vector.tensor_tensor(xs, xs, bank[:].rearrange("p (t n) -> p t n", t=2), ALU.add).then_inc(mine, 1)
                side.k += 1
                if kind == "MX" and index % NCH == NCH - 1:
                    h = index // NCH
                    side.all_read(v)
                    step.done(nc.vector.tensor_scalar(m_neg[:, 0, 0:4], m_part[:, 0:4, 0], -1.0, None, ALU.mult))
                    step.done(nc.vector.tensor_tensor(m_part[:, 4:8, 0], m_part[:, 4:8, 0], m_part[:, 4:8, 1], ALU.max))
                    step.wait()
                    step.done(nc.vector.tensor_scalar(m_neg[:, 0, 4:8], m_part[:, 4:8, 0], -1.0, None, ALU.mult))
                    step.wait()
                    step.done(nc.vector.tensor_copy(m_split[:, h, :, 0], m_neg[:, 0]))
                    step.wait()
                    step.done(nc.vector.tensor_tensor(m_neg[:, 1], m_neg[:, 0], m_split[:, h, :, 0], ALU.subtract))
                    step.wait()
                    step.done(nc.vector.tensor_copy(m_split[:, h, :, 1], m_neg[:, 1]))
                    step.wait()
                    nc.vector.tensor_tensor(m_split[:, h, :, 2], m_neg[:, 1], m_split[:, h, :, 1], ALU.subtract).then_inc(nm_ready, 1)

            def prologue():
                step.begin(0)
                statistics(0)
                normalize(0)
                for kind, index in PROLOGUE:
                    read(kind, index, 0, -1)
                step.end(dve_pro)

            def before(b, first, last):
                step.begin(dve_pro + (0 if first else dve_first + dve_mid * (b - 1)))

            def iteration(b, g, first, last):
                steps = side_units(g, first, last)
                for n in range(NSTEPS):
                    if g == 1 and not last:
                        if n == 0:
                            statistics(b + 1)
                        elif n == 16:
                            normalize(b + 1)
                    for kind, index in steps[n]:
                        read(kind, index, b, g)
                if g == NG - 1:
                    step.end(dve_first if first else dve_last if last else dve_mid)

            def epilogue():
                step.begin(dve_pro + dve_first + dve_mid * (B - 2) + dve_last)
                for kind, index in EPILOGUE:
                    read(kind, index, B, NG)
                side.all_read(v)

            nc.vector.memset(ksT[96:99, :, :, :], 1.0).then_inc(ones_set, 1)
            sequences(v, side, prologue, iteration, epilogue, before)


def mlp_weights(nc, w_ug, w_dn, wug_dram, wdn_dram, had_dram, su_dram, scale_ug, su_dp, scale_dp):
    KI = INTER // P
    with ExitStack() as ctx:
        sb, pb, sem, start = allocators(nc, ctx, "fold")
        raw_ug = sb("raw_ug", [P, KD, 2 * INTER], F32)
        raw_dn = sb("raw_dn", [P, KI, D], F32)
        had = sb("had", [P, 4, P], F32)
        su_u = sb("su_u", [P, KD], F32)
        su_d = sb("su_d", [P, KI], F32)
        sc_u = sb("sc_u", [P, 2 * INTER], F32)
        sc_d = sb("sc_d", [P, D], F32)
        ps = [pb(f"ps{i}", [P, 512], F32) for i in range(2)]
        landed, folded, scaled = sem("landed"), sem("folded"), sem("scaled")
        block = start()
        NLOAD = 7
        jobs = []
        for a1 in range(KD):
            for c in range(4):
                jobs.append((w_ug[:, a1, 512 * c:512 * c + 512], su_u[:, a1:a1 + 1], sc_u[:, 512 * c:512 * c + 512],
                             [((a0 & a1) % 2, raw_ug[:, a0, 512 * c:512 * c + 512]) for a0 in range(KD)]))
        for c1 in range(KI):
            jobs.append((w_dn[:, c1, :], su_d[:, c1:c1 + 1], sc_d[:],
                         [(2 + bin(c0 & c1).count("1") % 2, raw_dn[:, c0, :]) for c0 in range(KI)]))

        @block.sync
        def _(sp):
            sp.dma_start(had[:], had_dram.rearrange("m p n -> p m n")).then_inc(landed, 16)
            sp.dma_start(raw_ug[:], wug_dram.rearrange("(k p) n -> p k n", p=P)).then_inc(landed, 16)
            sp.dma_start(su_u[:], su_dram).then_inc(landed, 16)
            sp.dma_start(sc_u[:], scale_ug.partition_broadcast(P)).then_inc(landed, 16)
            sp.dma_start(raw_dn[:], wdn_dram.rearrange("(k p) n -> p k n", p=P)).then_inc(landed, 16)
            sp.dma_start(su_d[:], su_dp).then_inc(landed, 16)
            sp.dma_start(sc_d[:], scale_dp.partition_broadcast(P)).then_inc(landed, 16)

        @block.tensor
        def _(pe):
            pe.wait_ge(landed, START + 16 * NLOAD)
            for n, (dst, _, _, products) in enumerate(jobs):
                if n >= 2:
                    pe.wait_ge(scaled, START + n - 1)
                width = dst.shape[-1]
                for i, (which, moving) in enumerate(products):
                    mm = nc.tensor.matmul(ps[n % 2][:, 0:width], had[:, which, :], moving, start=(i == 0),
                                          stop=(i == len(products) - 1))
                mm.then_inc(folded, 1)

        @block.vector
        def _(v):
            v.wait_ge(landed, START + 16 * NLOAD)
            for n, (dst, sign, scale, _) in enumerate(jobs):
                v.wait_ge(folded, START + n + 1)
                nc.vector.scalar_tensor_tensor(dst, ps[n % 2][:, 0:dst.shape[-1]], sign, scale, ALU.mult, ALU.mult)\
                  .then_inc(scaled, 1)
            v.wait_ge(scaled, START + len(jobs))


def mlp_layer(nc, name, x_res, consts, w_ug, w_dn):
    ident = consts["ident"]
    CT = 4
    NC = NT // CT
    CW = CT * P
    KI = INTER // P
    with ExitStack() as ctx:
        sb, pb, sem, start = allocators(nc, ctx, name)
        stats = sb("stats", [P, NT, 6], F32)
        mv = sb("mv", [P, NT, 2], F32)
        rstd = sb("rstd", [P, 3, NT], F32)
        h_tok = sb("h_tok", [P, CT, D], F32)
        hT = sb("hT", [P, KD, CW], F32)
        gated = sb("gated", [P, 2, CW], F32)
        mid = sb("mid", [P, KI, CW], F32)
        ps_t = [pb(f"ps_t{i}", [P, 512], F32) for i in range(2)]
        ps_g = [pb(f"ps_g{i}", [P, 512], F32) for i in range(2)]
        ps_u = [pb(f"ps_u{i}", [P, 512], F32) for i in range(2)]
        ps_y = [pb(f"ps_y{i}", [P, 512], F32) for i in range(2)]
        dve = sem("dve")
        var_ready, std_ready = sem("var_ready"), sem("std_ready")
        h_ready, hT_psum, hT_ready = sem("h_ready"), sem("hT_psum"), sem("hT_ready")
        gu_psum, silu_ready, mid_ready = sem("gu_psum"), sem("silu_ready"), sem("mid_ready")
        y_psum, x_done = sem("y_psum"), sem("x_done")
        block = start()

        @block.tensor
        def _(pe):
            def to_features(c):
                for r in range(2):
                    pe.wait_ge(h_ready, START + 2 * c + r + 1)
                    for k in range(KD):
                        for tl in range(2):
                            mm = nc.tensor.transpose(ps_t[r][:, 256 * k + 128 * tl:256 * k + 128 * tl + 128],
                                                     h_tok[:, 2 * r + tl, 128 * k:128 * k + 128], ident[:])
                    mm.then_inc(hT_psum, 1)

            def chunk(c, last):
                pe.wait_ge(hT_ready, START + 2 * c + 2)
                for j in range(KI):
                    if j >= 2:
                        pe.wait_ge(mid_ready, START + KI * c + j - 1)
                    for base, ps in ((0, ps_u), (INTER, ps_g)):
                        for k in range(KD):
                            mm = nc.tensor.matmul(ps[j % 2][:], w_ug[:, k, base + P * j:base + P * j + P], hT[:, k, :],
                                                  start=(k == 0), stop=(k == KD - 1))
                    mm.then_inc(gu_psum, 1)
                if not last:
                    to_features(c + 1)
                for t in range(CT):
                    if t == 0:
                        pe.wait_ge(x_done, START + 2 * c)
                    for j in range(KI):
                        if t == 0:
                            pe.wait_ge(mid_ready, START + KI * c + j + 1)
                        mm = nc.tensor.matmul(ps_y[t // 2][:, D * (t % 2):D * (t % 2) + D], mid[:, j, P * t:P * t + P],
                                              w_dn[:, j, :], start=(j == 0), stop=(j == KI - 1))
                    if t % 2 == 1:
                        mm.then_inc(y_psum, 1)

            to_features(0)
            with pe.Fori(0, NC - 1) as c:
                chunk(c, False)
            chunk(NC - 1, True)

        @block.scalar
        def _(act):
            def to_features(c):
                for r in range(2):
                    act.wait_ge(hT_psum, START + 2 * c + r + 1)
                    if r == 0:
                        act.wait_ge(gu_psum, START + KI * c)
                    nc.scalar.copy(hT[:, :, 256 * r:256 * r + 256],
                                   ps_t[r][:].rearrange("p (k n) -> p k n", k=KD)).then_inc(hT_ready, 1)

            def chunk(c, last):
                for j in range(KI):
                    act.wait_ge(gu_psum, START + KI * c + j + 1)
                    if j >= 2:
                        act.wait_ge(mid_ready, START + KI * c + j - 1)
                    else:
                        act.wait_ge(mid_ready, START + KI * c)
                    nc.scalar.activation(gated[:, j % 2, :], ps_g[j % 2][:], ACT.Silu).then_inc(silu_ready, 1)
                if not last:
                    to_features(c + 1)

            act.wait_ge(var_ready, START + 1)
            nc.scalar.activation(rstd[:, 1], rstd[:, 0], ACT.Sqrt).then_inc(std_ready, 1)
            to_features(0)
            with act.Fori(0, NC - 1) as c:
                chunk(c, False)
            chunk(NC - 1, True)

        @block.vector
        def _(v):
            layer_norm_statistics(nc, v, x_res, stats, mv, rstd, dve, var_ready, std_ready)

            def normalize(c):
                v.wait_ge(hT_psum, START + 2 * c)
                for t in range(CT):
                    tile = c * CT + t
                    ins = nc.vector.tensor_scalar(h_tok[:, t, :], one_tile(x_res, tile), mean_of(mv, tile), rstd_of(rstd, tile),
                                                  ALU.subtract, ALU.mult)
                    if t % 2 == 1:
                        ins.then_inc(h_ready, 1)

            def chunk(c, last):
                if not last:
                    normalize(c + 1)
                for j in range(KI):
                    v.wait_ge(silu_ready, START + KI * c + j + 1)
                    if j == 0:
                        v.wait_ge(y_psum, START + 2 * c)
                    nc.vector.tensor_tensor(mid[:, j, :], gated[:, j % 2, :], ps_u[j % 2][:], ALU.mult).then_inc(mid_ready, 1)
                for r in range(2):
                    v.wait_ge(y_psum, START + 2 * c + r + 1)
                    xs = x_res[:, bass.ds(c * CT + 2 * r, 2), :]
                    nc.vector.tensor_tensor(xs, xs, ps_y[r][:].rearrange("p (t n) -> p t n", t=2), ALU.add).then_inc(x_done, 1)

            normalize(0)
            with v.Fori(0, NC - 1) as c:
                chunk(c, False)
            chunk(NC - 1, True)


def one_tile(x, t):
    return x[:, bass.ds(t, 1), :].rearrange("p o d -> p (o d)")


def mean_of(mv, t):
    return mv[:, bass.ds(t, 1), 0:1].rearrange("p o d -> p (o d)")


def rstd_of(rstd, t):
    return rstd[:, 2, bass.ds(t, 1)]


def layer_norm_statistics(nc, v, x_res, stats, mv, rstd, dve, var_ready, std_ready):
    step = Steps(v, dve)
    PER = 8
    with v.Fori(0, NT // PER) as i:
        step.begin(PER * i)
        for t in range(PER):
            step.done(nc.vector.bn_stats(stats[:, bass.ds(PER * i + t, 1), :].rearrange("p o d -> p (o d)"), one_tile(x_res, PER * i + t)))
    step.begin(NT)
    step.wait()
    for t in range(NT):
        step.done(nc.vector.bn_aggr(mv[:, t, :], stats[:, t, :]))
    step.wait()
    nc.vector.tensor_scalar(rstd[:, 0], mv[:, :, 1], LN_EPS, None, ALU.add).then_inc(var_ready, 1)
    v.wait_ge(std_ready, START + 1)
    step.done(nc.vector.reciprocal(rstd[:, 2], rstd[:, 1]))
    step.wait()
    return step


def moe_layer(nc, name, x_res, consts, router_dram, gate_up_dram, down_dram, keyval_dram, slot_no_dram, rows_dram, sums_dram):
    ident = consts["ident"]
    NI = NT // 2
    ROW = D + E
    with ExitStack() as outer:
        slot_token = outer.enter_context(nc.sbuf_tensor(f"{name}_slot_token", [P, E], I32))

        with ExitStack() as ctx:
            sb, pb, sem, start = allocators(nc, ctx, name)
            stats = sb("stats", [P, NT, 6], F32)
            mv = sb("mv", [P, NT, 2], F32)
            rstd = sb("rstd", [P, 3, NT], F32)
            waits_v = sb("waits_v", [P, 2], F32)
            w_r = sb("w_r", [P, KD, E], F32)
            zeros = sb("zeros", [P, ROW], F32)
            rows = sb("rows", [P, 2, 2, ROW], F32)
            hT = sb("hT", [P, 2, KD, P], F32)
            nmax = sb("nmax", [P, 2], F32)
            ex = sb("ex", [P, 2, E], F32)
            esum = sb("esum", [P, 2], F32)
            einv = sb("einv", [P, 2], F32)
            probs = sb("probs", [P, 2, E], F32)
            best = sb("best", [P, 2, TOPK], F32)
            left = sb("left", [P, 2, E], F32)
            mask = sb("mask", [P, 2, E], F32)
            wraw = sb("wraw", [P, 2, E], F32)
            wsum = sb("wsum", [P, 2], F32)
            winv = sb("winv", [P, 2], F32)
            keyval = sb("keyval", [P, T // 2], F32)
            keys = sb("keys", [P, T // 2], F32)
            first = sb("first", [P, CAP], F32)
            firstT = sb("firstT", [P, P], F32)
            both = sb("both", [E, 2 * CAP], F32)
            picked = sb("picked", [E, CAP], F32)
            empty = sb("empty", [P, E], F32)
            token_f = sb("token_f", [P, E], F32)
            slot_no = sb("slot_no", [P, 1], F32)
            ps_t = [pb(f"ps_t{i}", [P, 512], F32) for i in range(2)]
            ps_l = [pb(f"ps_l{i}", [P, 512], F32) for i in range(2)]
            ps_m = pb("ps_m", [P, 512], F32)
            landed, stored, rows_out, zeroed = sem("landed"), sem("stored"), sem("rows_out"), sem("zeroed")
            dve = sem("dve")
            var_ready, std_ready = sem("var_ready"), sem("std_ready")
            h_ready, hT_psum, hT_ready = sem("h_ready"), sem("hT_psum"), sem("hT_ready")
            logit_psum, nmax_ready, ex_ready = sem("logit_psum"), sem("nmax_ready"), sem("ex_ready")
            maskT_psum, key_done, w_ready = sem("maskT_psum"), sem("key_done"), sem("w_ready")
            first_ready, firstT_psum, firstT_ready, both_psum = sem("first_ready"), sem("firstT_psum"), sem("firstT_ready"), sem("both_psum")
            picked_ready, picked_psum, slots_ready = sem("picked_ready"), sem("picked_psum"), sem("slots_ready")
            block = start()
            PAIR = 8

            @block.sync
            def _(sp):
                sp.dma_start(w_r[:], router_dram.rearrange("(k p) e -> p k e", p=P)).then_inc(landed, 16)
                sp.dma_start(keyval[:], keyval_dram).then_inc(landed, 16)
                sp.dma_start(slot_no[:], slot_no_dram).then_inc(landed, 16)
                sp.dma_start(sums_dram[0][0:T, :].rearrange("(t p) d -> p t d", p=P), x_res[:]).then_inc(stored, 16)
                sp.wait_ge(zeroed, START + 1)
                sp.dma_start(rows_dram[T:T + P, :], zeros[:]).then_inc(stored, 16)
                sp.dma_start(sums_dram[0][T:T + P, :], zeros[:, 0:D]).then_inc(stored, 16)
                sp.dma_start(sums_dram[1].rearrange("(t p) d -> p t d", p=P),
                             zeros[:, 0:D].unsqueeze(1).to_broadcast([P, NT + 1, D])).then_inc(stored, 16)
                with sp.Fori(0, NI) as i:
                    for half in range(2):
                        sp.wait_ge(w_ready, START + 2 * i + half + 1)
                        sp.dma_start(rows_dram[bass.ds((i + NI * half) * P, P), :], rows[:, 0, half, :]).then_inc(rows_out, 16)
                sp.wait_ge(rows_out, START + 32 * NI)
                sp.wait_ge(stored, START + 64)

            @block.tensor
            def _(pe):
                pe.wait_ge(landed, START + 48)
                with pe.Fori(0, NI) as i:
                    for half in range(2):
                        n = 2 * i + half
                        pe.wait_ge(h_ready, START + n + 1)
                        for k in range(KD):
                            mm = nc.tensor.transpose(ps_t[half][:, P * k:P * k + P], rows[:, 0, half, P * k:P * k + P], ident[:])
                        mm.then_inc(hT_psum, 1)
                    for half in range(2):
                        n = 2 * i + half
                        pe.wait_ge(hT_ready, START + n + 1)
                        for k in range(KD):
                            mm = nc.tensor.matmul(ps_l[half][:, 0:E], hT[:, half, k, :], w_r[:, k, :], start=(k == 0), stop=(k == KD - 1))
                        mm.then_inc(logit_psum, 1)
                    pe.wait_ge(w_ready, START + 2 * i + 2)
                    nc.tensor.transpose(ps_m[:, 0:P], mask[:].rearrange("p a e -> p (a e)"), ident[:]).then_inc(maskT_psum, 1)
                pe.wait_ge(first_ready, START + 1)
                nc.tensor.transpose(ps_t[0][:, 0:P], first[:], ident[:]).then_inc(firstT_psum, 1)
                pe.wait_ge(firstT_ready, START + 1)
                for half in range(2):
                    mm = nc.tensor.transpose(ps_t[1][0:E, CAP * half:CAP * half + CAP], firstT[:, E * half:E * half + E], ident[:])
                mm.then_inc(both_psum, 1)
                pe.wait_ge(picked_ready, START + 1)
                nc.tensor.transpose(ps_l[0][:, 0:E], picked[:], ident[0:E, 0:E]).then_inc(picked_psum, 1)

            @block.scalar
            def _(act):
                act.wait_ge(var_ready, START + 1)
                nc.scalar.activation(rstd[:, 1], rstd[:, 0], ACT.Sqrt).then_inc(std_ready, 1)
                with act.Fori(0, NI) as i:
                    for half in range(2):
                        n = 2 * i + half
                        act.wait_ge(hT_psum, START + n + 1)
                        act.wait_ge(logit_psum, START + 2 * i)
                        nc.scalar.copy(hT[:, half, :, :], ps_t[half][:, 0:KD * P].rearrange("p (k n) -> p k n", k=KD))\
                          .then_inc(hT_ready, 1)
                    for half in range(2):
                        n = 2 * i + half
                        act.wait_ge(nmax_ready, START + n + 1)
                        nc.scalar.activation(ex[:, half, :], ps_l[half][:, 0:E], ACT.Exp, bias=nmax[:, half:half + 1],
                                             accum_out=esum[:, half:half + 1]).then_inc(ex_ready, 1)

            @block.gpsimd
            def _(pool):
                nc.gpsimd.memset(zeros[:], 0.0).then_inc(zeroed, 1)

            @block.vector
            def _(v):
                v.wait_ge(landed, START + 48)
                layer_norm_statistics(nc, v, x_res, stats, mv, rstd, dve, var_ready, std_ready)
                step = Steps(v, dve)
                with v.Fori(0, NI) as i:
                    step.begin(2 * NT + 1 + 2 * PAIR * i)
                    v.wait_ge(rows_out, START + 32 * i)
                    for half in range(2):
                        tile = i + NI * half
                        nc.vector.tensor_scalar(rows[:, 0, half, 0:D], one_tile(x_res, tile), mean_of(mv, tile), rstd_of(rstd, tile),
                                                ALU.subtract, ALU.mult).then_inc(h_ready, 1)
                    for half in range(2):
                        n = 2 * i + half
                        v.wait_ge(logit_psum, START + n + 1)
                        nc.vector.tensor_reduce(nmax[:, half:half + 1], ps_l[half][:, 0:E], AX.X, ALU.max, negate=True)\
                          .then_inc(nmax_ready, 1)
                    for half in range(2):
                        n = 2 * i + half
                        v.wait_ge(ex_ready, START + n + 1)
                        step.done(nc.vector.reciprocal(einv[:, half:half + 1], esum[:, half:half + 1]))
                        step.wait()
                        step.done(nc.vector.tensor_scalar(probs[:, half, :], ex[:, half, :], einv[:, half:half + 1], None, ALU.mult))
                        step.wait()
                        carry(nc, waits_v)
                        step.done(nc.vector.max(best[:, half, :], probs[:, half, :]))
                        step.wait()
                        carry(nc, waits_v)
                        step.done(nc.vector.match_replace(left[:, half, :], best[:, half, :], probs[:, half, :], -1.0))
                        step.wait()
                        v.wait_ge(maskT_psum, START + i)
                        step.done(nc.vector.tensor_scalar(mask[:, half, :], left[:, half, :], 0.0, None, ALU.is_lt))
                        step.wait()
                        step.done(nc.vector.tensor_tensor(wraw[:, half, :], mask[:, half, :], probs[:, half, :], ALU.mult))
                        step.wait()
                        step.done(nc.vector.tensor_reduce(wsum[:, half:half + 1], wraw[:, half, :], AX.X, ALU.add))
                        step.wait()
                        step.done(nc.vector.reciprocal(winv[:, half:half + 1], wsum[:, half:half + 1]))
                        step.wait()
                        nc.vector.tensor_scalar(rows[:, 0, half, D:ROW], wraw[:, half, :], winv[:, half:half + 1], None,
                                                ALU.mult).then_inc(w_ready, 1)
                    v.wait_ge(maskT_psum, START + i + 1)
                    nc.vector.tensor_tensor(keys[:, bass.ds(i * P, P)], ps_m[:, 0:P], keyval[:, bass.ds(i * P, P)], ALU.mult)\
                      .then_inc(key_done, 1)
                    step.end(2 * PAIR)
                step.begin(2 * NT + 1 + 2 * PAIR * NI)
                v.wait_ge(key_done, START + NI)
                for source, dest in ((keys, first), (both, picked)):
                    if source is both:
                        v.wait_ge(first_ready, START + 1)
                        v.wait_ge(firstT_psum, START + 1)
                        nc.vector.tensor_copy(firstT[:], ps_t[0][:, 0:P]).then_inc(firstT_ready, 1)
                        v.wait_ge(both_psum, START + 1)
                        step.done(nc.vector.tensor_copy(both[:], ps_t[1][0:E, 0:2 * CAP]))
                        step.wait()
                    for r in range(CAP // TOPK):
                        ins = nc.vector.max(dest[:, TOPK * r:TOPK * r + TOPK], source[:])
                        if r == CAP // TOPK - 1:
                            ins.then_inc(first_ready if source is keys else picked_ready, 1)
                            continue
                        step.done(ins)
                        step.wait()
                        step.done(nc.vector.match_replace(source[:], dest[:, TOPK * r:TOPK * r + TOPK], source[:], 0.0))
                        step.wait()
                v.wait_ge(picked_psum, START + 1)
                step.done(nc.vector.tensor_scalar(empty[:], ps_l[0][:, 0:E], 0.0, slot_no[:, 0:1], ALU.is_equal, ALU.mult))
                step.wait()
                step.done(nc.vector.tensor_tensor(token_f[:], empty[:], ps_l[0][:, 0:E], ALU.subtract))
                step.wait()
                nc.vector.tensor_scalar(slot_token[:], token_f[:], float(T), None, ALU.add).then_inc(slots_ready, 1)
                v.wait_ge(slots_ready, START + 1)

        experts(nc, name + "e", consts, slot_token, gate_up_dram, down_dram, rows_dram, sums_dram, x_res)


def experts(nc, name, consts, slot_token, gate_up_dram, down_dram, rows_dram, sums_dram, x_res):
    ident = consts["ident"]
    STEP, G, R = 16, 4, 8
    ROW = D + E
    with ExitStack() as ctx:
        sb, pb, sem, start = allocators(nc, ctx, name)
        waits_p = sb("waits_p", [P, 1 + STEP // G + STEP], F32)
        slot = [sb(f"slot{j}", [P, 1], I32) for j in range(STEP)]
        rows = [sb(f"rows{j}", [P, ROW], F32) for j in range(R)]
        w_gu = [sb(f"w_gu{j}", [P, KD, 2 * FE], F32) for j in range(R)]
        w_dn = [sb(f"w_dn{j}", [FE, D], F32) for j in range(R)]
        hT = [sb(f"hT{j}", [P, KD * P], F32) for j in range(2)]
        gated = [sb(f"gated{j}", [FE, P], F32) for j in range(2)]
        mid = [sb(f"mid{j}", [FE, P], F32) for j in range(2)]
        weight = [sb(f"weight{j}", [P, 1], F32) for j in range(R)]
        y = [sb(f"y{j}", [P, D], F32) for j in range(R)]
        odd = sb("odd", [P, NT, D], F32)
        ps_t = [pb(f"ps_t{i}", [P, 512], F32) for i in range(2)]
        ps_g = [pb(f"ps_g{i}", [P, 512], F32) for i in range(2)]
        ps_u = [pb(f"ps_u{i}", [P, 512], F32) for i in range(2)]
        ps_y = [pb(f"ps_y{i}", [P, 512], F32) for i in range(2)]
        gathered = [sem(f"gathered{j}", from_zero=True) for j in range(R)]
        added = [sem(f"added{i}", from_zero=True) for i in range(2)]
        w_landed = [sem(f"w_landed{j}") for j in range(R)]
        waits_set, carried = sem("waits_set"), sem("carried")
        slot_ready, hT_psum, hT_ready = sem("slot_ready"), sem("hT_psum"), sem("hT_ready")
        gu_psum, silu_ready, mid_ready, y_psum, y_ready = sem("gu_psum"), sem("silu_ready"), sem("mid_ready"), sem("y_psum"), sem("y_ready")
        weight_ready, back = sem("weight_ready"), [sem(f"back{i}") for i in range(2)]
        block = start()

        def count(n):
            return START + (max(n, 0) if isinstance(n, int) else n)

        def walk(engine, step, tail):
            for m in range(STEP):
                step(0, m, m)
            with engine.Fori(1, E // STEP) as i:
                for m in range(STEP):
                    step(i, STEP * i + m, m)
            tail()

        def wait_added(engine, i, m, back_by):
            n = STEP // 2 * i + (m - back_by) // 2 + 1
            if not isinstance(n, int) or n > 0:
                engine.wait_ge(added[(m - back_by) % 2], 16 * n)

        def is_gathered(engine, i, m):
            engine.wait_ge(gathered[m % R], 16 * (STEP // R * i + m // R + 1))

        @block.sync
        def _(sp):
            def step(i, e, m):
                j = m % R
                sp.wait_ge(y_psum, count(e - R + 1))
                sp.dma_start(w_gu[j][:], gate_up_dram[bass.ds(e, 1)].rearrange("o (k p) f -> p (o k) f", p=P)).then_inc(w_landed[j], 16)
                sp.dma_start(w_dn[j][:], down_dram[bass.ds(e, 1)].rearrange("o f d -> f (o d)")).then_inc(w_landed[j], 16)

            walk(sp, step, lambda: None)
            for par in range(2):
                sp.wait_ge(added[par], 16 * (E // 2))
                sp.dma_start((x_res, odd)[par][:], sums_dram[par][0:T, :].rearrange("(t p) d -> p t d", p=P)).then_inc(back[par], 16)

        @block.gpsimd
        def _(pool):
            PER = STEP + STEP // G

            def before(i):
                return 0 if isinstance(i, int) else PER * i - G

            def gather(i, e, m):
                pool.wait_ge(slot_ready, count(e + G))
                pool.wait_ge(hT_psum, count(e + G - R))
                pool.wait_ge(weight_ready, count(e + G - R))
                carry_on_pool(nc, waits_p, 1 + m // G, carried, before(i))
                for n in range(m, m + G):
                    nc.gpsimd.indirect_dma_start(rows[n % R][:], None, rows_dram, bass.IndirectOffsetOnAxis(slot[n][:, 0:1], 0))\
                      .then_inc(gathered[n % R], 16)

            def scatter(i, e, m, carried_before):
                n = (m - G) % STEP
                pool.wait_ge(y_ready, count(e - G + 1))
                wait_added(pool, i, m, G + 2)
                carry_on_pool(nc, waits_p, 1 + STEP // G + m, carried, carried_before)
                nc.gpsimd.indirect_dma_start(sums_dram[n % 2], bass.IndirectOffsetOnAxis(slot[n][:, 0:1], 0), y[n % R][:], None,
                                             bounds_check=T + P - 1, oob_is_err=True, compute_op=ALU.add).then_inc(added[n % 2], 16)

            def step(i, e, m):
                if m % G == 0:
                    gather(i, e, m)
                if not isinstance(i, int) or m >= G:
                    scatter(i, e, m, before(i))

            def tail():
                for m in range(G):
                    scatter(E // STEP, E + m, m, PER * (E // STEP) - G)
                for par in range(2):
                    pool.wait_ge(added[par], 16 * (E // 2))

            nc.gpsimd.memset(waits_p[:], 0.0).then_inc(waits_set, 1)
            pool.wait_ge(waits_set, START + 1)
            walk(pool, step, tail)

        @block.tensor
        def _(pe):
            def rows_to_features(i, e, m):
                is_gathered(pe, i, m)
                pe.wait_ge(hT_ready, count(e - 1))
                for k in range(KD):
                    mm = nc.tensor.transpose(ps_t[m % 2][:, P * k:P * k + P], rows[m % R][:, P * k:P * k + P], ident[:])
                mm.then_inc(hT_psum, 1)

            def gate_and_up(i, e, m):
                j = m % R
                pe.wait_ge(w_landed[j], START + 32 * (STEP // R * i + m // R + 1))
                pe.wait_ge(hT_ready, count(e + 1))
                pe.wait_ge(mid_ready, count(e - 1))
                for base, ps in ((FE, ps_u), (0, ps_g)):
                    for k in range(KD):
                        mm = nc.tensor.matmul(ps[m % 2][0:FE, 0:P], w_gu[j][:, k, base:base + FE], hT[m % 2][:, P * k:P * k + P],
                                              start=(k == 0), stop=(k == KD - 1))
                mm.then_inc(gu_psum, 1)

            def down(i, e, m):
                pe.wait_ge(mid_ready, count(e + 1))
                pe.wait_ge(y_ready, count(e - 1))
                nc.tensor.matmul(ps_y[m % 2][:, 0:D], mid[m % 2][:], w_dn[m % R][:], start=True, stop=True).then_inc(y_psum, 1)

            def step(i, e, m):
                rows_to_features(i, e, m)
                if not isinstance(i, int) or m >= 1:
                    gate_and_up(i if m >= 1 else i - 1, e - 1, (m - 1) % STEP)
                if not isinstance(i, int) or m >= 2:
                    down(i, e - 2, (m - 2) % STEP)

            def tail():
                gate_and_up(E // STEP - 1, E - 1, STEP - 1)
                down(None, E - 2, STEP - 2)
                down(None, E - 1, STEP - 1)

            walk(pe, step, tail)

        @block.scalar
        def _(act):
            def to_sbuf(i, e, m):
                act.wait_ge(hT_psum, count(e + 1))
                act.wait_ge(gu_psum, count(e - 1))
                nc.scalar.copy(hT[m % 2][:], ps_t[m % 2][:, 0:KD * P]).then_inc(hT_ready, 1)

            def silu(i, e, m):
                act.wait_ge(gu_psum, count(e + 1))
                act.wait_ge(mid_ready, count(e - 1))
                nc.scalar.activation(gated[m % 2][:], ps_g[m % 2][0:FE, 0:P], ACT.Silu).then_inc(silu_ready, 1)

            def step(i, e, m):
                to_sbuf(i, e, m)
                if not isinstance(i, int) or m >= 1:
                    silu(i, e - 1, (m - 1) % STEP)

            walk(act, step, lambda: silu(None, E - 1, STEP - 1))

        @block.vector
        def _(v):
            def slots(i, e, m):
                for n in range(G):
                    wait_added(v, i, m + n, STEP)
                    nc.vector.tensor_copy(slot[m + n][:], slot_token[:, bass.ds(e + n, 1)]).then_inc(slot_ready, 1)

            def middle(i, e, m):
                is_gathered(v, i, m)
                wait_added(v, i, m, R)
                nc.vector.tensor_copy(weight[m % R][:], rows[m % R][:, bass.ds(D + e, 1)]).then_inc(weight_ready, 1)
                v.wait_ge(silu_ready, count(e + 1))
                v.wait_ge(y_psum, count(e - 1))
                nc.vector.tensor_tensor(mid[m % 2][:], gated[m % 2][:], ps_u[m % 2][0:FE, 0:P], ALU.mult).then_inc(mid_ready, 1)

            def weigh(i, e, m):
                v.wait_ge(y_psum, count(e + 1))
                v.wait_ge(weight_ready, count(e + 1))
                nc.vector.tensor_scalar(y[m % R][:], ps_y[m % 2][:, 0:D], weight[m % R][:, 0:1], None, ALU.mult).then_inc(y_ready, 1)

            def step(i, e, m):
                if m % G == 0:
                    slots(i, e, m)
                if not isinstance(i, int) or m >= G:
                    middle(i if m >= G else i - 1, e - G, (m - G) % STEP)
                if not isinstance(i, int) or m >= G + 1:
                    weigh(i, e - G - 1, (m - G - 1) % STEP)

            def tail():
                for m in range(G):
                    middle(E // STEP - 1, E - G + m, STEP - G + m)
                    weigh(None, E - G - 1 + m, STEP - G - 1 + m)
                weigh(None, E - 1, STEP - 1)
                for par in range(2):
                    v.wait_ge(back[par], START + 16)
                for t in range(0, NT, 8):
                    ins = nc.vector.tensor_tensor(x_res[:, t:t + 8, :], x_res[:, t:t + 8, :], odd[:, t:t + 8, :], ALU.add)
                ins.then_inc(back[0], 1)
                v.wait_ge(back[0], START + 17)

            walk(v, step, tail)


def state_space_layer(nc, x_res, consts, w_in_dram, w_out_dram, vec, mats):
    ident = consts["ident"]
    NH, NP_, DI, TAPS = 4, 128, 512, 4
    KI = DI // P
    PROJ = 2 * DI + NH + 2 * P
    DT0, B0, C0 = 2 * DI, 2 * DI + NH, 2 * DI + NH + P
    RMS_EPS = 1e-6
    with ExitStack() as ctx:
        sb, pb, sem, start = allocators(nc, ctx, "ssm")
        w_in = sb("w_in", [P, KD, PROJ], F32)
        w_out = sb("w_out", [P, KI, D], F32)
        cols = sb("cols", [P, KD + 2 * KI + KI * TAPS], F32)
        norm_c = cols[:, 0:KD]
        conv_b = cols[:, KD:KD + KI]
        skip_c = cols[:, KD + KI:KD + 2 * KI]
        conv_w = cols[:, KD + 2 * KI:].rearrange("p (c k) -> p c k", k=TAPS)
        heads = sb("heads", [P, 2, NH], F32)
        upper = sb("upper", [P, P], F32)
        last = sb("last", [P, P], F32)
        waits_p = sb("waits_p", [P, 2], F32)
        h_all = sb("h_all", [P, NT, D], F32)
        hT_all = sb("hT_all", [P, KD, T], F32)
        stats = sb("stats", [P, NT, 6], F32)
        mv = sb("mv", [P, NT, 2], F32)
        rstd = sb("rstd", [P, 3, NT], F32)
        rms = sb("rms", [P, 4, NT], F32)
        z = sb("z", [P, NT, NH], F32)
        spl = sb("spl", [P, 3, NT * NH], F32)
        dt = sb("dt", [P, NT, NH], F32)
        a_neg = sb("a_neg", [P, NH], F32)
        log_a = sb("log_a", [P, NT, NH], F32)
        cum = sb("cum", [P, NT, NH], F32)
        to_end = sb("to_end", [P, NT, NH], F32)
        dec_end = sb("dec_end", [P, NT, NH], F32)
        dec_in = sb("dec_in", [P, NT, NH], F32)
        dec_chunk = sb("dec_chunk", [P, NT, NH], F32)

        with ExitStack() as ctx1:
            sb1, pb1, sem1, start = allocators(nc, ctx1, "ssm_a")
            square = sb1("square", [P, 2, D], F32)
            hn = sb1("hn", [P, 2, D], F32)
            hT = sb1("hT", [P, 2, KD, P], F32)
            ps_t = [pb1(f"ps_t{i}", [P, 512], F32) for i in range(2)]
            ps_d = [pb1(f"ps_d{i}", [P, 512], F32) for i in range(2)]
            landed, scaled = sem1("landed"), sem1("scaled")
            dve = sem1("dve")
            var_ready, std_ready = sem1("var_ready"), sem1("std_ready")
            h_ready, squared, ms_ready, root_ready = sem1("h_ready"), sem1("squared"), sem1("ms_ready"), sem1("root_ready")
            hn_ready, hT_psum, hT_ready, dt_psum, z_done = sem1("hn_ready"), sem1("hT_psum"), sem1("hT_ready"), sem1("dt_psum"), sem1("z_done")
            carried = sem1("carried")
            kept, added = sem1("kept"), sem1("added")
            z_parts, exp_ready, log_ready = sem1("z_parts"), sem1("exp_ready"), sem1("log_ready")
            la_ready, cum_psum, cum_ready, end_psum, ends_ready, decays = (sem1(n) for n in (
                "la_ready", "cum_psum", "cum_ready", "end_psum", "ends_ready", "decays"))
            block = start()
            LOADS = 6

            @block.sync
            def _(sp):
                sp.dma_start(w_in[:], w_in_dram.rearrange("(k p) n -> p k n", p=P)).then_inc(landed, 16)
                sp.dma_start(w_out[:], w_out_dram.rearrange("(k p) n -> p k n", p=P)).then_inc(landed, 16)
                sp.dma_start(cols[:], vec[0]).then_inc(landed, 16)
                sp.dma_start(heads[:].rearrange("p a h -> p (a h)"), vec[1].partition_broadcast(P)).then_inc(landed, 16)
                sp.dma_start(upper[:], mats[0]).then_inc(landed, 16)
                sp.dma_start(last[:], mats[1]).then_inc(landed, 16)

            @block.tensor
            def _(pe):
                pe.wait_ge(scaled, START + KD)
                with pe.Fori(0, NT // 2) as i:
                    for par in range(2):
                        n = 2 * i + par
                        pe.wait_ge(hn_ready, START + n + 1)
                        for k in range(KD):
                            mm = nc.tensor.transpose(ps_t[par][:, P * k:P * k + P], hn[:, par, P * k:P * k + P], ident[:])
                        mm.then_inc(hT_psum, 1)
                    for par in range(2):
                        n = 2 * i + par
                        pe.wait_ge(hT_ready, START + n + 1)
                        for k in range(KD):
                            mm = nc.tensor.matmul(ps_d[par][:, 0:NH], hT[:, par, k, :], w_in[:, k, DT0:DT0 + NH],
                                                  start=(k == 0), stop=(k == KD - 1))
                        mm.then_inc(dt_psum, 1)
                pe.wait_ge(la_ready, START + 1)
                nc.tensor.matmul(ps_t[0][:, 0:NT * NH], upper[:], log_a[:].rearrange("p t h -> p (t h)"), start=True, stop=True)\
                  .then_inc(cum_psum, 1)
                pe.wait_ge(cum_ready, START + 1)
                nc.tensor.matmul(ps_t[1][:, 0:NT * NH], last[:], cum[:].rearrange("p t h -> p (t h)"), start=True, stop=True)\
                  .then_inc(end_psum, 1)

            @block.scalar
            def _(act):
                act.wait_ge(var_ready, START + 1)
                nc.scalar.activation(rstd[:, 1], rstd[:, 0], ACT.Sqrt).then_inc(std_ready, 1)
                with act.Fori(0, NT // 2) as i:
                    for par in range(2):
                        n = 2 * i + par
                        act.wait_ge(h_ready, START + n + 1)
                        act.wait_ge(squared, START + n)
                        nc.scalar.activation(square[:, 0, :], one_tile(h_all, n), ACT.Square,
                                             accum_out=rms[:, 0, bass.ds(n, 1)]).then_inc(squared, 1)
                act.wait_ge(ms_ready, START + 1)
                nc.scalar.activation(rms[:, 2], rms[:, 1], ACT.Sqrt).then_inc(root_ready, 1)
                with act.Fori(0, NT // 2) as i:
                    for par in range(2):
                        n = 2 * i + par
                        act.wait_ge(hT_psum, START + n + 1)
                        act.wait_ge(dt_psum, START + 2 * i)
                        act.wait_ge(kept, START + 2 * i + 1)
                        nc.scalar.copy(hT[:, par, :, :], ps_t[par][:, 0:KD * P].rearrange("p (k n) -> p k n", k=KD))\
                          .then_inc(hT_ready, 1)
                act.wait_ge(z_parts, START + 1)
                nc.scalar.activation(spl[:, 1], spl[:, 0], ACT.Exp).then_inc(exp_ready, 1)
                nc.scalar.activation(a_neg[:], heads[:, 0, :], ACT.Exp).then_inc(exp_ready, 1)
                act.wait_ge(exp_ready, START + 1)
                nc.scalar.activation(spl[:, 2], spl[:, 1], ACT.Ln, bias=1.0).then_inc(log_ready, 1)
                act.wait_ge(ends_ready, START + 1)
                for out, in_ in ((dec_end, to_end), (dec_in, cum), (dec_chunk, dec_chunk)):
                    nc.scalar.activation(out[:], in_[:], ACT.Exp).then_inc(decays, 1)

            @block.gpsimd
            def _(pool):
                nc.gpsimd.memset(waits_p[:], 0.0).then_inc(kept, 1)
                pool.wait_ge(kept, START + 1)
                with pool.Fori(0, NT // 2) as i:
                    for par in range(2):
                        n = 2 * i + par
                        pool.wait_ge(hT_ready, START + n + 1)
                        carry_on_pool(nc, waits_p, 1, carried, n)
                        nc.gpsimd.tensor_copy(hT_all[:, :, bass.ds(n * P, P)], hT[:, par, :, :]).then_inc(kept, 1)
                        nc.gpsimd.tensor_tensor(one_tile(x_res, n), one_tile(x_res, n), one_tile(h_all, n), ALU.add).then_inc(added, 1)

            @block.vector
            def _(v):
                v.wait_ge(landed, START + 16 * LOADS)
                for k in range(KD):
                    nc.vector.tensor_scalar(w_in[:, k, :], w_in[:, k, :], norm_c[:, k:k + 1], None, ALU.mult).then_inc(scaled, 1)
                layer_norm_statistics(nc, v, x_res, stats, mv, rstd, dve, var_ready, std_ready)
                step = Steps(v, dve)
                with v.Fori(0, NT // 4) as i:
                    for j in range(4):
                        n = 4 * i + j
                        nc.vector.tensor_scalar(one_tile(h_all, n), one_tile(x_res, n), mean_of(mv, n), rstd_of(rstd, n),
                                                ALU.subtract, ALU.mult).then_inc(h_ready, 1)
                v.wait_ge(squared, START + NT)
                v.wait_ge(h_ready, START + NT)
                nc.vector.tensor_scalar(rms[:, 1], rms[:, 0], 1.0 / D, RMS_EPS, ALU.mult, ALU.add).then_inc(ms_ready, 1)
                v.wait_ge(root_ready, START + 1)
                step.begin(2 * NT + 1)
                step.done(nc.vector.reciprocal(rms[:, 3], rms[:, 2]))
                step.wait()
                with v.Fori(0, NT // 2) as i:
                    for par in range(2):
                        n = 2 * i + par
                        v.wait_ge(hT_psum, START + 2 * i)
                        nc.vector.tensor_scalar(hn[:, par, :], one_tile(h_all, n), rms[:, 3, bass.ds(n, 1)], None, ALU.mult)\
                          .then_inc(hn_ready, 1)
                    for par in range(2):
                        n = 2 * i + par
                        v.wait_ge(dt_psum, START + n + 1)
                        nc.vector.tensor_tensor(z[:, bass.ds(n, 1), :].rearrange("p o h -> p (o h)"), ps_d[par][:, 0:NH],
                                                heads[:, 1, :], ALU.add).then_inc(z_done, 1)
                v.wait_ge(z_done, START + NT)
                zf = z[:].rearrange("p t h -> p (t h)")
                step.done(nc.vector.tensor_scalar(spl[:, 1], zf, -1.0, None, ALU.mult))
                step.wait()
                nc.vector.tensor_tensor(spl[:, 0], zf, spl[:, 1], ALU.min).then_inc(z_parts, 1)
                v.wait_ge(log_ready, START + 1)
                dtf, laf = dt[:].rearrange("p t h -> p (t h)"), log_a[:]
                step.done(nc.vector.scalar_tensor_tensor(dtf, zf, 0.0, spl[:, 2], ALU.max, ALU.add))
                step.wait()
                v.wait_ge(exp_ready, START + 2)
                nc.vector.scalar_tensor_tensor(laf, dt[:], -1.0, a_neg[:].unsqueeze(1).to_broadcast([P, NT, NH]), ALU.mult, ALU.mult)\
                  .then_inc(la_ready, 1)
                v.wait_ge(cum_psum, START + 1)
                nc.vector.tensor_copy(cum[:].rearrange("p t h -> p (t h)"), ps_t[0][:, 0:NT * NH]).then_inc(cum_ready, 1)
                v.wait_ge(end_psum, START + 1)
                v.wait_ge(cum_ready, START + 1)
                end = ps_t[1][:, 0:NT * NH]
                step.done(nc.vector.tensor_tensor(to_end[:].rearrange("p t h -> p (t h)"), end, cum[:].rearrange("p t h -> p (t h)"),
                                                  ALU.subtract))
                nc.vector.tensor_copy(dec_chunk[:].rearrange("p t h -> p (t h)"), end).then_inc(ends_ready, 1)
                v.wait_ge(decays, START + 3)

        with ExitStack() as ctx2:
            sb2, pb2, sem2, start = allocators(nc, ctx2, "ssm_b")
            gate = sb2("gate", [P, KI, S], F32)
            HIST = TAPS - 1
            u = sb2("u", [P, KI, HIST + S], F32)
            acc = sb2("acc", [P, 2, S], F32)
            xs = u
            bT = sb2("bT", [P, S], F32)
            cT = sb2("cT", [P, S], F32)
            state = sb2("state", [P, NH, NP_], F32)
            b_tok = sb2("b_tok", [P, P], F32)
            x_dt = sb2("x_dt", [P, NH, NP_], F32)
            x_end = sb2("x_end", [P, NH, NP_], F32)
            diff = sb2("diff", [P, NH, P], F32)
            decay = sb2("decay", [P, NH, P], F32)
            cb = sb2("cb", [P, P], F32)
            cum_c = sb2("cum_c", [P, NH], F32)
            mix = sb2("mix", [P, NH, P], F32)
            y_in = sb2("y_in", [P, NH, NP_], F32)
            y_tok = sb2("y_tok", [P, NH, NP_], F32)
            yT = sb2("yT", [P, NH, P], F32)
            zT = sb2("zT", [P, NH, P], F32)
            ps_x, ps_b, ps_r, ps_y, ps_i, ps_s, ps_z, ps_o = (pb2(f"ps{i}", [P, 512], F32) for i in range(8))
            proj_banks = (ps_y, ps_i, ps_s, ps_z)
            dve = sem2("dve")
            proj_psum, gate_done, other_done = sem2("proj_psum"), sem2("gate_done"), sem2("other_done")
            conv_ready, conv_done = sem2("conv_ready"), sem2("conv_done")
            x_psum, bc_psum, row_psum, diff_ready, decay_ready = (sem2(n) for n in ("x_psum", "bc_psum", "row_psum", "diff_ready", "decay_ready"))
            cum_c_ready, carried = sem2("cum_c_ready"), sem2("carried")
            cb_ready, mix_ready, xdt_ready, xend_ready, state_ready = (sem2(n) for n in ("cb_ready", "mix_ready", "xdt_ready", "xend_ready", "state_ready"))
            intra_psum, inter_psum, local_psum, y_ready = (sem2(n) for n in ("intra_psum", "inter_psum", "local_psum", "y_ready"))
            yT_psum, zT_ready, out_psum, x_done = (sem2(n) for n in ("yT_psum", "zT_ready", "out_psum", "x_done"))
            block = start()
            HALF = 512
            UNITS = []
            for half in range(S // HALF):
                for c in range(KI):
                    UNITS += [(c * P, "gate", c, half), (DI + c * P, "u", c, half)]
                UNITS += [(B0, "b", 0, half), (C0, "c", 0, half)]
            NG_ = sum(kind == "gate" for _, kind, _, _ in UNITS)
            NO_ = len(UNITS) - NG_

            def done_before(n):
                g = sum(kind == "gate" for _, kind, _, _ in UNITS[:n])
                return g, n - g

            DVE_B = KI * (TAPS - 1)
            DVE_C = 2

            def of_heads(values, n):
                return values[:, bass.ds(n, 1), :].rearrange("p o h -> p (o h)").unsqueeze(2).to_broadcast([P, NH, NP_])

            @block.tensor
            def _(pe):
                def spread(n, c):
                    tok = slice(P * c, P * c + P)
                    pe.wait_ge(xdt_ready, START + n)
                    for h in range(NH):
                        mm = nc.tensor.transpose(ps_x[:, P * h:P * h + P], xs[:, h, HIST + P * c:HIST + P * c + P], ident[:])
                    mm.then_inc(x_psum, 1)
                    pe.wait_ge(cb_ready, START + n)
                    nc.tensor.transpose(ps_b[:, 0:P], bT[:, tok], ident[:])
                    nc.tensor.matmul(ps_b[:, P:2 * P], bT[:, tok], cT[:, tok], start=True, stop=True).then_inc(bc_psum, 1)
                    pe.wait_ge(diff_ready, START + n)
                    pe.wait_ge(cum_c_ready, START + n + 1)
                    for h in range(NH):
                        mm = nc.tensor.transpose(ps_r[:, P * h:P * h + P], cum_c[:, h:h + 1].to_broadcast([P, P]), ident[:])
                    mm.then_inc(row_psum, 1)

                def scan(b, c):
                    n = TS * b + c
                    pe.wait_ge(y_ready, START + n)
                    pe.wait_ge(state_ready, START + (TS + 1) * b + c + 1)
                    nc.tensor.matmul(ps_i[:], cT[:, P * c:P * c + P], state[:].rearrange("p h d -> p (h d)"), start=True, stop=True)\
                      .then_inc(inter_psum, 1)
                    pe.wait_ge(mix_ready, START + n + 1)
                    pe.wait_ge(xdt_ready, START + n + 1)
                    for h in range(NH):
                        mm = nc.tensor.matmul(ps_y[:, P * h:P * h + P], mix[:, h, :], x_dt[:, h, :], start=True, stop=True)
                    mm.then_inc(intra_psum, 1)
                    pe.wait_ge(xend_ready, START + n + 1)
                    pe.wait_ge(cb_ready, START + n + 1)
                    nc.tensor.matmul(ps_s[:], b_tok[:], x_end[:].rearrange("p h d -> p (h d)"), start=True, stop=True).then_inc(local_psum, 1)

                def finish(n):
                    pe.wait_ge(y_ready, START + n + 1)
                    pe.wait_ge(zT_ready, START + n)
                    for h in range(NH):
                        mm = nc.tensor.transpose(ps_z[:, P * h:P * h + P], y_tok[:, h, :], ident[:])
                    mm.then_inc(yT_psum, 1)
                    pe.wait_ge(zT_ready, START + n + 1)
                    pe.wait_ge(x_done, START + n)
                    for h in range(NH):
                        mm = nc.tensor.matmul(ps_o[:, 0:D], zT[:, h, :], w_out[:, h, :], start=(h == 0), stop=(h == NH - 1))
                    mm.then_inc(out_psum, 1)

                with pe.Fori(0, B) as b:
                    for n, (col, kind, c, half) in enumerate(UNITS):
                        if n >= 4:
                            g, o = done_before(n - 3)
                            if UNITS[n - 4][1] == "gate":
                                pe.wait_ge(gate_done, START + NG_ * b + g)
                            else:
                                pe.wait_ge(other_done, START + NO_ * b + o)
                        elif n == 0:
                            pe.wait_ge(x_done, START + TS * b)
                        for k in range(KD):
                            mm = nc.tensor.matmul(proj_banks[n % 4][:], w_in[:, k, col:col + P],
                                                  hT_all[:, k, bass.ds(b * S + half * HALF, HALF)], start=(k == 0), stop=(k == KD - 1))
                        mm.then_inc(proj_psum, 1)
                    pe.wait_ge(conv_done, START + KI * b + KI)
                    pe.wait_ge(other_done, START + NO_ * b + NO_)
                    pe.wait_ge(gate_done, START + NG_ * b + NG_)
                    spread(TS * b, 0)
                    for c in range(TS):
                        scan(b, c)
                        if c < TS - 1:
                            spread(TS * b + c + 1, c + 1)
                        finish(TS * b + c)

            @block.scalar
            def _(act):
                with act.Fori(0, B) as b:
                    act.wait_ge(zT_ready, START + TS * b)
                    g = 0
                    for n, (col, kind, c, half) in enumerate(UNITS):
                        if kind == "gate":
                            act.wait_ge(proj_psum, START + len(UNITS) * b + n + 1)
                            nc.scalar.activation(gate[:, c, HALF * half:HALF * half + HALF], proj_banks[n % 4][:], ACT.Silu).then_inc(gate_done, 1)
                    for c in range(KI):
                        act.wait_ge(conv_ready, START + KI * b + c + 1)
                        nc.scalar.activation(xs[:, c, HIST:], acc[:, c % 2, :], ACT.Silu).then_inc(conv_done, 1)
                    for c in range(TS):
                        n = TS * b + c
                        act.wait_ge(diff_ready, START + n + 1)
                        act.wait_ge(mix_ready, START + n)
                        nc.scalar.activation(decay[:], diff[:], ACT.Exp).then_inc(decay_ready, 1)

            @block.gpsimd
            def _(pool):
                with pool.Fori(0, B) as b:
                    for c in range(TS):
                        n = TS * b + c
                        pool.wait_ge(row_psum, START + n)
                        carry_on_pool(nc, waits_p, 1, carried, n)
                        nc.gpsimd.tensor_copy(cum_c[:], cum[:, bass.ds(n, 1), :].rearrange("p o h -> p (o h)")).then_inc(cum_c_ready, 1)
                        pool.wait_ge(xdt_ready, START + n + 1)
                        pool.wait_ge(local_psum, START + n)
                        nc.gpsimd.tensor_tensor(x_end[:], x_dt[:], of_heads(dec_end, n), ALU.mult).then_inc(xend_ready, 1)

            @block.vector
            def _(v):
                step = Steps(v, dve)
                nc.vector.memset(u[:, :, 0:HIST], 0.0).then_inc(dve, 1)
                v.wait_ge(dve, START + 1)

                def inputs(n):
                    v.wait_ge(x_psum, START + n + 1)
                    v.wait_ge(intra_psum, START + n)
                    v.wait_ge(xend_ready, START + n)
                    nc.vector.tensor_tensor(x_dt[:], ps_x[:].rearrange("p (h d) -> p h d", h=NH), of_heads(dt, n), ALU.mult)\
                      .then_inc(xdt_ready, 1)
                    v.wait_ge(bc_psum, START + n + 1)
                    v.wait_ge(local_psum, START + n)
                    nc.vector.tensor_copy(b_tok[:], ps_b[:, 0:P])
                    nc.vector.tensor_tensor(cb[:], ps_b[:, P:2 * P], upper[:], ALU.mult).then_inc(cb_ready, 1)
                    v.wait_ge(row_psum, START + n + 1)
                    v.wait_ge(decay_ready, START + n)
                    for h in range(NH):
                        ins = nc.vector.tensor_scalar(diff[:, h, :], ps_r[:, P * h:P * h + P], cum[:, bass.ds(n, 1), h:h + 1].rearrange("p o h -> p (o h)"),
                                                      0.0, ALU.subtract, ALU.min)
                    ins.then_inc(diff_ready, 1)

                with v.Fori(0, B) as b:
                    step.begin(1 + (DVE_B + DVE_C * TS) * b)
                    v.wait_ge(x_psum, START + TS * b)
                    v.wait_ge(inter_psum, START + TS * b)
                    for n, (col, kind, c, half) in enumerate(UNITS):
                        if kind == "gate":
                            continue
                        v.wait_ge(proj_psum, START + len(UNITS) * b + n + 1)
                        dst = {"u": u[:, c, HIST + HALF * half:HIST + HALF * half + HALF], "b": bT[:, HALF * half:HALF * half + HALF],
                               "c": cT[:, HALF * half:HALF * half + HALF]}[kind]
                        nc.vector.tensor_copy(dst, proj_banks[n % 4][:]).then_inc(other_done, 1)
                    nc.vector.memset(state[:], 0.0).then_inc(state_ready, 1)
                    v.wait_ge(other_done, START + NO_ * b + NO_)
                    for c in range(KI):
                        v.wait_ge(conv_done, START + KI * b + max(c - 1, 0))
                        for k in range(TAPS):
                            tap = u[:, c, k:k + S]
                            if k == 0:
                                step.done(nc.vector.tensor_scalar(acc[:, c % 2, :], tap, conv_w[:, c, 0:1], conv_b[:, c:c + 1], ALU.mult, ALU.add))
                                step.wait()
                                continue
                            ins = nc.vector.scalar_tensor_tensor(acc[:, c % 2, :], tap, conv_w[:, c, k:k + 1], acc[:, c % 2, :], ALU.mult, ALU.add)
                            if k < TAPS - 1:
                                step.done(ins)
                                step.wait()
                            else:
                                ins.then_inc(conv_ready, 1)
                    inputs(TS * b)
                    for c in range(TS):
                        n = TS * b + c
                        v.wait_ge(decay_ready, START + n + 1)
                        v.wait_ge(cb_ready, START + n + 1)
                        v.wait_ge(intra_psum, START + n)
                        nc.vector.tensor_tensor(mix[:], decay[:], cb[:].unsqueeze(1).to_broadcast([P, NH, P]), ALU.mult).then_inc(mix_ready, 1)
                        v.wait_ge(inter_psum, START + n + 1)
                        step.done(nc.vector.tensor_tensor(y_in[:], ps_i[:].rearrange("p (h d) -> p h d", h=NH), of_heads(dec_in, n), ALU.mult))
                        step.wait()
                        v.wait_ge(intra_psum, START + n + 1)
                        v.wait_ge(yT_psum, START + n)
                        nc.vector.tensor_tensor(y_tok[:], y_in[:], ps_y[:].rearrange("p (h d) -> p h d", h=NH), ALU.add).then_inc(y_ready, 1)
                        v.wait_ge(local_psum, START + n + 1)
                        v.wait_ge(state_ready, START + (TS + 1) * b + c + 1)
                        for h in range(NH):
                            ins = nc.vector.scalar_tensor_tensor(state[:, h, :], state[:, h, :], dec_chunk[:, bass.ds(n, 1), h:h + 1].rearrange("p o h -> p (o h)"),
                                                                 ps_s[:, P * h:P * h + P], ALU.mult, ALU.add)
                        ins.then_inc(state_ready, 1)
                        if c < TS - 1:
                            inputs(n + 1)
                        v.wait_ge(yT_psum, START + n + 1)
                        for h in range(NH):
                            ins = nc.vector.scalar_tensor_tensor(yT[:, h, :], xs[:, h, HIST + P * c:HIST + P * c + P], skip_c[:, h:h + 1],
                                                                 ps_z[:, P * h:P * h + P], ALU.mult, ALU.add)
                        step.done(ins)
                        step.wait()
                        v.wait_ge(out_psum, START + n)
                        nc.vector.tensor_tensor(zT[:], yT[:], gate[:, :, P * c:P * c + P], ALU.mult).then_inc(zT_ready, 1)
                        v.wait_ge(out_psum, START + n + 1)
                        nc.vector.tensor_tensor(one_tile(x_res, n), one_tile(x_res, n), ps_o[:, 0:D], ALU.add).then_inc(x_done, 1)
                    step.end(DVE_B + DVE_C * TS)

def load_phase(nc, x_dram, const_dram, x_res, consts):
    with ExitStack() as ctx:
        sb, pb, sem, start = allocators(nc, ctx, "load")
        masks = sb("masks", [P, 3, P], F32)
        landed, copied = sem("landed"), sem("copied")
        block = start()

        @block.sync
        def _(sp):
            sp.dma_start(consts["ident"][:], const_dram[0]).then_inc(landed, 16)
            sp.dma_start(masks[:], const_dram[0:3].rearrange("m p n -> p m n")).then_inc(landed, 16)
            sp.dma_start(x_res[:], x_dram.rearrange("(t p) d -> p t d", p=P)).then_inc(landed, 16)
            sp.wait_ge(landed, START + 48)

        @block.vector
        def _(v):
            v.wait_ge(landed, START + 48)
            for i, what in enumerate(("ident_b", "causal_q", "causal_k")):
                nc.vector.tensor_copy(consts[what][:], masks[:, i, :]).then_inc(copied, 1)
            v.wait_ge(copied, START + 3)


def store_phase(nc, x_res, out_dram):
    with ExitStack() as ctx:
        sb, pb, sem, start = allocators(nc, ctx, "store")
        stored = sem("stored")
        block = start()

        @block.sync
        def _(sp):
            sp.dma_start(out_dram.rearrange("(t p) d -> p t d", p=P), x_res[:]).then_inc(stored, 16)
            sp.wait_ge(stored, START + 16)


def program(nc, a, out):
    moe_rows = nc.dram_tensor("moe_rows", [T + P, D + E], F32).ap()
    moe_sums = [nc.dram_tensor(f"moe_sums{i}", [T + P, D], F32).ap() for i in range(2)]
    with ExitStack() as ctx:
        def sb(what, shape, dt):
            return ctx.enter_context(nc.sbuf_tensor(what, shape, dt))

        x_res = sb("x_res", [P, NT, D], F32)
        consts = {"ident": sb("ident", [P, P], F32), "ident_b": sb("ident_b", [P, P], BF16),
                  "causal_q": sb("causal_q", [P, P], BF16), "causal_k": sb("causal_k", [P, P], BF16)}
        load_phase(nc, a["x"], a["masks"], x_res, consts)
        attention_layer(nc, "attn1", x_res, consts, a["wqkv1"], a["wo1"], a["rope"])
        with ExitStack() as mlp:
            w_ug = mlp.enter_context(nc.sbuf_tensor("w_ug", [P, KD, 2 * INTER], F32))
            w_dn = mlp.enter_context(nc.sbuf_tensor("w_dn", [P, INTER // P, D], F32))
            mlp_weights(nc, w_ug, w_dn, a["wug"], a["wdn"], a["had"], a["su_ug"], a["scale_ug"], a["su_dp"], a["scale_dp"])
            mlp_layer(nc, "mlp1", x_res, consts, w_ug, w_dn)
            attention_layer(nc, "attn2", x_res, consts, a["wqkv2"], a["wo2"], None)
            mlp_layer(nc, "mlp2", x_res, consts, w_ug, w_dn)
        attention_layer(nc, "attn3", x_res, consts, a["wqkv3"], a["wo3"], None)
        moe_layer(nc, "moe1", x_res, consts, a["router"], a["gate_up"], a["down"], a["keyval"], a["slot_no"], moe_rows, moe_sums)
        state_space_layer(nc, x_res, consts, a["ssm_in"], a["ssm_out"], (a["ssm_cols"], a["ssm_heads"]), a["ssm_mats"])
        moe_layer(nc, "moe2", x_res, consts, a["router"], a["gate_up"], a["down"], a["keyval"], a["slot_no"], moe_rows, moe_sums)
        store_phase(nc, x_res, out)


def layouts(i):
    def grouped(wq, wk, wv):
        w = np.stack([wq.T, wk.T, wv.T], axis=1).reshape(D, 3, NG, HG * DH)
        return w.transpose(0, 2, 1, 3).reshape(D, NG * GW)

    row, col = np.arange(P)[:, None], np.arange(P)[None, :]
    masks = np.stack([row == col, np.where(col > row, MASKED, 0.0), np.where(row > col, MASKED, 0.0)])
    freq = (10000.0 ** (-2.0 * np.arange(DH // 2, dtype=np.float32) / DH)).astype(np.float32)
    ang = np.arange(S, dtype=np.float32)[:, None] * freq[None, :]
    rope = np.stack([np.tile(np.repeat(f(ang), 2, axis=-1), (1, 2 * HG)) for f in (np.cos, np.sin)])
    def columns(v):
        return v.reshape(-1, P).T

    had = np.array([[1.0]])
    while had.shape[0] < P:
        had = np.block([[had, had], [had, -had]])
    had = np.stack([had / 16, -had / 16, had / 32, -had / 32])
    x = i["L0_attn_a_x"].reshape(T, D)
    token = np.arange(T).reshape(2, 1, T // 2) + np.zeros((1, E, 1), np.int64)
    qkv2 = np.split(i["L0_attn_b_W_qkv"], 3, axis=0)
    d = {
        "x": x, "masks": masks.astype(np.float32), "rope": rope.astype(np.float32),
        "wqkv1": grouped(i["L0_attn_a_wq"], i["L0_attn_a_wk"], i["L0_attn_a_wv"]), "wo1": i["L0_attn_a_wo"].T,
        "keyval": (T - token).reshape(P, T // 2).astype(np.float32), "slot_no": np.arange(P, dtype=np.float32)[:, None], "router": i["L1_ffn_router_weight"].T,
        "gate_up": i["L1_ffn_gate_up_proj"], "down": i["L1_ffn_down_proj"],
        "ssm_in": i["L1_attn_b_in_proj_w"], "ssm_out": i["L1_attn_b_out_proj_w"],
        "ssm_cols": np.concatenate([columns(i["L1_attn_b_norm_scale"]), columns(i["L1_attn_b_conv_bias"]), columns(i["L1_attn_b_D"]),
                                    i["L1_attn_b_conv_weight"].reshape(4, 4, P).transpose(2, 1, 0).reshape(P, 16)], axis=1),
        "ssm_heads": np.concatenate([i["L1_attn_b_A_log"], i["L1_attn_b_dt_bias"]]),
        "ssm_mats": np.stack([row <= col, row + 0 * col == P - 1]).astype(np.float32),
        "wqkv2": grouped(*qkv2), "wo2": i["L0_attn_b_W_out"].T,
        "wqkv3": grouped(i["L1_attn_a_Wq"], i["L1_attn_a_Wk"], i["L1_attn_a_Wv"]), "wo3": i["L1_attn_a_Wo"].T,
        "had": had.astype(np.float32), "wug": np.concatenate([i["L0_ffn_W_up"].T, i["L0_ffn_W_gate"].T], axis=1),
        "wdn": i["L0_ffn_W_down"].T, "su_ug": columns(i["L0_ffn_SU_ug"]), "su_dp": columns(i["L0_ffn_SU_dp"]),
        "scale_ug": i["L0_ffn_Wscale_ug"], "scale_dp": i["L0_ffn_Wscale_dp"],
    }
    return {k: np.ascontiguousarray(v) for k, v in d.items()}


def kernel(**inputs):
    import concourse.bacc as bacc
    from concourse.bass_utils import run_bass_kernel_spmd

    arrays = layouts({name: np.asarray(a) for name, a in inputs.items()})
    nc = bacc.Bacc("TRN2", target_bir_lowering=False, num_devices=1)
    a = {name: nc.dram_tensor(f"in_{name}", v.shape, mybir.dt.from_np(v.dtype), kind="ExternalInput").ap()
         for name, v in arrays.items()}
    out = nc.dram_tensor("out", (T, D), F32, kind="ExternalOutput").ap()
    program(nc, a, out)
    r = run_bass_kernel_spmd(nc, [{f"in_{name}": v for name, v in arrays.items()}], core_ids=[0])
    return r.results[0]["out"].reshape(B, S, D)
```

```python
from contextlib import ExitStack

import numpy as np
import concourse.bass as bass
from concourse import mybir

F32 = mybir.dt.float32
F32R = mybir.dt.float32r
BF16 = mybir.dt.bfloat16
I32 = mybir.dt.int32
U32 = mybir.dt.uint32
ALU = mybir.AluOpType
ACT = mybir.ActivationFunctionType
AX = mybir.AxisListType

P = 128
B, S, D = 4, 1024, 256
T = B * S
NT = T // P
TS = S // P
KD = D // P
LN_EPS = 1e-5

HEADS, DH = 16, 16
HG = 4
NG = HEADS // HG
GW = 3 * HG * DH
GQ = 2 * HG * DH
Q_PARTS = (0, 0, 1, 0, 2, 1)
K_PARTS = (0, 1, 0, 2, 0, 1)
NS = len(Q_PARTS)
MASKED = -1e30

INTER = 1024
E, FE, TOPK, CAP = 64, 96, 8, 128


START = 1


class Steps:

    def __init__(self, engine, sem):
        self.engine, self.sem = engine, sem

    def begin(self, base):
        self.base, self.n = base, 0

    def done(self, instruction):
        instruction.then_inc(self.sem, 1)
        self.n += 1

    def wait(self):
        self.engine.wait_ge(self.sem, START + self.base + self.n)

    def end(self, planned):
        assert self.n == planned, (self.n, planned)


def carry(nc, tile):
    nc.vector.memset(tile[:, 0:1], 0.0)


def carry_on_pool(nc, tile, column, carried, before):
    nc.gpsimd.wait_ge(carried, START + before)
    nc.gpsimd.tensor_tensor(tile[:, column:column + 1], tile[:, 0:1], tile[:, 0:1], ALU.mult).then_inc(carried, 1)


def allocators(nc, ctx, name):
    def sb(what, shape, dt):
        return ctx.enter_context(nc.sbuf_tensor(f"{name}_{what}", shape, dt))

    def pb(what, shape, dt):
        return ctx.enter_context(nc.psum_tensor(f"{name}_{what}", shape, dt))

    used, at_zero = [], []

    def sem(what, from_zero=False):
        used.append(nc.alloc_semaphore(f"{name}_{what}"))
        if from_zero:
            at_zero.append(used[-1])
        return used[-1]

    def release():
        if used:
            nc.clear_and_free_semaphores(used)
            nc.all_engine_barrier()

    ctx.callback(release)

    def start():
        engines = (nc.gpsimd, nc.scalar, nc.vector, nc.sync, nc.tensor)
        for n, s in enumerate(s for s in used if s not in at_zero):
            engines[n % len(engines)].sem_inc(s, START)
        nc.all_engine_barrier()
        return ctx.enter_context(nc.Block())

    return sb, pb, sem, start




HEAD_CHUNKS = [(qt, c, 512 * c, min(512, 128 * (qt + 1) - 512 * c), 128 * (qt + 1) <= 512 * (c + 1))
               for qt in range(TS) for c in range(2) if 512 * c < 128 * (qt + 1)]
NCH = len(HEAD_CHUNKS)
STEPS = [(kt, h, c) for kt in range(TS) for h in range(HG) for c in range(kt // 4, 2)]
NSTEPS = len(STEPS)
ENDS = [1 + max(n for n, s in enumerate(STEPS) if s[0] == kt) for kt in range(TS)]
PRODUCTS = {ENDS[kp] + 1 + 2 * c: (kp, c) for kp in range(TS - 1) for c in range(kp // 4, 2)}
SIDE = 4


def side_schedule(g, first, last, qkv_at):
    steps = [[] for _ in range(NSTEPS)]
    if not (last and g == NG - 1):
        for j in range(2 * HG):
            steps[ST_AT[j]].append(("ST", j))
    if g == 2 and not last:
        for r in range(4):
            steps[1 + 2 * r].append(("HT", r))
    for r in range(2):
        steps[5 + r].append(("PAD" if first and g == 0 else "O", r))
    if g == 0 and not first:
        for r in range(4):
            steps[11 + 2 * r].append(("AT", r))
            steps[22 + 3 * r].append(("Y", r))
    if not (last and g >= 2):
        for r in range(4):
            steps[qkv_at[r]].append(("QKV", r))
    if not (last and g == NG - 1):
        for i in range(HG * NCH):
            at = MX_FROM + i * (MX_TO - MX_FROM) // (HG * NCH)
            steps[at].append(("MX", i))
            if i % NCH == NCH - 1:
                steps[at + 4].insert(0, ("NM", i // NCH))
    return steps


QKV_AT = (9, 11, 13, 15)
QKV_AT_ROPE = (7, 8, 9, 10)
MX_FROM, MX_TO = 2, 41
ST_AT = (0, 1, 5, 8, 14, 17, 22, 26)


PROLOGUE = [("HT", r) for r in range(4)] + [("QKV", r) for r in range(4)] + [("ST", j) for j in range(2 * HG)] + \
           [("QKV", r) for r in range(4)] + [u for h in range(HG) for u in [("MX", NCH * h + i) for i in range(NCH)] + [("NM", h)]]
EPILOGUE = [("O", 0), ("O", 1)] + [("AT", r) for r in range(4)] + [("Y", r) for r in range(4)]
READ_BY_SCALAR = lambda kind, index: kind in ("HT", "QKV", "AT", "PAD") or (kind in ("ST", "NM") and index % 2 == 0)


def units_of(first, last):
    return sum(len(s) for g in range(NG) for s in side_schedule(g, first, last, QKV_AT))


class Side:

    def __init__(self, filled, read):
        self.filled, self.read = filled, read

    def begin(self, turns):
        self.turns, self.k = turns, 0

    def bank_free(self, engine):
        engine.wait_ge(self.read[self.k % SIDE], START + self.turns + self.k // SIDE)

    def is_filled(self, engine):
        engine.wait_ge(self.filled, START + self.turns * SIDE + self.k + 1)

    def units_read(self, engine, units):
        last = {k % SIDE: k for k in sorted(units)}
        for i, k in last.items():
            if i != self.k % SIDE:
                engine.wait_ge(self.read[i], START + self.turns + k // SIDE + 1)

    def all_read(self, engine):
        for i in range(SIDE):
            engine.wait_ge(self.read[i], START + self.turns + (self.k + SIDE - 1 - i) // SIDE)


def attention_layer(nc, name, x_res, consts, wqkv_dram, wout_dram, rope_dram):
    ident, ident_b, causal_q, causal_k = (consts[k] for k in ("ident", "ident_b", "causal_q", "causal_k"))
    rope = rope_dram is not None
    qkv_at = QKV_AT_ROPE if rope else QKV_AT
    with ExitStack() as ctx:
        sb, pb, sem, start = allocators(nc, ctx, name)
        w_qkv = sb("w_qkv", [P, KD, NG * GW], F32)
        w_out = sb("w_out", [P, KD, D], F32)
        if rope:
            cos_t = sb("cos_t", [P, TS, GQ], F32)
            sin_t = sb("sin_t", [P, TS, GQ], F32)
            rot_a = sb("rot_a", [P, TS, GQ], F32)
            rot_b = sb("rot_b", [P, TS, GQ], F32)
            qk = sb("qk", [P, TS, GQ], F32)
        waits_v = sb("waits_v", [P, 2], F32)
        ones = sb("ones", [P, 1], F32)
        pad = sb("pad", [P, 2], F32)
        h_tok = sb("h_tok", [P, TS, D], F32)
        hT = sb("hT", [P, KD, S], F32)
        aT = sb("aT", [P, KD, S], F32)
        stats = sb("stats", [P, TS, 6], F32)
        mv = sb("mv", [P, TS, 2], F32)
        rstd = sb("rstd", [P, 3, TS], F32)
        qkv = sb("qkv", [P, TS, GW], F32)
        part = sb("part", [P, 3, TS, GQ], BF16)
        rest = sb("rest", [P, TS, GQ], F32)
        q_stack = sb("q_stack", [P, TS, HG, NS, DH], BF16)
        k_stack = sb("k_stack", [P, TS, HG, NS, DH], BF16)
        qsT = sb("qsT", [P, 2, HG, S], BF16)
        ksT = sb("ksT", [P, 2, HG, S], BF16)
        v_aug = sb("v_aug", [P, 2, TS, HG, 32], F32)
        m_part = sb("m_part", [P, TS, 2], F32)
        m_neg = sb("m_neg", [P, 2, TS], F32)
        m_split = sb("m_split", [P, HG, TS, 3], BF16)
        probs = sb("probs", [P, 2, HG, S], F32)
        oT = sb("oT", [P, S], F32)
        rsum = sb("rsum", [P, TS, HG], F32)
        attn = sb("attn", [P, TS, D], F32)
        ps_s = [pb(f"ps_s{i}", [P, 512], F32) for i in range(2)]
        ps_o = pb("ps_o", [P, 1024], F32)
        ps_a = [pb(f"ps_a{i}", [P, 512], F32) for i in range(SIDE)]

        w_in = sem("w_in")
        ones_set = sem("ones_set")
        dve, pool_steps = sem("dve"), sem("pool_steps")
        side_filled = sem("side_filled")
        side_read = [sem(f"side_read{i}") for i in range(SIDE)]
        var_ready, std_ready, h_ready = sem("var_ready"), sem("std_ready"), sem("h_ready")
        v_ready, stack_ready, nm_ready = sem("v_ready"), sem("stack_ready"), sem("nm_ready")
        s_psum, p_ready, pv_done, oT_ready = sem("s_psum"), sem("p_ready"), sem("pv_done"), sem("oT_ready")
        NIT = B * NG

        DVE_LN, DVE_MAX, DVE_O = 2 * TS + 1, 6 * HG, 2
        POOL_IT = 5 + (5 if rope else 0)
        n_pro, n_first, n_mid = len(PROLOGUE), units_of(True, False), units_of(False, False)
        n_last = units_of(False, True)
        dve_pro, dve_first, dve_mid = DVE_LN + POOL_IT + DVE_MAX, DVE_LN + NG * DVE_MAX + (NG - 1) * DVE_O, DVE_LN + NG * (DVE_MAX + DVE_O)
        dve_last = (NG - 1) * DVE_MAX + NG * DVE_O
        assert not (n_pro % SIDE or n_first % SIDE or n_mid % SIDE or n_last % SIDE), (n_pro, n_first, n_mid, n_last)
        block = start()

        def sequences(engine, side, prologue, iteration, epilogue, before=lambda b, first, last: None):
            side.begin(0)
            prologue()
            for first, last in ((True, False), (False, False), (False, True)):
                if first or last:
                    b = 0 if first else B - 1
                    side.begin((n_pro + (0 if first else n_first + n_mid * (B - 2))) // SIDE)
                    before(b, first, last)
                    for g in range(NG):
                        iteration(b, g, first, last)
                else:
                    with engine.Fori(1, B - 1) as b:
                        side.begin((n_pro + n_first - n_mid) // SIDE + b * (n_mid // SIDE))
                        before(b, first, last)
                        for g in range(NG):
                            iteration(b, g, first, last)
            side.begin((n_pro + n_first + n_mid * (B - 2) + n_last) // SIDE)
            epilogue()

        def prepare(ops, copy, step, stacks_free):
            if rope:
                two = lambda ap: ap.rearrange("p t (n two) -> p t n two", two=2)
                src, sn, ra, rb, qq = two(qkv[:, :, 0:GQ]), two(sin_t[:]), two(rot_a[:]), two(rot_b[:]), two(qk[:])
                step.done(ops.tensor_tensor(rot_a[:], qkv[:, :, 0:GQ], cos_t[:], ALU.mult))
                step.done(ops.tensor_tensor(rb[:, :, :, 0], src[:, :, :, 1], sn[:, :, :, 0], ALU.mult))
                step.done(ops.tensor_tensor(rb[:, :, :, 1], src[:, :, :, 0], sn[:, :, :, 1], ALU.mult))
                step.wait()
                step.done(ops.tensor_tensor(qq[:, :, :, 0], ra[:, :, :, 0], rb[:, :, :, 0], ALU.subtract))
                step.done(ops.tensor_tensor(qq[:, :, :, 1], ra[:, :, :, 1], rb[:, :, :, 1], ALU.add))
                step.wait()
            src = qk[:] if rope else qkv[:, :, 0:GQ]
            step.done(copy(part[:, 0], src))
            step.wait()
            step.done(ops.tensor_tensor(rest[:], src, part[:, 0], ALU.subtract))
            step.wait()
            step.done(copy(part[:, 1], rest[:]))
            step.wait()
            step.done(ops.tensor_tensor(rest[:], rest[:], part[:, 1], ALU.subtract))
            step.wait()
            step.done(copy(part[:, 2], rest[:]))
            step.wait()
            stacks_free()
            for stack, order, o in ((q_stack, Q_PARTS, 0), (k_stack, K_PARTS, HG * DH)):
                for s in range(NS):
                    to = stack[:, :, :, s, :]
                    of = part[:, order[s], :, o:o + HG * DH].rearrange("p t (h d) -> p t h d", h=HG)
                    ins = copy(to, of)
            ins.then_inc(stack_ready, 1)

        @block.sync
        def _(sp):
            sp.dma_start(w_qkv[:], wqkv_dram.rearrange("(k p) n -> p k n", p=P)).then_inc(w_in, 16)
            sp.dma_start(w_out[:], wout_dram.rearrange("(k p) n -> p k n", p=P)).then_inc(w_in, 16)
            if rope:
                sp.dma_start(cos_t[:], rope_dram[0].rearrange("(t p) n -> p t n", p=P)).then_inc(w_in, 16)
                sp.dma_start(sin_t[:], rope_dram[1].rearrange("(t p) n -> p t n", p=P)).then_inc(w_in, 16)
        LOADED = 64 if rope else 32

        @block.gpsimd
        def _(pool):
            side, step = Side(side_filled, side_read), Steps(pool, pool_steps)

            def copy(out, in_):
                one = ones[:, 0:1]
                for _ in range(len(in_.shape) - 2):
                    one = one.unsqueeze(1)
                return nc.gpsimd.tensor_tensor(out, in_, one.to_broadcast(list(in_.shape)), ALU.mult)

            def prepare_next(before, stacks_free):
                step.begin(POOL_IT * before)
                prepare(nc.gpsimd, copy, step, stacks_free)
                step.end(POOL_IT)

            def take_v(it, par):
                pool.wait_ge(pv_done, START + TS * (max(it - 1, 0) if isinstance(it, int) else it - 1))
                copy(v_aug[:, par, :, :, 0:DH], qkv[:, :, GQ:GW].rearrange("p t (h d) -> p t h d", h=HG)).then_inc(v_ready, 1)

            def prologue():
                for kind, index in PROLOGUE:
                    side.k += 1
                    if (kind, index) == ("QKV", 3):
                        side.all_read(pool)
                        if side.k == 8:
                            take_v(0, 0)
                        else:
                            pool.wait_ge(stack_ready, START + 1)
                            prepare_next(0, lambda: pool.wait_ge(side_filled, START + 16))

            def iteration(b, g, first, last):
                it = b * NG + g
                units = [u for s in side_schedule(g, first, last, qkv_at) for u in s]
                if not (last and g == NG - 1):
                    take_v(it + 1, (g + 1) % 2)
                k0 = side.k
                if ("QKV", 3) in units:
                    side.k = k0 + units.index(("QKV", 3)) + 1
                    side.all_read(pool)
                    side.k = k0 + units.index(("ST", 2 * HG - 1))
                    prepare_next(it + 1, lambda: side.is_filled(pool))
                side.k = k0 + len(units)

            nc.gpsimd.memset(v_aug[:], 1.0).then_inc(ones_set, 1)
            nc.gpsimd.memset(ones[:], 1.0).then_inc(ones_set, 1)
            pool.wait_ge(ones_set, START + 3)
            pool.wait_ge(w_in, START + LOADED)
            sequences(pool, side, prologue, iteration, lambda: None)

        @block.tensor
        def _(pe):
            side = Side(side_filled, side_read)

            at = {}
            needs = {"QKV": ("HT", 3), "AT": ("O", 1), "Y": ("AT", 3)}

            def unit(kind, index, it, b, par):
                bank = ps_a[side.k % SIDE]
                r = index
                at[(kind, index)] = side.k
                if kind == "HT" and r >= 0:
                    pe.wait_ge(h_ready, START + 4 * b + r + 1)
                elif kind == "ST" and index == 0:
                    pe.wait_ge(stack_ready, START + it + 1)
                elif kind == "NM":
                    pe.wait_ge(nm_ready, START + HG * it + index + 1)
                elif kind == "O":
                    pe.wait_ge(oT_ready, START + it)
                elif kind == "MX" and index % NCH == 0:
                    side.units_read(pe, [at[("ST", 2 * (index // NCH) + n)] for n in range(2)])
                elif r == 0 and needs.get(kind) in at:
                    side.units_read(pe, [at[(needs[kind][0], n)] for n in range(needs[kind][1] + 1)])
                side.bank_free(pe)
                if kind in ("HT", "AT"):
                    src = h_tok if kind == "HT" else attn
                    for k in range(KD):
                        for tl in range(2):
                            mm = nc.tensor.transpose(bank[:, 256 * k + 128 * tl:256 * k + 128 * tl + 128],
                                                     src[:, 2 * r + tl, 128 * k:128 * k + 128], ident[:])
                elif kind == "QKV":
                    for tl in range(2):
                        t = 2 * r + tl
                        for k in range(KD):
                            mm = nc.tensor.matmul(bank[:, GW * tl:GW * tl + GW], hT[:, k, 128 * t:128 * t + 128],
                                                  w_qkv[:, k, qkv_columns[0]], start=(k == 0), stop=(k == KD - 1))
                elif kind == "ST":
                    stack, h = (q_stack, k_stack)[index % 2], index // 2
                    for t in range(TS):
                        mm = nc.tensor.transpose(bank[:].bitcast(BF16)[0:96, 128 * t:128 * t + 128],
                                                 stack[:, t, h].rearrange("p s d -> p (s d)"), ident_b[:])
                elif kind == "MX":
                    h, (qt, c, k0, kn, diag) = index // NCH, HEAD_CHUNKS[index % NCH]
                    mm = nc.tensor.matmul(bank[:, 0:kn], qsT[0:96, par, h, 128 * qt:128 * qt + 128],
                                          ksT[0:96, par, h, k0:k0 + kn], start=True, stop=not diag)
                    if diag:
                        mm = nc.tensor.matmul(bank[:, kn - 128:kn], ident_b[:], causal_q[:], start=False, stop=True)
                elif kind == "NM":
                    for t in range(TS):
                        mm = nc.tensor.transpose(bank[:].bitcast(BF16)[96:99, 128 * t:128 * t + 128],
                                                 m_split[:, index, t, :], ident_b[:])
                elif kind == "O":
                    for t in range(4):
                        q0 = 512 * r + 128 * t
                        mm = nc.tensor.transpose(bank[:, 128 * t:128 * t + 128], oT[:, q0:q0 + 128], ident[:])
                elif kind == "Y":
                    for tl in range(2):
                        t = 2 * r + tl
                        for k in range(KD):
                            mm = nc.tensor.matmul(bank[:, D * tl:D * tl + D], aT[:, k, 128 * t:128 * t + 128],
                                                  w_out[:, k, :], start=(k == 0), stop=(k == KD - 1))
                else:
                    mm = nc.tensor.matmul(bank[:, 0:128], ident_b[:], ident_b[:], start=True, stop=True)
                mm.then_inc(side_filled, 1)
                side.k += 1

            qkv_columns = [None]

            def prologue():
                for n, (kind, index) in enumerate(PROLOGUE):
                    qkv_columns[0] = slice(0, GW) if n < 8 else slice(GW, 2 * GW)
                    unit(kind, index, 0, 0, 0)

            def scores(it, par, n):
                kt, h, c = STEPS[n]
                if n >= 2:
                    pe.wait_ge(p_ready, START + NSTEPS * it + n - 1)
                q0, q1 = max(512 * c, 128 * kt), 512 * (c + 1)
                diag, bank = q0 == 128 * kt, ps_s[n % 2]
                mm = nc.tensor.matmul(bank[:, q0 - 512 * c:512], ksT[0:99, par, h, 128 * kt:128 * kt + 128],
                                      qsT[0:99, par, h, q0:q1], start=True, stop=not diag)
                if diag:
                    mm = nc.tensor.matmul(bank[:, q0 - 512 * c:q0 - 512 * c + 128], ident_b[:], causal_k[:], start=False, stop=True)
                mm.then_inc(s_psum, 1)

            def products(it, par, kp, c):
                pe.wait_ge(p_ready, START + NSTEPS * it + ENDS[kp])
                if kp == 0:
                    pe.wait_ge(v_ready, START + it + 1)
                    pe.wait_ge(oT_ready, START + it)
                q0, q1 = max(512 * c, 128 * kp), 512 * (c + 1)
                for h in range(HG):
                    mm = nc.tensor.matmul(ps_o[32 * h:32 * h + 32, q0:q1], v_aug[:, par, kp, h, :],
                                          probs[:, kp % 2, h, q0:q1], start=(kp == 0), stop=(kp == 4 * c + 3))
                if c == 1:
                    mm.then_inc(pv_done, 1)

            def iteration(b, g, first, last):
                it = b * NG + g
                steps = side_schedule(g, first, last, qkv_at)
                g2 = (g + 2) % NG
                qkv_columns[0] = slice(g2 * GW, g2 * GW + GW)
                side.all_read(pe)
                at.clear()
                scores(it, g % 2, 0)
                for n in range(NSTEPS):
                    if n + 1 < NSTEPS:
                        scores(it, g % 2, n + 1)
                    for kind, index in steps[n]:
                        if kind in ("ST", "NM"):
                            unit(kind, index, it + 1, b, (g + 1) % 2)
                        elif kind == "HT":
                            unit(kind, index, it, b + 1, None)
                        else:
                            unit(kind, index, it, b, (g + 1) % 2)
                    if n in PRODUCTS:
                        products(it, g % 2, *PRODUCTS[n])
                products(it, g % 2, TS - 1, 1)

            pe.wait_ge(w_in, START + LOADED)
            pe.wait_ge(ones_set, START + 3)
            sequences(pe, side, prologue, iteration,
                      lambda: [at.clear()] + [unit(kind, index, NIT, B, None) for kind, index in EPILOGUE])

        @block.scalar
        def _(act):
            side = Side(side_filled, side_read)

            def read(kind, index, par):
                bank = ps_a[side.k % SIDE]
                if READ_BY_SCALAR(kind, index):
                    side.is_filled(act)
                    if kind in ("HT", "AT"):
                        ins = nc.scalar.copy((hT if kind == "HT" else aT)[:, :, 256 * index:256 * index + 256],
                                             bank[:].rearrange("p (k n) -> p k n", k=KD))
                    elif kind == "QKV":
                        ins = nc.scalar.copy(qkv[:, 2 * index:2 * index + 2, :], bank[:, 0:2 * GW].rearrange("p (t n) -> p t n", t=2))
                    elif kind == "ST":
                        ins = nc.scalar.copy(qsT[0:96, par, index // 2, :], bank[:].bitcast(BF16)[0:96, :])
                    elif kind == "PAD":
                        ins = nc.scalar.copy(pad[:, index:index + 1], bank[:, 0:1])
                    else:
                        ins = nc.scalar.copy(qsT[96:99, par, index, :], bank[:].bitcast(BF16)[96:99, :])
                    ins.then_inc(side_read[side.k % SIDE], 1)
                side.k += 1

            def root():
                nc.scalar.activation(rstd[:, 1], rstd[:, 0], ACT.Sqrt).then_inc(std_ready, 1)

            def prologue():
                act.wait_ge(var_ready, START + 1)
                root()
                for n, (kind, index) in enumerate(PROLOGUE):
                    if (kind, index) == ("QKV", 0) and n > 8:
                        act.wait_ge(v_ready, START + 1)
                        act.wait_ge(stack_ready, START + 1)
                    read(kind, index, 0)

            def iteration(b, g, first, last):
                it = b * NG + g
                steps = side_schedule(g, first, last, qkv_at)
                for n, (kt, h, c) in enumerate(STEPS):
                    act.wait_ge(s_psum, START + NSTEPS * it + n + 1)
                    if h == 0:
                        act.wait_ge(pv_done, START + TS * it + (kt - 1 if kt >= 2 else 0))
                    q0, q1 = max(512 * c, 128 * kt), 512 * (c + 1)
                    nc.scalar.activation(probs[:, kt % 2, h, q0:q1], ps_s[n % 2][:, q0 - 512 * c:512], ACT.Exp,
                                         scale=DH ** -0.5).then_inc(p_ready, 1)
                    if n == 2 and not (first and g == 0):
                        act.wait_ge(pv_done, START + TS * it)
                        nc.scalar.copy(oT[:], ps_o[:]).then_inc(oT_ready, 1)
                    if n == 12 and g == 1 and not last:
                        act.wait_ge(var_ready, START + b + 2)
                        root()
                    for kind, index in steps[n]:
                        if (kind, index) == ("QKV", 0):
                            act.wait_ge(v_ready, START + it + 2)
                            act.wait_ge(stack_ready, START + it + 2)
                        read(kind, index, (g + 1) % 2)

            def epilogue():
                act.wait_ge(pv_done, START + TS * NIT)
                nc.scalar.copy(oT[:], ps_o[:]).then_inc(oT_ready, 1)
                for kind, index in EPILOGUE:
                    read(kind, index, None)

            sequences(act, side, prologue, iteration, epilogue)

        @block.vector
        def _(v):
            side, step = Side(side_filled, side_read), Steps(v, dve)

            def statistics(b):
                for t in range(TS):
                    step.done(nc.vector.bn_stats(stats[:, t, :], one_tile(x_res, b * TS + t)))
                step.wait()
                carry(nc, waits_v)
                for t in range(TS):
                    step.done(nc.vector.bn_aggr(mv[:, t, :], stats[:, t, :]))
                step.wait()
                nc.vector.tensor_scalar(rstd[:, 0], mv[:, :, 1], LN_EPS, None, ALU.add).then_inc(var_ready, 1)

            def normalize(b):
                v.wait_ge(std_ready, START + b + 1)
                step.done(nc.vector.reciprocal(rstd[:, 2], rstd[:, 1]))
                step.wait()
                for t in range(TS):
                    ins = nc.vector.tensor_scalar(h_tok[:, t, :], one_tile(x_res, b * TS + t), mv[:, t, 0:1], rstd[:, 2, t:t + 1],
                                                  ALU.subtract, ALU.mult)
                    if t % 2 == 1:
                        ins.then_inc(h_ready, 1)

            def read(kind, index, b, g):
                bank = ps_a[side.k % SIDE]
                mine = side_read[side.k % SIDE]
                if not READ_BY_SCALAR(kind, index):
                    side.is_filled(v)
                    if kind == "MX":
                        qt, c, k0, kn, diag = HEAD_CHUNKS[index % NCH]
                        nc.vector.tensor_reduce(m_part[:, qt, c:c + 1], bank[:, 0:kn], AX.X, ALU.max, negate=False).then_inc(mine, 1)
                    elif kind == "ST":
                        nc.vector.tensor_copy(ksT[0:96, (g + 1) % 2, index // 2, :], bank[:].bitcast(BF16)[0:96, :]).then_inc(mine, 1)
                    elif kind == "NM":
                        nc.vector.tensor_copy(qsT[96:99, (g + 1) % 2, index, :], bank[:].bitcast(BF16)[96:99, :]).then_inc(mine, 1)
                    elif kind == "O":
                        o_tok = bank[:].rearrange("p (t h e) -> p t h e", t=4, h=HG)
                        rs = rsum[:, 4 * index:4 * index + 4, :]
                        step.done(nc.vector.reciprocal(rs, o_tok[:, :, :, DH]))
                        step.wait()
                        gp = (g - 1) % NG
                        nc.vector.tensor_tensor(attn[:, 4 * index:4 * index + 4, gp * HG * DH:(gp + 1) * HG * DH]
                                                .rearrange("p t (h d) -> p t h d", h=HG), o_tok[:, :, :, 0:DH],
                                                rs.unsqueeze(3).to_broadcast([P, 4, HG, DH]), ALU.mult).then_inc(mine, 1)
                    else:
                        xs = x_res[:, bass.ds((b - 1) * TS + 2 * index, 2), :]
                        nc.vector.tensor_tensor(xs, xs, bank[:].rearrange("p (t n) -> p t n", t=2), ALU.add).then_inc(mine, 1)
                side.k += 1
                if kind == "MX" and index % NCH == NCH - 1:
                    h = index // NCH
                    side.all_read(v)
                    step.done(nc.vector.tensor_scalar(m_neg[:, 0, 0:4], m_part[:, 0:4, 0], -1.0, None, ALU.mult))
                    step.done(nc.vector.tensor_tensor(m_part[:, 4:8, 0], m_part[:, 4:8, 0], m_part[:, 4:8, 1], ALU.max))
                    step.wait()
                    step.done(nc.vector.tensor_scalar(m_neg[:, 0, 4:8], m_part[:, 4:8, 0], -1.0, None, ALU.mult))
                    step.wait()
                    step.done(nc.vector.tensor_copy(m_split[:, h, :, 0], m_neg[:, 0]))
                    step.wait()
                    step.done(nc.vector.tensor_tensor(m_neg[:, 1], m_neg[:, 0], m_split[:, h, :, 0], ALU.subtract))
                    step.wait()
                    step.done(nc.vector.tensor_copy(m_split[:, h, :, 1], m_neg[:, 1]))
                    step.wait()
                    nc.vector.tensor_tensor(m_split[:, h, :, 2], m_neg[:, 1], m_split[:, h, :, 1], ALU.subtract).then_inc(nm_ready, 1)

            def prologue():
                step.begin(0)
                statistics(0)
                normalize(0)
                for n, (kind, index) in enumerate(PROLOGUE):
                    if n == 8:
                        side.all_read(v)
                        v.wait_ge(w_in, START + LOADED)
                        prepare(nc.vector, nc.vector.tensor_copy, step, lambda: None)
                    read(kind, index, 0, -1)
                step.end(dve_pro)

            def before(b, first, last):
                step.begin(dve_pro + (0 if first else dve_first + dve_mid * (b - 1)))

            def iteration(b, g, first, last):
                steps = side_schedule(g, first, last, qkv_at)
                for n in range(NSTEPS):
                    if g == 1 and not last:
                        if n == 0:
                            statistics(b + 1)
                        elif n == 16:
                            normalize(b + 1)
                    for kind, index in steps[n]:
                        read(kind, index, b, g)
                if g == NG - 1:
                    step.end(dve_first if first else dve_last if last else dve_mid)

            def epilogue():
                step.begin(dve_pro + dve_first + dve_mid * (B - 2) + dve_last)
                for kind, index in EPILOGUE:
                    read(kind, index, B, NG)
                side.all_read(v)

            nc.vector.memset(ksT[96:99, :, :, :], 1.0).then_inc(ones_set, 1)
            sequences(v, side, prologue, iteration, epilogue, before)


def mlp_weights(nc, w_ug, w_dn, wug_dram, wdn_dram, had_dram, su_dram, scale_ug, su_dp, scale_dp):
    KI = INTER // P
    with ExitStack() as ctx:
        sb, pb, sem, start = allocators(nc, ctx, "fold")
        raw_ug = sb("raw_ug", [P, KD, 2 * INTER], F32)
        raw_dn = sb("raw_dn", [P, KI, D], F32)
        had = sb("had", [P, 4, P], F32)
        su_u = sb("su_u", [P, KD], F32)
        su_d = sb("su_d", [P, KI], F32)
        sc_u = sb("sc_u", [P, 2 * INTER], F32)
        sc_d = sb("sc_d", [P, D], F32)
        ps = [pb(f"ps{i}", [P, 512], F32) for i in range(2)]
        landed, folded, scaled = sem("landed"), sem("folded"), sem("scaled")
        block = start()
        NLOAD = 7
        jobs = []
        for a1 in range(KD):
            for c in range(4):
                jobs.append((w_ug[:, a1, 512 * c:512 * c + 512], su_u[:, a1:a1 + 1], sc_u[:, 512 * c:512 * c + 512],
                             [((a0 & a1) % 2, raw_ug[:, a0, 512 * c:512 * c + 512]) for a0 in range(KD)]))
        for c1 in range(KI):
            jobs.append((w_dn[:, c1, :], su_d[:, c1:c1 + 1], sc_d[:],
                         [(2 + bin(c0 & c1).count("1") % 2, raw_dn[:, c0, :]) for c0 in range(KI)]))

        @block.sync
        def _(sp):
            sp.dma_start(had[:], had_dram.rearrange("m p n -> p m n")).then_inc(landed, 16)
            sp.dma_start(raw_ug[:], wug_dram.rearrange("(k p) n -> p k n", p=P)).then_inc(landed, 16)
            sp.dma_start(su_u[:], su_dram).then_inc(landed, 16)
            sp.dma_start(sc_u[:], scale_ug.partition_broadcast(P)).then_inc(landed, 16)
            sp.dma_start(raw_dn[:], wdn_dram.rearrange("(k p) n -> p k n", p=P)).then_inc(landed, 16)
            sp.dma_start(su_d[:], su_dp).then_inc(landed, 16)
            sp.dma_start(sc_d[:], scale_dp.partition_broadcast(P)).then_inc(landed, 16)

        @block.tensor
        def _(pe):
            pe.wait_ge(landed, START + 16 * NLOAD)
            for n, (dst, _, _, products) in enumerate(jobs):
                if n >= 2:
                    pe.wait_ge(scaled, START + n - 1)
                width = dst.shape[-1]
                for i, (which, moving) in enumerate(products):
                    mm = nc.tensor.matmul(ps[n % 2][:, 0:width], had[:, which, :], moving, start=(i == 0),
                                          stop=(i == len(products) - 1))
                mm.then_inc(folded, 1)

        @block.vector
        def _(v):
            v.wait_ge(landed, START + 16 * NLOAD)
            for n, (dst, sign, scale, _) in enumerate(jobs):
                v.wait_ge(folded, START + n + 1)
                nc.vector.scalar_tensor_tensor(dst, ps[n % 2][:, 0:dst.shape[-1]], sign, scale, ALU.mult, ALU.mult)\
                  .then_inc(scaled, 1)
            v.wait_ge(scaled, START + len(jobs))


def mlp_layer(nc, name, x_res, consts, w_ug, w_dn):
    ident = consts["ident"]
    CT = 4
    NC = NT // CT
    CW = CT * P
    KI = INTER // P
    with ExitStack() as ctx:
        sb, pb, sem, start = allocators(nc, ctx, name)
        stats = sb("stats", [P, NT, 6], F32)
        mv = sb("mv", [P, NT, 2], F32)
        rstd = sb("rstd", [P, 3, NT], F32)
        h_tok = sb("h_tok", [P, CT, D], F32)
        hT = [sb(f"hT_{part}", [P, KD, CW], F32R) for part in ("hi", "lo")]
        ug = [sb(f"ug_{part}", [P, KD, 2 * INTER], F32R) for part in ("hi", "lo")]
        dn = [sb(f"dn_{part}", [P, KI, D], F32R) for part in ("hi", "lo")]
        gated = sb("gated", [P, 2, CW], F32)
        whole = sb("whole", [P, 2, CW], F32)
        mid = [sb(f"mid_{part}", [P, KI, CW], F32R) for part in ("hi", "lo")]
        ps_t = [pb(f"ps_t{i}", [P, 512], F32) for i in range(2)]
        ps_g = [pb(f"ps_g{i}", [P, 512], F32) for i in range(2)]
        ps_u = [pb(f"ps_u{i}", [P, 512], F32) for i in range(2)]
        ps_y = [pb(f"ps_y{i}", [P, 512], F32) for i in range(2)]
        dve = sem("dve")
        var_ready, std_ready = sem("var_ready"), sem("std_ready")
        h_ready, hT_psum, hT_ready = sem("h_ready"), sem("hT_psum"), sem("hT_ready")
        gu_psum, silu_ready, mid_ready = sem("gu_psum"), sem("silu_ready"), sem("mid_ready")
        w_hi, w_lo = sem("w_hi"), sem("w_lo")
        lo_ready, mid_hi, mid_lo = sem("lo_ready"), sem("mid_hi"), sem("mid_lo")
        y_psum, x_done = sem("y_psum"), sem("x_done")
        block = start()
        PIECES = [(w_ug[:, k, c:c + 512], ug[0][:, k, c:c + 512], ug[1][:, k, c:c + 512]) for c in range(0, 2 * INTER, 512) for k in range(KD)] + \
                 [(w_dn[:, j:j + 2, :], dn[0][:, j:j + 2, :], dn[1][:, j:j + 2, :]) for j in range(0, KI, 2)]

        @block.tensor
        def _(pe):
            def to_features(c):
                for r in range(2):
                    pe.wait_ge(h_ready, START + 2 * c + r + 1)
                    for k in range(KD):
                        for tl in range(2):
                            mm = nc.tensor.transpose(ps_t[r][:, 256 * k + 128 * tl:256 * k + 128 * tl + 128],
                                                     h_tok[:, 2 * r + tl, 128 * k:128 * k + 128], ident[:])
                    mm.then_inc(hT_psum, 1)

            def chunk(c, last):
                pe.wait_ge(lo_ready, START + 2 * c + 2)
                for j in range(KI):
                    if j >= 2:
                        pe.wait_ge(mid_ready, START + KI * c + j - 1)
                    for base, ps in ((0, ps_u), (INTER, ps_g)):
                        for k in range(KD):
                            mm = three(nc, ps[j % 2][:], [w[:, k, base + P * j:base + P * j + P] for w in ug], [h[:, k, :] for h in hT],
                                       k == 0, k == KD - 1)
                    mm.then_inc(gu_psum, 1)
                if not last:
                    to_features(c + 1)
                for t in range(CT):
                    if t == 0:
                        pe.wait_ge(x_done, START + 2 * c)
                    for j in range(KI):
                        if t == 0:
                            pe.wait_ge(mid_lo, START + KI * c + j + 1)
                        mm = three(nc, ps_y[t // 2][:, D * (t % 2):D * (t % 2) + D], [m[:, j, P * t:P * t + P] for m in mid],
                                   [w[:, j, :] for w in dn], j == 0, j == KI - 1)
                    if t % 2 == 1:
                        mm.then_inc(y_psum, 1)

            to_features(0)
            pe.wait_ge(w_lo, START + len(PIECES))
            with pe.Fori(0, NC - 1) as c:
                chunk(c, False)
            chunk(NC - 1, True)

        @block.gpsimd
        def _(pool):
            for n, (w, hi, lo) in enumerate(PIECES):
                pool.wait_ge(w_hi, START + n + 1)
                nc.gpsimd.tensor_tensor(lo, w, hi.bitcast(F32), ALU.subtract).then_inc(w_lo, 1)
            with pool.Fori(0, NC) as c:
                for j in range(KI):
                    pool.wait_ge(mid_hi, START + KI * c + j + 1)
                    if j == 0:
                        pool.wait_ge(y_psum, START + 2 * c)
                    nc.gpsimd.tensor_tensor(mid[1][:, j, :], whole[:, j % 2, :], mid[0][:, j, :].bitcast(F32), ALU.subtract)\
                      .then_inc(mid_lo, 1)

        @block.scalar
        def _(act):
            def to_features(c):
                for r in range(2):
                    act.wait_ge(hT_psum, START + 2 * c + r + 1)
                    if r == 0:
                        act.wait_ge(gu_psum, START + KI * c)
                    nc.scalar.copy(hT[0][:, :, 256 * r:256 * r + 256],
                                   ps_t[r][:].rearrange("p (k n) -> p k n", k=KD)).then_inc(hT_ready, 1)

            def middle_hi(c, j):
                act.wait_ge(mid_ready, START + KI * c + j + 1)
                if j == 0:
                    act.wait_ge(y_psum, START + 2 * c)
                nc.scalar.copy(mid[0][:, j, :], whole[:, j % 2, :]).then_inc(mid_hi, 1)

            def chunk(c, last):
                for j in range(KI):
                    act.wait_ge(gu_psum, START + KI * c + j + 1)
                    if j >= 2:
                        act.wait_ge(mid_ready, START + KI * c + j - 1)
                    else:
                        act.wait_ge(mid_ready, START + KI * c)
                    nc.scalar.activation(gated[:, j % 2, :], ps_g[j % 2][:], ACT.Silu).then_inc(silu_ready, 1)
                    if j >= 1:
                        middle_hi(c, j - 1)
                middle_hi(c, KI - 1)
                if not last:
                    to_features(c + 1)

            for w, hi, lo in PIECES:
                nc.scalar.copy(hi, w).then_inc(w_hi, 1)
            act.wait_ge(var_ready, START + 1)
            nc.scalar.activation(rstd[:, 1], rstd[:, 0], ACT.Sqrt).then_inc(std_ready, 1)
            to_features(0)
            with act.Fori(0, NC - 1) as c:
                chunk(c, False)
            chunk(NC - 1, True)

        @block.vector
        def _(v):
            layer_norm_statistics(nc, v, x_res, stats, mv, rstd, dve, var_ready, std_ready)

            def normalize(c):
                v.wait_ge(hT_psum, START + 2 * c)
                for t in range(CT):
                    tile = c * CT + t
                    ins = nc.vector.tensor_scalar(h_tok[:, t, :], one_tile(x_res, tile), mean_of(mv, tile), rstd_of(rstd, tile),
                                                  ALU.subtract, ALU.mult)
                    if t % 2 == 1:
                        ins.then_inc(h_ready, 1)

            def features_lo(c):
                for r in range(2):
                    v.wait_ge(hT_ready, START + 2 * c + r + 1)
                    if r == 0:
                        v.wait_ge(gu_psum, START + KI * c)
                    nc.vector.tensor_tensor(hT[1][:, :, 256 * r:256 * r + 256], ps_t[r][:].rearrange("p (k n) -> p k n", k=KD),
                                            hT[0][:, :, 256 * r:256 * r + 256].bitcast(F32), ALU.subtract).then_inc(lo_ready, 1)

            def chunk(c, last):
                if not last:
                    normalize(c + 1)
                for j in range(KI):
                    v.wait_ge(silu_ready, START + KI * c + j + 1)
                    v.wait_ge(mid_lo, START + KI * c + (j - 1 if j >= 2 else 0))
                    nc.vector.tensor_tensor(whole[:, j % 2, :], gated[:, j % 2, :], ps_u[j % 2][:], ALU.mult).then_inc(mid_ready, 1)
                if not last:
                    features_lo(c + 1)
                for r in range(2):
                    v.wait_ge(y_psum, START + 2 * c + r + 1)
                    xs = x_res[:, bass.ds(c * CT + 2 * r, 2), :]
                    nc.vector.tensor_tensor(xs, xs, ps_y[r][:].rearrange("p (t n) -> p t n", t=2), ALU.add).then_inc(x_done, 1)

            normalize(0)
            features_lo(0)
            with v.Fori(0, NC - 1) as c:
                chunk(c, False)
            chunk(NC - 1, True)


def one_tile(x, t):
    return x[:, bass.ds(t, 1), :].rearrange("p o d -> p (o d)")


def three(nc, out, still, moving, first, last):
    for n, (a, b) in enumerate(((0, 0), (1, 0), (0, 1))):
        mm = nc.tensor.matmul(out, still[a], moving[b], start=(first and n == 0), stop=(last and n == 2))
    return mm


def slice_of(x, t, n):
    return x[:, bass.ds(t, n), :]


def mean_of(mv, t):
    return mv[:, bass.ds(t, 1), 0:1].rearrange("p o d -> p (o d)")


def rstd_of(rstd, t):
    return rstd[:, 2, bass.ds(t, 1)]


def layer_norm_statistics(nc, v, x_res, stats, mv, rstd, dve, var_ready, std_ready):
    step = Steps(v, dve)
    PER = 8
    with v.Fori(0, NT // PER) as i:
        step.begin(PER * i)
        for t in range(PER):
            step.done(nc.vector.bn_stats(stats[:, bass.ds(PER * i + t, 1), :].rearrange("p o d -> p (o d)"), one_tile(x_res, PER * i + t)))
    step.begin(NT)
    step.wait()
    for t in range(NT):
        step.done(nc.vector.bn_aggr(mv[:, t, :], stats[:, t, :]))
    step.wait()
    nc.vector.tensor_scalar(rstd[:, 0], mv[:, :, 1], LN_EPS, None, ALU.add).then_inc(var_ready, 1)
    v.wait_ge(std_ready, START + 1)
    step.done(nc.vector.reciprocal(rstd[:, 2], rstd[:, 1]))
    step.wait()
    return step


def moe_layer(nc, name, x_res, consts, router_dram, gate_up_dram, down_dram, keyval_dram, slot_no_dram, rows_dram, sums_dram):
    ident = consts["ident"]
    GA = 4
    GT = 2 * GA
    NC = NT // GT
    ROW = D + E
    with ExitStack() as outer:
        slot_token = outer.enter_context(nc.sbuf_tensor(f"{name}_slot_token", [P, E], I32))

        with ExitStack() as ctx:
            sb, pb, sem, start = allocators(nc, ctx, name)
            stats = sb("stats", [P, NT, 6], F32)
            mv = sb("mv", [P, NT, 2], F32)
            rstd = sb("rstd", [P, 3, NT], F32)
            waits_v = sb("waits_v", [P, 2], F32)
            w_r = sb("w_r", [P, KD, E], F32)
            zeros = sb("zeros", [P, ROW], F32)
            rows = sb("rows", [P, 2, GT, ROW], F32)
            hT = sb("hT", [P, 2, 2, KD, P], F32)
            top = sb("top", [P, GT], F32)
            diff = sb("diff", [P, GT, E], F32)
            ex = sb("ex", [P, GT, E], F32)
            esum = sb("esum", [P, GT], F32)
            einv = sb("einv", [P, GT], F32)
            probs = sb("probs", [P, GT, E], F32)
            best = sb("best", [P, GT, TOPK], F32)
            left = sb("left", [P, GT, E], F32)
            mask = sb("mask", [P, GT, E], F32)
            wraw = sb("wraw", [P, GT, E], F32)
            wsum = sb("wsum", [P, GT], F32)
            winv = sb("winv", [P, GT], F32)
            keyval = sb("keyval", [P, T // 2], F32)
            keys = sb("keys", [P, T // 2], F32)
            first = sb("first", [P, CAP], F32)
            firstT = sb("firstT", [P, P], F32)
            both = sb("both", [E, 2 * CAP], F32)
            picked = sb("picked", [E, CAP], F32)
            empty = sb("empty", [P, E], F32)
            token_f = sb("token_f", [P, E], F32)
            slot_no = sb("slot_no", [P, 1], F32)
            ps_t = [pb(f"ps_t{i}", [P, 512], F32) for i in range(2)]
            ps_l = pb("ps_l", [P, 512], F32)
            ps_m = pb("ps_m", [P, 512], F32)
            landed, stored, rows_out, zeroed = sem("landed"), sem("stored"), sem("rows_out"), sem("zeroed")
            dve = sem("dve")
            var_ready, std_ready = sem("var_ready"), sem("std_ready")
            h_ready, hT_psum, hT_ready = sem("h_ready"), sem("hT_psum"), sem("hT_ready")
            logit_psum, diff_ready, ex_ready = sem("logit_psum"), sem("diff_ready"), sem("ex_ready")
            mask_ready, maskT_psum, key_done, w_ready = sem("mask_ready"), sem("maskT_psum"), sem("key_done"), sem("w_ready")
            first_ready, firstT_psum, firstT_ready, both_psum = sem("first_ready"), sem("firstT_psum"), sem("firstT_ready"), sem("both_psum")
            picked_ready, picked_psum, slots_ready = sem("picked_ready"), sem("picked_psum"), sem("slots_ready")
            block = start()
            OWN = 2 * GT + 7

            def by_half(t):
                return t.rearrange("p (a h) e -> p a h e", h=2)

            @block.sync
            def _(sp):
                sp.dma_start(w_r[:], router_dram.rearrange("(k p) e -> p k e", p=P)).then_inc(landed, 16)
                sp.dma_start(keyval[:], keyval_dram).then_inc(landed, 16)
                sp.dma_start(slot_no[:], slot_no_dram).then_inc(landed, 16)
                sp.dma_start(sums_dram[0][0:T, :].rearrange("(t p) d -> p t d", p=P), x_res[:]).then_inc(stored, 16)
                sp.wait_ge(zeroed, START + 1)
                sp.dma_start(rows_dram[T:T + P, :], zeros[:]).then_inc(stored, 16)
                sp.dma_start(sums_dram[0][T:T + P, :], zeros[:, 0:D]).then_inc(stored, 16)
                sp.dma_start(sums_dram[1].rearrange("(t p) d -> p t d", p=P),
                             zeros[:, 0:D].unsqueeze(1).to_broadcast([P, NT + 1, D])).then_inc(stored, 16)
                with sp.Fori(0, NC // 2) as i:
                    for par in range(2):
                        c = 2 * i + par
                        for half in range(2):
                            sp.wait_ge(w_ready, START + 2 * c + half + 1)
                            sp.dma_start(rows_dram[bass.ds((c * GA + NT // 2 * half) * P, GA * P), :].rearrange("(t p) r -> p t r", p=P),
                                         by_half(rows[:, par])[:, :, half, :]).then_inc(rows_out, 16)
                sp.wait_ge(rows_out, START + 32 * NC)
                sp.wait_ge(stored, START + 64)

            @block.tensor
            def _(pe):
                pe.wait_ge(landed, START + 48)

                def to_features(c, par, a):
                    n = GA * c + a
                    pe.wait_ge(h_ready, START + 2 * n + 2)
                    if a >= 2:
                        pe.wait_ge(hT_ready, START + n - 1)
                    else:
                        pe.wait_ge(hT_ready, START + GA * c)
                    for half in range(2):
                        for k in range(KD):
                            at = P * (KD * half + k)
                            mm = nc.tensor.transpose(ps_t[a % 2][:, at:at + P],
                                                     rows[:, par, 2 * a + half, P * k:P * k + P], ident[:])
                    mm.then_inc(hT_psum, 1)

                def logits(c, a):
                    pe.wait_ge(hT_ready, START + GA * c + a + 1)
                    if a == 0:
                        pe.wait_ge(diff_ready, START + c)
                    for half in range(2):
                        for k in range(KD):
                            at = E * (2 * a + half)
                            mm = nc.tensor.matmul(ps_l[:, at:at + E], hT[:, a % 2, half, k, :], w_r[:, k, :],
                                                  start=(k == 0), stop=(k == KD - 1))
                    mm.then_inc(logit_psum, 1)

                def group(c, par):
                    for a in range(GA):
                        to_features(c, par, a)
                        if a >= 1:
                            logits(c, a - 1)
                    logits(c, GA - 1)

                def masks(c):
                    pe.wait_ge(mask_ready, START + c + 1)
                    pe.wait_ge(key_done, START + c)
                    for a in range(GA):
                        mm = nc.tensor.transpose(ps_m[:, P * a:P * a + P], mask[:, 2 * a:2 * a + 2, :].rearrange("p h e -> p (h e)"), ident[:])
                    mm.then_inc(maskT_psum, 1)

                with pe.Fori(0, NC // 2) as i:
                    group(2 * i, 0)
                    group(2 * i + 1, 1)
                    masks(2 * i)
                    masks(2 * i + 1)
                pe.wait_ge(first_ready, START + 1)
                nc.tensor.transpose(ps_t[0][:, 0:P], first[:], ident[:]).then_inc(firstT_psum, 1)
                pe.wait_ge(firstT_ready, START + 1)
                for half in range(2):
                    mm = nc.tensor.transpose(ps_t[1][0:E, CAP * half:CAP * half + CAP], firstT[:, E * half:E * half + E], ident[:])
                mm.then_inc(both_psum, 1)
                pe.wait_ge(picked_ready, START + 1)
                nc.tensor.transpose(ps_l[:, 0:E], picked[:], ident[0:E, 0:E]).then_inc(picked_psum, 1)

            @block.scalar
            def _(act):
                act.wait_ge(var_ready, START + 1)
                nc.scalar.activation(rstd[:, 1], rstd[:, 0], ACT.Sqrt).then_inc(std_ready, 1)

                def to_features(c, a):
                    n = GA * c + a
                    act.wait_ge(hT_psum, START + n + 1)
                    act.wait_ge(logit_psum, START + (n - 1 if a >= 2 else GA * c))
                    nc.scalar.copy(hT[:, a % 2].rearrange("p h k n -> p (h k n)"), ps_t[a % 2][:]).then_inc(hT_ready, 1)

                def exponentials(c):
                    act.wait_ge(diff_ready, START + c + 1)
                    nc.scalar.activation(ex[:], diff[:], ACT.Exp).then_inc(ex_ready, 1)

                with act.Fori(0, NC // 2) as i:
                    for a in range(GA):
                        to_features(2 * i, a)
                    for a in range(GA):
                        if a == 2:
                            exponentials(2 * i)
                        to_features(2 * i + 1, a)
                    exponentials(2 * i + 1)

            @block.gpsimd
            def _(pool):
                nc.gpsimd.memset(zeros[:], 0.0).then_inc(zeroed, 1)

            @block.vector
            def _(v):
                v.wait_ge(landed, START + 48)
                layer_norm_statistics(nc, v, x_res, stats, mv, rstd, dve, var_ready, std_ready)
                step = Steps(v, dve)

                def normalize(c, par):
                    for a in range(GA):
                        for half in range(2):
                            tile = c * GA + a + NT // 2 * half
                            nc.vector.tensor_scalar(rows[:, par, 2 * a + half, 0:D], one_tile(x_res, tile),
                                                    mean_of(mv, tile), rstd_of(rstd, tile), ALU.subtract, ALU.mult).then_inc(h_ready, 1)

                def choose(c, par):
                    wide = lambda t: t.unsqueeze(2).to_broadcast([P, GT, E])
                    step.begin(2 * NT + 1 + OWN * c)
                    v.wait_ge(logit_psum, START + GA * c + GA)
                    logit = ps_l[:].rearrange("p (t e) -> p t e", e=E)
                    step.done(nc.vector.tensor_reduce(top[:], logit, AX.X, ALU.max))
                    step.wait()
                    nc.vector.tensor_tensor(diff[:], logit, wide(top[:]), ALU.subtract).then_inc(diff_ready, 1)
                    v.wait_ge(ex_ready, START + c + 1)
                    step.done(nc.vector.tensor_reduce(esum[:], ex[:], AX.X, ALU.add))
                    step.wait()
                    step.done(nc.vector.reciprocal(einv[:], esum[:]))
                    step.wait()
                    step.done(nc.vector.tensor_tensor(probs[:], ex[:], wide(einv[:]), ALU.mult))
                    step.wait()
                    carry(nc, waits_v)
                    for t in range(GT):
                        step.done(nc.vector.max(best[:, t, :], probs[:, t, :]))
                    step.wait()
                    carry(nc, waits_v)
                    for t in range(GT):
                        step.done(nc.vector.match_replace(left[:, t, :], best[:, t, :], probs[:, t, :], -1.0))
                    step.wait()
                    v.wait_ge(maskT_psum, START + c)
                    nc.vector.tensor_scalar(mask[:], left[:], 0.0, None, ALU.is_lt).then_inc(mask_ready, 1)
                    v.wait_ge(mask_ready, START + c + 1)
                    step.done(nc.vector.tensor_tensor(wraw[:], mask[:], probs[:], ALU.mult))
                    step.wait()
                    step.done(nc.vector.tensor_reduce(wsum[:], wraw[:], AX.X, ALU.add))
                    step.wait()
                    step.done(nc.vector.reciprocal(winv[:], wsum[:]))
                    step.wait()
                    for half in range(2):
                        nc.vector.tensor_tensor(by_half(rows[:, par])[:, :, half, D:ROW], by_half(wraw[:])[:, :, half, :],
                                                winv[:].rearrange("p (a h) -> p a h", h=2)[:, :, half].unsqueeze(2).to_broadcast([P, GA, E]),
                                                ALU.mult).then_inc(w_ready, 1)
                    v.wait_ge(maskT_psum, START + c + 1)
                    nc.vector.tensor_tensor(keys[:, bass.ds(c * GA * P, GA * P)], ps_m[:], keyval[:, bass.ds(c * GA * P, GA * P)], ALU.mult)\
                      .then_inc(key_done, 1)
                    step.end(OWN)

                with v.Fori(0, NC // 2) as i:
                    v.wait_ge(rows_out, START + 64 * i)
                    for par in range(2):
                        normalize(2 * i + par, par)
                    for par in range(2):
                        choose(2 * i + par, par)
                step.begin(2 * NT + 1 + OWN * NC)
                v.wait_ge(key_done, START + NC)
                for source, dest in ((keys, first), (both, picked)):
                    if source is both:
                        v.wait_ge(first_ready, START + 1)
                        v.wait_ge(firstT_psum, START + 1)
                        nc.vector.tensor_copy(firstT[:], ps_t[0][:, 0:P]).then_inc(firstT_ready, 1)
                        v.wait_ge(both_psum, START + 1)
                        step.done(nc.vector.tensor_copy(both[:], ps_t[1][0:E, 0:2 * CAP]))
                        step.wait()
                    for r in range(CAP // TOPK):
                        ins = nc.vector.max(dest[:, TOPK * r:TOPK * r + TOPK], source[:])
                        if r == CAP // TOPK - 1:
                            ins.then_inc(first_ready if source is keys else picked_ready, 1)
                            continue
                        step.done(ins)
                        step.wait()
                        step.done(nc.vector.match_replace(source[:], dest[:, TOPK * r:TOPK * r + TOPK], source[:], 0.0))
                        step.wait()
                v.wait_ge(picked_psum, START + 1)
                step.done(nc.vector.tensor_scalar(empty[:], ps_l[:, 0:E], 0.0, slot_no[:, 0:1], ALU.is_equal, ALU.mult))
                step.wait()
                step.done(nc.vector.tensor_tensor(token_f[:], empty[:], ps_l[:, 0:E], ALU.subtract))
                step.wait()
                nc.vector.tensor_scalar(slot_token[:], token_f[:], float(T), None, ALU.add).then_inc(slots_ready, 1)
                v.wait_ge(slots_ready, START + 1)

        experts(nc, name + "e", consts, slot_token, gate_up_dram, down_dram, rows_dram, sums_dram, x_res)


def experts(nc, name, consts, slot_token, gate_up_dram, down_dram, rows_dram, sums_dram, x_res):
    ident = consts["ident"]
    STEP, G, R = 16, 4, 8
    ROW = D + E
    with ExitStack() as ctx:
        sb, pb, sem, start = allocators(nc, ctx, name)
        waits_p = sb("waits_p", [P, 1 + STEP // G + STEP], F32)
        slot = [sb(f"slot{j}", [P, 1], I32) for j in range(STEP)]
        rows = [sb(f"rows{j}", [P, ROW], F32) for j in range(R)]
        w_gu = [sb(f"w_gu{j}", [P, KD, 2 * FE], F32) for j in range(R)]
        w_dn = [sb(f"w_dn{j}", [FE, D], F32) for j in range(R)]
        hT = [sb(f"hT{j}", [P, KD * P], F32) for j in range(2)]
        gated = [sb(f"gated{j}", [FE, P], F32) for j in range(2)]
        mid = [sb(f"mid{j}", [FE, P], F32) for j in range(2)]
        weight = [sb(f"weight{j}", [P, 1], F32) for j in range(R)]
        y = [sb(f"y{j}", [P, D], F32) for j in range(R)]
        odd = sb("odd", [P, NT, D], F32)
        ps_t = [pb(f"ps_t{i}", [P, 512], F32) for i in range(2)]
        ps_g = [pb(f"ps_g{i}", [P, 512], F32) for i in range(2)]
        ps_u = [pb(f"ps_u{i}", [P, 512], F32) for i in range(2)]
        ps_y = [pb(f"ps_y{i}", [P, 512], F32) for i in range(2)]
        gathered = [sem(f"gathered{j}", from_zero=True) for j in range(R)]
        added = [sem(f"added{i}", from_zero=True) for i in range(2)]
        w_landed = [sem(f"w_landed{j}") for j in range(R)]
        waits_set, carried = sem("waits_set"), sem("carried")
        slot_ready, hT_psum, hT_ready = sem("slot_ready"), sem("hT_psum"), sem("hT_ready")
        gu_psum, silu_ready, mid_ready, y_psum, y_ready = sem("gu_psum"), sem("silu_ready"), sem("mid_ready"), sem("y_psum"), sem("y_ready")
        weight_ready, back = sem("weight_ready"), [sem(f"back{i}") for i in range(2)]
        block = start()

        def count(n):
            return START + (max(n, 0) if isinstance(n, int) else n)

        def walk(engine, step, tail):
            for m in range(STEP):
                step(0, m, m)
            with engine.Fori(1, E // STEP) as i:
                for m in range(STEP):
                    step(i, STEP * i + m, m)
            tail()

        def wait_added(engine, i, m, back_by):
            n = STEP // 2 * i + (m - back_by) // 2 + 1
            if not isinstance(n, int) or n > 0:
                engine.wait_ge(added[(m - back_by) % 2], 16 * n)

        def is_gathered(engine, i, m):
            engine.wait_ge(gathered[m % R], 16 * (STEP // R * i + m // R + 1))

        @block.sync
        def _(sp):
            def step(i, e, m):
                j = m % R
                sp.wait_ge(y_psum, count(e - R + 1))
                sp.dma_start(w_gu[j][:], gate_up_dram[bass.ds(e, 1)].rearrange("o (k p) f -> p (o k) f", p=P)).then_inc(w_landed[j], 16)
                sp.dma_start(w_dn[j][:], down_dram[bass.ds(e, 1)].rearrange("o f d -> f (o d)")).then_inc(w_landed[j], 16)

            walk(sp, step, lambda: None)
            for par in range(2):
                sp.wait_ge(added[par], 16 * (E // 2))
                sp.dma_start((x_res, odd)[par][:], sums_dram[par][0:T, :].rearrange("(t p) d -> p t d", p=P)).then_inc(back[par], 16)

        @block.gpsimd
        def _(pool):
            PER = STEP + STEP // G

            def before(i):
                return 0 if isinstance(i, int) else PER * i - G

            def gather(i, e, m):
                pool.wait_ge(slot_ready, count(e + G))
                pool.wait_ge(hT_psum, count(e + G - R))
                pool.wait_ge(weight_ready, count(e + G - R))
                carry_on_pool(nc, waits_p, 1 + m // G, carried, before(i))
                for n in range(m, m + G):
                    nc.gpsimd.indirect_dma_start(rows[n % R][:], None, rows_dram, bass.IndirectOffsetOnAxis(slot[n][:, 0:1], 0))\
                      .then_inc(gathered[n % R], 16)

            def scatter(i, e, m, carried_before):
                n = (m - G) % STEP
                pool.wait_ge(y_ready, count(e - G + 1))
                wait_added(pool, i, m, G + 2)
                carry_on_pool(nc, waits_p, 1 + STEP // G + m, carried, carried_before)
                nc.gpsimd.indirect_dma_start(sums_dram[n % 2], bass.IndirectOffsetOnAxis(slot[n][:, 0:1], 0), y[n % R][:], None,
                                             bounds_check=T + P - 1, oob_is_err=True, compute_op=ALU.add).then_inc(added[n % 2], 16)

            def step(i, e, m):
                if m % G == 0:
                    gather(i, e, m)
                if not isinstance(i, int) or m >= G:
                    scatter(i, e, m, before(i))

            def tail():
                for m in range(G):
                    scatter(E // STEP, E + m, m, PER * (E // STEP) - G)
                for par in range(2):
                    pool.wait_ge(added[par], 16 * (E // 2))

            nc.gpsimd.memset(waits_p[:], 0.0).then_inc(waits_set, 1)
            pool.wait_ge(waits_set, START + 1)
            walk(pool, step, tail)

        @block.tensor
        def _(pe):
            def rows_to_features(i, e, m):
                is_gathered(pe, i, m)
                pe.wait_ge(hT_ready, count(e - 1))
                for k in range(KD):
                    mm = nc.tensor.transpose(ps_t[m % 2][:, P * k:P * k + P], rows[m % R][:, P * k:P * k + P], ident[:])
                mm.then_inc(hT_psum, 1)

            def gate_and_up(i, e, m):
                j = m % R
                pe.wait_ge(w_landed[j], START + 32 * (STEP // R * i + m // R + 1))
                pe.wait_ge(hT_ready, count(e + 1))
                pe.wait_ge(mid_ready, count(e - 1))
                for base, ps in ((FE, ps_u), (0, ps_g)):
                    for k in range(KD):
                        mm = nc.tensor.matmul(ps[m % 2][0:FE, 0:P], w_gu[j][:, k, base:base + FE], hT[m % 2][:, P * k:P * k + P],
                                              start=(k == 0), stop=(k == KD - 1))
                mm.then_inc(gu_psum, 1)

            def down(i, e, m):
                pe.wait_ge(mid_ready, count(e + 1))
                pe.wait_ge(y_ready, count(e - 1))
                nc.tensor.matmul(ps_y[m % 2][:, 0:D], mid[m % 2][:], w_dn[m % R][:], start=True, stop=True).then_inc(y_psum, 1)

            def step(i, e, m):
                rows_to_features(i, e, m)
                if not isinstance(i, int) or m >= 1:
                    gate_and_up(i if m >= 1 else i - 1, e - 1, (m - 1) % STEP)
                if not isinstance(i, int) or m >= 2:
                    down(i, e - 2, (m - 2) % STEP)

            def tail():
                gate_and_up(E // STEP - 1, E - 1, STEP - 1)
                down(None, E - 2, STEP - 2)
                down(None, E - 1, STEP - 1)

            walk(pe, step, tail)

        @block.scalar
        def _(act):
            def to_sbuf(i, e, m):
                act.wait_ge(hT_psum, count(e + 1))
                act.wait_ge(gu_psum, count(e - 1))
                nc.scalar.copy(hT[m % 2][:], ps_t[m % 2][:, 0:KD * P]).then_inc(hT_ready, 1)

            def silu(i, e, m):
                act.wait_ge(gu_psum, count(e + 1))
                act.wait_ge(mid_ready, count(e - 1))
                nc.scalar.activation(gated[m % 2][:], ps_g[m % 2][0:FE, 0:P], ACT.Silu).then_inc(silu_ready, 1)

            def step(i, e, m):
                to_sbuf(i, e, m)
                if not isinstance(i, int) or m >= 1:
                    silu(i, e - 1, (m - 1) % STEP)

            walk(act, step, lambda: silu(None, E - 1, STEP - 1))

        @block.vector
        def _(v):
            def slots(i, e, m):
                for n in range(G):
                    wait_added(v, i, m + n, STEP)
                    nc.vector.tensor_copy(slot[m + n][:], slot_token[:, bass.ds(e + n, 1)]).then_inc(slot_ready, 1)

            def middle(i, e, m):
                is_gathered(v, i, m)
                wait_added(v, i, m, R)
                nc.vector.tensor_copy(weight[m % R][:], rows[m % R][:, bass.ds(D + e, 1)]).then_inc(weight_ready, 1)
                v.wait_ge(silu_ready, count(e + 1))
                v.wait_ge(y_psum, count(e - 1))
                nc.vector.tensor_tensor(mid[m % 2][:], gated[m % 2][:], ps_u[m % 2][0:FE, 0:P], ALU.mult).then_inc(mid_ready, 1)

            def weigh(i, e, m):
                v.wait_ge(y_psum, count(e + 1))
                v.wait_ge(weight_ready, count(e + 1))
                nc.vector.tensor_scalar(y[m % R][:], ps_y[m % 2][:, 0:D], weight[m % R][:, 0:1], None, ALU.mult).then_inc(y_ready, 1)

            def step(i, e, m):
                if m % G == 0:
                    slots(i, e, m)
                if not isinstance(i, int) or m >= G:
                    middle(i if m >= G else i - 1, e - G, (m - G) % STEP)
                if not isinstance(i, int) or m >= G + 1:
                    weigh(i, e - G - 1, (m - G - 1) % STEP)

            def tail():
                for m in range(G):
                    middle(E // STEP - 1, E - G + m, STEP - G + m)
                    weigh(None, E - G - 1 + m, STEP - G - 1 + m)
                weigh(None, E - 1, STEP - 1)
                for par in range(2):
                    v.wait_ge(back[par], START + 16)
                for t in range(0, NT, 8):
                    ins = nc.vector.tensor_tensor(x_res[:, t:t + 8, :], x_res[:, t:t + 8, :], odd[:, t:t + 8, :], ALU.add)
                ins.then_inc(back[0], 1)
                v.wait_ge(back[0], START + 17)

            walk(v, step, tail)


def state_space_layer(nc, x_res, consts, w_in_dram, w_out_dram, vec, mats):
    ident = consts["ident"]
    NH, NP_, DI, TAPS = 4, 128, 512, 4
    KI = DI // P
    PROJ = 2 * DI + NH + 2 * P
    DT0, B0, C0 = 2 * DI, 2 * DI + NH, 2 * DI + NH + P
    RMS_EPS = 1e-6
    with ExitStack() as ctx:
        sb, pb, sem, start = allocators(nc, ctx, "ssm")
        w_out = sb("w_out", [P, KI, D], F32)
        cols = sb("cols", [P, KD + 2 * KI + KI * TAPS], F32)
        norm_c = cols[:, 0:KD]
        conv_b = cols[:, KD:KD + KI]
        skip_c = cols[:, KD + KI:KD + 2 * KI]
        conv_w = cols[:, KD + 2 * KI:].rearrange("p (c k) -> p c k", k=TAPS)
        heads = sb("heads", [P, 2, NH], F32)
        upper = sb("upper", [P, P], F32)
        last = sb("last", [P, P], F32)
        waits_p = sb("waits_p", [P, 2], F32)
        hT_all = [sb(f"hT_all_{part}", [P, KD, T], F32R) for part in ("hi", "lo")]
        w_parts = [sb(f"w_in_{part}", [P, KD, PROJ], F32R) for part in ("hi", "lo")]
        dt = sb("dt", [P, NT, NH], F32)
        a_neg = sb("a_neg", [P, NH], F32)
        cum = sb("cum", [P, NT, NH], F32)
        dec_end = sb("dec_end", [P, NT, NH], F32)
        dec_in = sb("dec_in", [P, NT, NH], F32)
        dec_chunk = sb("dec_chunk", [P, NT, NH], F32)

        with ExitStack() as ctx1:
            sb1, pb1, sem1, start = allocators(nc, ctx1, "ssm_a")
            w_in = sb1("w_in", [P, KD, PROJ], F32)
            stats = sb1("stats", [P, NT, 6], F32)
            mv = sb1("mv", [P, NT, 2], F32)
            rstd = sb1("rstd", [P, 3, NT], F32)
            rms = sb1("rms", [P, 4, NT], F32)
            z = sb1("z", [P, NT, NH], F32)
            spl = sb1("spl", [P, 3, NT * NH], F32)
            log_a = sb1("log_a", [P, NT, NH], F32)
            to_end = sb1("to_end", [P, NT, NH], F32)
            h_all = sb1("h_all", [P, NT, D], F32)
            square = sb1("square", [P, 2, D], F32)
            hn = sb1("hn", [P, 2, 2, D], F32)
            hT = sb1("hT", [P, 2, KD, 2 * P], F32)
            ps_t = [pb1(f"ps_t{i}", [P, 512], F32) for i in range(2)]
            ps_d = pb1("ps_d", [P, 512], F32)
            landed, scaled = sem1("landed"), sem1("scaled")
            dve = sem1("dve")
            var_ready, std_ready = sem1("var_ready"), sem1("std_ready")
            h_ready, squared, ms_ready, root_ready = sem1("h_ready"), sem1("squared"), sem1("ms_ready"), sem1("root_ready")
            hn_ready, hT_psum, hT_ready, dt_psum, z_done = sem1("hn_ready"), sem1("hT_psum"), sem1("hT_ready"), sem1("dt_psum"), sem1("z_done")
            kept, added, w_hi, w_lo = sem1("kept"), sem1("added"), sem1("w_hi"), sem1("w_lo")
            z_parts, exp_ready, log_ready = sem1("z_parts"), sem1("exp_ready"), sem1("log_ready")
            la_ready, cum_psum, cum_ready, end_psum, ends_ready, decays = (sem1(n) for n in (
                "la_ready", "cum_psum", "cum_ready", "end_psum", "ends_ready", "decays"))
            block = start()
            LOADS = 6

            @block.sync
            def _(sp):
                sp.dma_start(w_in[:], w_in_dram.rearrange("(k p) n -> p k n", p=P)).then_inc(landed, 16)
                sp.dma_start(w_out[:], w_out_dram.rearrange("(k p) n -> p k n", p=P)).then_inc(landed, 16)
                sp.dma_start(cols[:], vec[0]).then_inc(landed, 16)
                sp.dma_start(heads[:].rearrange("p a h -> p (a h)"), vec[1].partition_broadcast(P)).then_inc(landed, 16)
                sp.dma_start(upper[:], mats[0]).then_inc(landed, 16)
                sp.dma_start(last[:], mats[1]).then_inc(landed, 16)

            @block.tensor
            def _(pe):
                pe.wait_ge(scaled, START + KD)
                with pe.Fori(0, NT // 4) as i:
                    for a in range(2):
                        n = 2 * i + a
                        pe.wait_ge(hn_ready, START + 2 * n + 2)
                        for k in range(KD):
                            for tl in range(2):
                                mm = nc.tensor.transpose(ps_t[a][:, P * (2 * k + tl):P * (2 * k + tl) + P],
                                                         hn[:, a, tl, P * k:P * k + P], ident[:])
                        mm.then_inc(hT_psum, 1)
                    for a in range(2):
                        n = 2 * i + a
                        pe.wait_ge(hT_ready, START + n + 1)
                        for tl in range(2):
                            for k in range(KD):
                                mm = nc.tensor.matmul(ps_d[:, bass.ds(NH * (2 * n + tl), NH)], hT[:, a, k, P * tl:P * tl + P],
                                                      w_in[:, k, DT0:DT0 + NH], start=(k == 0), stop=(k == KD - 1))
                        mm.then_inc(dt_psum, 1)
                pe.wait_ge(la_ready, START + 1)
                nc.tensor.matmul(ps_t[0][:, 0:NT * NH], upper[:], log_a[:].rearrange("p t h -> p (t h)"), start=True, stop=True)\
                  .then_inc(cum_psum, 1)
                pe.wait_ge(cum_ready, START + 1)
                nc.tensor.matmul(ps_t[1][:, 0:NT * NH], last[:], cum[:].rearrange("p t h -> p (t h)"), start=True, stop=True)\
                  .then_inc(end_psum, 1)

            @block.scalar
            def _(act):
                act.wait_ge(var_ready, START + 1)
                nc.scalar.activation(rstd[:, 1], rstd[:, 0], ACT.Sqrt).then_inc(std_ready, 1)
                with act.Fori(0, NT // 2) as i:
                    for par in range(2):
                        n = 2 * i + par
                        act.wait_ge(h_ready, START + n + 1)
                        act.wait_ge(squared, START + 2 * i)
                        nc.scalar.activation(square[:, par, :], one_tile(h_all, n), ACT.Square,
                                             accum_out=rms[:, 0, bass.ds(n, 1)]).then_inc(squared, 1)
                act.wait_ge(ms_ready, START + 1)
                nc.scalar.activation(rms[:, 2], rms[:, 1], ACT.Sqrt).then_inc(root_ready, 1)
                with act.Fori(0, NT // 4) as i:
                    for a in range(2):
                        act.wait_ge(hT_psum, START + 2 * i + a + 1)
                        act.wait_ge(dt_psum, START + 2 * i)
                        act.wait_ge(kept, START + 4 * i)
                        nc.scalar.copy(hT[:, a].rearrange("p k n -> p (k n)"), ps_t[a][:]).then_inc(hT_ready, 1)
                for k in range(KD):
                    act.wait_ge(scaled, START + k + 1)
                    nc.scalar.copy(w_parts[0][:, k, :], w_in[:, k, :]).then_inc(w_hi, 1)
                act.wait_ge(z_parts, START + 1)
                nc.scalar.activation(spl[:, 1], spl[:, 0], ACT.Exp).then_inc(exp_ready, 1)
                nc.scalar.activation(a_neg[:], heads[:, 0, :], ACT.Exp).then_inc(exp_ready, 1)
                act.wait_ge(exp_ready, START + 1)
                nc.scalar.activation(spl[:, 2], spl[:, 1], ACT.Ln, bias=1.0).then_inc(log_ready, 1)
                act.wait_ge(ends_ready, START + 1)
                for out, in_ in ((dec_end, to_end), (dec_in, cum), (dec_chunk, dec_chunk)):
                    nc.scalar.activation(out[:], in_[:], ACT.Exp).then_inc(decays, 1)

            @block.gpsimd
            def _(pool):
                nc.gpsimd.memset(waits_p[:], 0.0).then_inc(added, 1)
                with pool.Fori(0, NT // 4) as i:
                    pool.wait_ge(h_ready, START + 4 * i + 4)
                    four = slice_of(x_res, 4 * i, 4)
                    nc.gpsimd.tensor_tensor(four, four, slice_of(h_all, 4 * i, 4), ALU.add).then_inc(added, 1)
                for k in range(KD):
                    pool.wait_ge(w_hi, START + k + 1)
                    nc.gpsimd.tensor_tensor(w_parts[1][:, k, :], w_in[:, k, :], w_parts[0][:, k, :].bitcast(F32), ALU.subtract)\
                      .then_inc(w_lo, 1)

            @block.vector
            def _(v):
                v.wait_ge(landed, START + 16 * LOADS)
                for k in range(KD):
                    nc.vector.tensor_scalar(w_in[:, k, :], w_in[:, k, :], norm_c[:, k:k + 1], None, ALU.mult).then_inc(scaled, 1)
                layer_norm_statistics(nc, v, x_res, stats, mv, rstd, dve, var_ready, std_ready)
                step = Steps(v, dve)
                with v.Fori(0, NT // 4) as i:
                    for j in range(4):
                        n = 4 * i + j
                        nc.vector.tensor_scalar(one_tile(h_all, n), one_tile(x_res, n), mean_of(mv, n), rstd_of(rstd, n),
                                                ALU.subtract, ALU.mult).then_inc(h_ready, 1)
                v.wait_ge(squared, START + NT)
                v.wait_ge(h_ready, START + NT)
                nc.vector.tensor_scalar(rms[:, 1], rms[:, 0], 1.0 / D, RMS_EPS, ALU.mult, ALU.add).then_inc(ms_ready, 1)
                v.wait_ge(root_ready, START + 1)
                step.begin(2 * NT + 1)
                step.done(nc.vector.reciprocal(rms[:, 3], rms[:, 2]))
                step.wait()
                with v.Fori(0, NT // 4) as i:
                    v.wait_ge(hT_psum, START + 2 * i)
                    for t in range(4):
                        nc.vector.tensor_scalar(hn[:, t // 2, t % 2, :], one_tile(h_all, 4 * i + t), rms[:, 3, bass.ds(4 * i + t, 1)], None, ALU.mult)\
                          .then_inc(hn_ready, 1)
                    for a in range(2):
                        v.wait_ge(hT_ready, START + 2 * i + a + 1)
                        tokens = bass.ds((4 * i + 2 * a) * P, 2 * P)
                        nc.vector.tensor_copy(hT_all[0][:, :, tokens], hT[:, a]).then_inc(kept, 1)
                        v.wait_ge(kept, START + 4 * i + 2 * a + 1)
                        nc.vector.tensor_tensor(hT_all[1][:, :, tokens], hT[:, a], hT_all[0][:, :, tokens].bitcast(F32), ALU.subtract)\
                          .then_inc(kept, 1)
                v.wait_ge(dt_psum, START + NT // 2)
                nc.vector.tensor_tensor(z[:], ps_d[:, 0:NT * NH].rearrange("p (t h) -> p t h", h=NH),
                                        heads[:, 1, :].unsqueeze(1).to_broadcast([P, NT, NH]), ALU.add).then_inc(z_done, 1)
                v.wait_ge(z_done, START + 1)
                zf = z[:].rearrange("p t h -> p (t h)")
                step.done(nc.vector.tensor_scalar(spl[:, 1], zf, -1.0, None, ALU.mult))
                step.wait()
                nc.vector.tensor_tensor(spl[:, 0], zf, spl[:, 1], ALU.min).then_inc(z_parts, 1)
                v.wait_ge(log_ready, START + 1)
                dtf, laf = dt[:].rearrange("p t h -> p (t h)"), log_a[:]
                step.done(nc.vector.scalar_tensor_tensor(dtf, zf, 0.0, spl[:, 2], ALU.max, ALU.add))
                step.wait()
                v.wait_ge(exp_ready, START + 2)
                nc.vector.scalar_tensor_tensor(laf, dt[:], -1.0, a_neg[:].unsqueeze(1).to_broadcast([P, NT, NH]), ALU.mult, ALU.mult)\
                  .then_inc(la_ready, 1)
                v.wait_ge(cum_psum, START + 1)
                nc.vector.tensor_copy(cum[:].rearrange("p t h -> p (t h)"), ps_t[0][:, 0:NT * NH]).then_inc(cum_ready, 1)
                v.wait_ge(end_psum, START + 1)
                v.wait_ge(cum_ready, START + 1)
                end = ps_t[1][:, 0:NT * NH]
                step.done(nc.vector.tensor_tensor(to_end[:].rearrange("p t h -> p (t h)"), end, cum[:].rearrange("p t h -> p (t h)"),
                                                  ALU.subtract))
                nc.vector.tensor_copy(dec_chunk[:].rearrange("p t h -> p (t h)"), end).then_inc(ends_ready, 1)
                v.wait_ge(decays, START + 3)

        with ExitStack() as ctx2:
            sb2, pb2, sem2, start = allocators(nc, ctx2, "ssm_b")
            HALF = S // 2
            CH = HALF // P
            HIST = TAPS - 1
            gate = sb2("gate", [P, 2, KI, HALF], F32)
            u = sb2("u", [P, 2, KI, HIST + HALF], F32)
            xs = sb2("xs", [P, 2, KI, HALF], F32)
            bT = sb2("bT", [P, 2, HALF], F32)
            cT = sb2("cT", [P, 2, HALF], F32)
            acc = sb2("acc", [P, 2, HALF], F32)
            state = sb2("state", [P, NH, NP_], F32)
            b_tok = sb2("b_tok", [P, P], F32)
            x_dt = sb2("x_dt", [P, NH, NP_], F32)
            x_end = sb2("x_end", [P, NH, NP_], F32)
            diff = sb2("diff", [P, NH, P], F32)
            decay = sb2("decay", [P, NH, P], F32)
            cb = sb2("cb", [P, P], F32)
            cum_c = sb2("cum_c", [P, NH], F32)
            mix = sb2("mix", [P, NH, P], F32)
            y_in = sb2("y_in", [P, NH, NP_], F32)
            y_tok = sb2("y_tok", [P, NH, NP_], F32)
            yT = sb2("yT", [P, NH, P], F32)
            zT = sb2("zT", [P, NH, P], F32)
            ps_x, ps_b, ps_r, ps_y, ps_i, ps_s, ps_p0, ps_p1 = (pb2(f"ps{i}", [P, 512], F32) for i in range(8))
            ps_p = (ps_p0, ps_p1)
            dve = sem2("dve")
            proj_psum, proj_read = sem2("proj_psum"), sem2("proj_read")
            conv_ready, conv_done = sem2("conv_ready"), sem2("conv_done")
            x_psum, bc_psum, row_psum, diff_ready, decay_ready = (sem2(n) for n in ("x_psum", "bc_psum", "row_psum", "diff_ready", "decay_ready"))
            cum_c_ready, carried, state_used = sem2("cum_c_ready"), sem2("carried"), sem2("state_used")
            cb_ready, mix_ready, xdt_ready, xend_ready, state_ready = (sem2(n) for n in ("cb_ready", "mix_ready", "xdt_ready", "xend_ready", "state_ready"))
            intra_psum, inter_psum, local_psum, y_ready = (sem2(n) for n in ("intra_psum", "inter_psum", "local_psum", "y_ready"))
            yT_psum, yT_ready, zT_ready, out_psum, x_done = (sem2(n) for n in ("yT_psum", "yT_ready", "zT_ready", "out_psum", "x_done"))
            block = start()
            gate_unit = lambda c: (c * P, "gate", c)
            u_unit = lambda c: (DI + c * P, "u", c)
            UNITS = ([u_unit(0), u_unit(1), u_unit(2)], [u_unit(3), (B0, "b", 0), (C0, "c", 0)],
                     [gate_unit(0), gate_unit(1)], [gate_unit(2), gate_unit(3)])
            NU = sum(len(us) for us in UNITS)
            before_units = [sum(len(us) for us in UNITS[:c]) for c in range(CH)]
            CONV = ((), (0, 1), (2, 3), ())

            def of_heads(values, n):
                return values[:, bass.ds(n, 1), :].rearrange("p o h -> p (o h)").unsqueeze(2).to_broadcast([P, NH, NP_])

            def halves(engine, project, scan, end):
                def sequence(b, final):
                    for half in range(2):
                        for c in range(CH):
                            closing = final and half == 1
                            scan(b, half, c, (lambda: None) if closing else (lambda: project(2 * b + half + 1, 1 - half, c)),
                                 not (closing and c == CH - 1))
                    end(b)

                for c in range(CH):
                    project(0, 0, c)
                with engine.Fori(0, B - 1) as b:
                    sequence(b, False)
                sequence(B - 1, True)

            @block.tensor
            def _(pe):
                def project(hh, par, c):
                    for n, (col, kind, _) in enumerate(UNITS[c]):
                        unit = before_units[c] + n
                        if unit >= 2:
                            pe.wait_ge(proj_read, START + NU * hh + unit - 1)
                        else:
                            pe.wait_ge(proj_read, START + NU * hh)
                        for k in range(KD):
                            mm = three(nc, ps_p[unit % 2][:], [w[:, k, col:col + P] for w in w_parts],
                                       [h[:, k, bass.ds(hh * HALF, HALF)] for h in hT_all], k == 0, k == KD - 1)
                        mm.then_inc(proj_psum, 1)

                def spread(n, par, c):
                    tok = slice(P * c, P * c + P)
                    if c == 0:
                        hh = 2 * (n[0]) + par
                        pe.wait_ge(conv_done, START + KI * (hh + 1))
                        pe.wait_ge(proj_read, START + NU * hh + before_units[2])
                    n = TS * n[0] + CH * par + c
                    pe.wait_ge(yT_ready, START + (n if c == 0 and par == 0 else n - 1))
                    for h in range(NH):
                        mm = nc.tensor.transpose(ps_x[:, P * h:P * h + P], xs[:, par, h, tok], ident[:])
                    mm.then_inc(x_psum, 1)
                    pe.wait_ge(diff_ready, START + n)
                    pe.wait_ge(cum_c_ready, START + n + 1)
                    for h in range(NH):
                        mm = nc.tensor.transpose(ps_r[:, P * h:P * h + P], cum_c[:, h:h + 1].to_broadcast([P, P]), ident[:])
                    mm.then_inc(row_psum, 1)
                    pe.wait_ge(cb_ready, START + n)
                    if c == 0 and par == 0:
                        pe.wait_ge(x_done, START + n)
                    else:
                        pe.wait_ge(x_done, START + n - 1)
                    nc.tensor.transpose(ps_b[:, 0:P], bT[:, par, tok], ident[:])
                    nc.tensor.matmul(ps_b[:, P:2 * P], bT[:, par, tok], cT[:, par, tok], start=True, stop=True).then_inc(bc_psum, 1)

                def output(n):
                    pe.wait_ge(zT_ready, START + n + 1)
                    pe.wait_ge(x_done, START + n)
                    for h in range(NH):
                        mm = nc.tensor.matmul(ps_b[:, 2 * P:2 * P + D], zT[:, h, :], w_out[:, h, :], start=(h == 0), stop=(h == NH - 1))
                    mm.then_inc(out_psum, 1)

                def scan(b, half, c, project, more):
                    n = TS * b + CH * half + c
                    if half == 0 and c == 0:
                        spread((b,), 0, 0)
                    pe.wait_ge(y_ready, START + n)
                    pe.wait_ge(state_ready, START + (TS + 1) * b + CH * half + c + 1)
                    nc.tensor.matmul(ps_i[:], cT[:, half, P * c:P * c + P], state[:].rearrange("p h d -> p (h d)"), start=True, stop=True)\
                      .then_inc(inter_psum, 1)
                    pe.wait_ge(xend_ready, START + n + 1)
                    pe.wait_ge(cb_ready, START + n + 1)
                    pe.wait_ge(state_ready, START + (TS + 1) * b + CH * half + c + 1)
                    nc.tensor.matmul(ps_s[:], b_tok[:], x_end[:].rearrange("p h d -> p (h d)"), start=True, stop=True).then_inc(local_psum, 1)
                    pe.wait_ge(mix_ready, START + n + 1)
                    pe.wait_ge(xdt_ready, START + n + 1)
                    for h in range(NH):
                        mm = nc.tensor.matmul(ps_y[:, P * h:P * h + P], mix[:, h, :], x_dt[:, h, :], start=True, stop=True)
                    mm.then_inc(intra_psum, 1)
                    if not (half == 0 and c == 0):
                        output(n - 1)
                    if c < CH - 1:
                        spread((b,), half, c + 1)
                    elif half == 0:
                        spread((b,), 1, 0)
                    project()
                    pe.wait_ge(y_ready, START + n + 1)
                    pe.wait_ge(xdt_ready, START + n + (1 if half == 1 and c == CH - 1 else 2))
                    for h in range(NH):
                        mm = nc.tensor.transpose(ps_x[:, P * h:P * h + P], y_tok[:, h, :], ident[:])
                    mm.then_inc(yT_psum, 1)

                halves(pe, project, scan, lambda b: output(TS * b + TS - 1))

            @block.scalar
            def _(act):
                def project(hh, par, c):
                    for tile in CONV[c]:
                        act.wait_ge(conv_ready, START + KI * hh + tile + 1)
                        nc.scalar.activation(xs[:, par, tile, :], acc[:, tile % 2, :], ACT.Silu).then_inc(conv_done, 1)
                    for n, (_, kind, tile) in enumerate(UNITS[c]):
                        unit = before_units[c] + n
                        act.wait_ge(proj_psum, START + NU * hh + unit + 1)
                        bank = ps_p[unit % 2]
                        if c == 0 and n == 0:
                            act.wait_ge(zT_ready, START + earlier(CH * hh - CH))
                            act.wait_ge(inter_psum, START + earlier(CH * hh - CH))
                            act.wait_ge(bc_psum, START + earlier(CH * hh - CH))
                            act.wait_ge(conv_ready, START + KI * hh)
                        if kind == "gate":
                            ins = nc.scalar.activation(gate[:, par, tile, :], bank[:], ACT.Silu)
                        elif kind == "u":
                            ins = nc.scalar.copy(u[:, par, tile, HIST:], bank[:])
                        else:
                            ins = nc.scalar.copy((bT if kind == "b" else cT)[:, par, :], bank[:])
                        ins.then_inc(proj_read, 1)

                def earlier(n):
                    return max(n, 0) if isinstance(n, int) else n

                def exponentials(n):
                    act.wait_ge(diff_ready, START + n + 1)
                    act.wait_ge(mix_ready, START + n)
                    nc.scalar.activation(decay[:], diff[:], ACT.Exp).then_inc(decay_ready, 1)

                def scan(b, half, c, project, more):
                    n = TS * b + CH * half + c
                    if half == 0 and c == 0:
                        exponentials(n)
                    if not (half == 1 and c == CH - 1):
                        exponentials(n + 1)
                    project()

                halves(act, project, scan, lambda b: None)

            @block.gpsimd
            def _(pool):
                def gated(b, c):
                    n = TS * b + c
                    pool.wait_ge(yT_ready, START + n + 1)
                    pool.wait_ge(out_psum, START + n)
                    pool.wait_ge(proj_read, START + NU * (2 * b + c // CH + 1))
                    at = P * (c % CH)
                    nc.gpsimd.tensor_tensor(zT[:], yT[:], gate[:, c // CH, :, at:at + P], ALU.mult).then_inc(zT_ready, 1)

                with pool.Fori(0, B) as b:
                    for c in range(TS):
                        n = TS * b + c
                        pool.wait_ge(row_psum, START + n)
                        carry_on_pool(nc, waits_p, 1, carried, n)
                        nc.gpsimd.tensor_copy(cum_c[:], cum[:, bass.ds(n, 1), :].rearrange("p o h -> p (o h)")).then_inc(cum_c_ready, 1)
                        pool.wait_ge(xdt_ready, START + n + 1)
                        pool.wait_ge(local_psum, START + n)
                        nc.gpsimd.tensor_tensor(x_end[:], x_dt[:], of_heads(dec_end, n), ALU.mult).then_inc(xend_ready, 1)
                        if c > 0:
                            gated(b, c - 1)
                    gated(b, TS - 1)

            @block.vector
            def _(v):
                step = Steps(v, dve)
                OWN = 2 * (KI * (TAPS - 1)) + 1
                nc.vector.memset(u[:, 0, :, 0:HIST], 0.0).then_inc(dve, 1)
                v.wait_ge(dve, START + 1)

                def inputs(n):
                    v.wait_ge(x_psum, START + n + 1)
                    v.wait_ge(intra_psum, START + n)
                    v.wait_ge(xend_ready, START + n)
                    nc.vector.tensor_tensor(x_dt[:], ps_x[:].rearrange("p (h d) -> p h d", h=NH), of_heads(dt, n), ALU.mult)\
                      .then_inc(xdt_ready, 1)
                    v.wait_ge(bc_psum, START + n + 1)
                    v.wait_ge(local_psum, START + n)
                    nc.vector.tensor_copy(b_tok[:], ps_b[:, 0:P])
                    nc.vector.tensor_tensor(cb[:], ps_b[:, P:2 * P], upper[:], ALU.mult).then_inc(cb_ready, 1)
                    v.wait_ge(row_psum, START + n + 1)
                    v.wait_ge(decay_ready, START + n)
                    for h in range(NH):
                        ins = nc.vector.tensor_scalar(diff[:, h, :], ps_r[:, P * h:P * h + P], cum[:, bass.ds(n, 1), h:h + 1].rearrange("p o h -> p (o h)"),
                                                      0.0, ALU.subtract, ALU.min)
                    ins.then_inc(diff_ready, 1)

                def project(hh, par, c):
                    for tile in CONV[c]:
                        v.wait_ge(proj_read, START + NU * hh + (tile + 1))
                        if tile == 0 and par == 1:
                            v.wait_ge(proj_read, START + NU * hh)
                            step.done(nc.vector.tensor_copy(u[:, 1, :, 0:HIST], u[:, 0, :, HALF:HALF + HIST]))
                            step.wait()
                        v.wait_ge(conv_done, START + KI * hh + max(tile - 1, 0))
                        for k in range(TAPS):
                            tap = u[:, par, tile, k:k + HALF]
                            to = acc[:, tile % 2, :]
                            if k == 0:
                                step.done(nc.vector.tensor_scalar(to, tap, conv_w[:, tile, 0:1], conv_b[:, tile:tile + 1], ALU.mult, ALU.add))
                                step.wait()
                                continue
                            ins = nc.vector.scalar_tensor_tensor(to, tap, conv_w[:, tile, k:k + 1], to, ALU.mult, ALU.add)
                            if k < TAPS - 1:
                                step.done(ins)
                                step.wait()
                            else:
                                ins.then_inc(conv_ready, 1)

                def add(n):
                    v.wait_ge(out_psum, START + n + 1)
                    nc.vector.tensor_tensor(one_tile(x_res, n), one_tile(x_res, n), ps_b[:, 2 * P:2 * P + D], ALU.add).then_inc(x_done, 1)

                def scan(b, half, c, project, more):
                    n = TS * b + CH * half + c
                    if half == 0 and c == 0:
                        step.begin(1 + KI * (TAPS - 1) + OWN * b)
                        v.wait_ge(inter_psum, START + n)
                        v.wait_ge(state_ready, START + (TS + 1) * b)
                        nc.vector.memset(state[:], 0.0).then_inc(state_ready, 1)
                        inputs(n)
                    v.wait_ge(decay_ready, START + n + 1)
                    v.wait_ge(cb_ready, START + n + 1)
                    v.wait_ge(intra_psum, START + n)
                    nc.vector.tensor_tensor(mix[:], decay[:], cb[:].unsqueeze(1).to_broadcast([P, NH, P]), ALU.mult).then_inc(mix_ready, 1)
                    v.wait_ge(inter_psum, START + n + 1)
                    nc.vector.tensor_tensor(y_in[:], ps_i[:].rearrange("p (h d) -> p h d", h=NH), of_heads(dec_in, n), ALU.mult).then_inc(state_used, 1)
                    v.wait_ge(local_psum, START + n + 1)
                    v.wait_ge(state_ready, START + (TS + 1) * b + CH * half + c + 1)
                    for h in range(NH):
                        ins = nc.vector.scalar_tensor_tensor(state[:, h, :], state[:, h, :], dec_chunk[:, bass.ds(n, 1), h:h + 1].rearrange("p o h -> p (o h)"),
                                                             ps_s[:, P * h:P * h + P], ALU.mult, ALU.add)
                    ins.then_inc(state_ready, 1)
                    v.wait_ge(state_used, START + n + 1)
                    v.wait_ge(intra_psum, START + n + 1)
                    v.wait_ge(yT_psum, START + n)
                    nc.vector.tensor_tensor(y_tok[:], y_in[:], ps_y[:].rearrange("p (h d) -> p h d", h=NH), ALU.add).then_inc(y_ready, 1)
                    project()
                    if not (half == 0 and c == 0):
                        add(n - 1)
                    if not (half == 1 and c == CH - 1):
                        inputs(n + 1)
                    v.wait_ge(yT_psum, START + n + 1)
                    v.wait_ge(zT_ready, START + n)
                    for h in range(NH):
                        ins = nc.vector.scalar_tensor_tensor(yT[:, h, :], xs[:, half, h, P * c:P * c + P], skip_c[:, h:h + 1],
                                                             ps_x[:, P * h:P * h + P], ALU.mult, ALU.add)
                    ins.then_inc(yT_ready, 1)

                def end(b):
                    add(TS * b + TS - 1)
                    if not isinstance(b, int):
                        step.end(OWN)

                step.begin(1)
                halves(v, project, scan, end)

def load_phase(nc, x_dram, const_dram, x_res, consts):
    with ExitStack() as ctx:
        sb, pb, sem, start = allocators(nc, ctx, "load")
        masks = sb("masks", [P, 3, P], F32)
        landed, copied = sem("landed"), sem("copied")
        block = start()

        @block.sync
        def _(sp):
            sp.dma_start(consts["ident"][:], const_dram[0]).then_inc(landed, 16)
            sp.dma_start(masks[:], const_dram[0:3].rearrange("m p n -> p m n")).then_inc(landed, 16)
            sp.dma_start(x_res[:], x_dram.rearrange("(t p) d -> p t d", p=P)).then_inc(landed, 16)
            sp.wait_ge(landed, START + 48)

        @block.vector
        def _(v):
            v.wait_ge(landed, START + 48)
            for i, what in enumerate(("ident_b", "causal_q", "causal_k")):
                nc.vector.tensor_copy(consts[what][:], masks[:, i, :]).then_inc(copied, 1)
            v.wait_ge(copied, START + 3)


def store_phase(nc, x_res, out_dram):
    with ExitStack() as ctx:
        sb, pb, sem, start = allocators(nc, ctx, "store")
        stored = sem("stored")
        block = start()

        @block.sync
        def _(sp):
            sp.dma_start(out_dram.rearrange("(t p) d -> p t d", p=P), x_res[:]).then_inc(stored, 16)
            sp.wait_ge(stored, START + 16)


def program(nc, a, out):
    moe_rows = nc.dram_tensor("moe_rows", [T + P, D + E], F32).ap()
    moe_sums = [nc.dram_tensor(f"moe_sums{i}", [T + P, D], F32).ap() for i in range(2)]
    with ExitStack() as ctx:
        def sb(what, shape, dt):
            return ctx.enter_context(nc.sbuf_tensor(what, shape, dt))

        x_res = sb("x_res", [P, NT, D], F32)
        consts = {"ident": sb("ident", [P, P], F32), "ident_b": sb("ident_b", [P, P], BF16),
                  "causal_q": sb("causal_q", [P, P], BF16), "causal_k": sb("causal_k", [P, P], BF16)}
        load_phase(nc, a["x"], a["masks"], x_res, consts)
        attention_layer(nc, "attn1", x_res, consts, a["wqkv1"], a["wo1"], a["rope"])
        with ExitStack() as mlp:
            w_ug = mlp.enter_context(nc.sbuf_tensor("w_ug", [P, KD, 2 * INTER], F32))
            w_dn = mlp.enter_context(nc.sbuf_tensor("w_dn", [P, INTER // P, D], F32))
            mlp_weights(nc, w_ug, w_dn, a["wug"], a["wdn"], a["had"], a["su_ug"], a["scale_ug"], a["su_dp"], a["scale_dp"])
            mlp_layer(nc, "mlp1", x_res, consts, w_ug, w_dn)
            attention_layer(nc, "attn2", x_res, consts, a["wqkv2"], a["wo2"], None)
            mlp_layer(nc, "mlp2", x_res, consts, w_ug, w_dn)
        attention_layer(nc, "attn3", x_res, consts, a["wqkv3"], a["wo3"], None)
        moe_layer(nc, "moe1", x_res, consts, a["router"], a["gate_up"], a["down"], a["keyval"], a["slot_no"], moe_rows, moe_sums)
        state_space_layer(nc, x_res, consts, a["ssm_in"], a["ssm_out"], (a["ssm_cols"], a["ssm_heads"]), a["ssm_mats"])
        moe_layer(nc, "moe2", x_res, consts, a["router"], a["gate_up"], a["down"], a["keyval"], a["slot_no"], moe_rows, moe_sums)
        store_phase(nc, x_res, out)


def layouts(i):
    def grouped(wq, wk, wv):
        w = np.stack([wq.T, wk.T, wv.T], axis=1).reshape(D, 3, NG, HG * DH)
        return w.transpose(0, 2, 1, 3).reshape(D, NG * GW)

    row, col = np.arange(P)[:, None], np.arange(P)[None, :]
    masks = np.stack([row == col, np.where(col > row, MASKED, 0.0), np.where(row > col, MASKED, 0.0)])
    freq = (10000.0 ** (-2.0 * np.arange(DH // 2, dtype=np.float32) / DH)).astype(np.float32)
    ang = np.arange(S, dtype=np.float32)[:, None] * freq[None, :]
    rope = np.stack([np.tile(np.repeat(f(ang), 2, axis=-1), (1, 2 * HG)) for f in (np.cos, np.sin)])
    def columns(v):
        return v.reshape(-1, P).T

    had = np.array([[1.0]])
    while had.shape[0] < P:
        had = np.block([[had, had], [had, -had]])
    had = np.stack([had / 16, -had / 16, had / 32, -had / 32])
    x = i["L0_attn_a_x"].reshape(T, D)
    token = np.arange(T).reshape(2, 1, T // 2) + np.zeros((1, E, 1), np.int64)
    qkv2 = np.split(i["L0_attn_b_W_qkv"], 3, axis=0)
    d = {
        "x": x, "masks": masks.astype(np.float32), "rope": rope.astype(np.float32),
        "wqkv1": grouped(i["L0_attn_a_wq"], i["L0_attn_a_wk"], i["L0_attn_a_wv"]), "wo1": i["L0_attn_a_wo"].T,
        "keyval": (T - token).reshape(P, T // 2).astype(np.float32), "slot_no": np.arange(P, dtype=np.float32)[:, None], "router": i["L1_ffn_router_weight"].T,
        "gate_up": i["L1_ffn_gate_up_proj"], "down": i["L1_ffn_down_proj"],
        "ssm_in": i["L1_attn_b_in_proj_w"], "ssm_out": i["L1_attn_b_out_proj_w"],
        "ssm_cols": np.concatenate([columns(i["L1_attn_b_norm_scale"]), columns(i["L1_attn_b_conv_bias"]), columns(i["L1_attn_b_D"]),
                                    i["L1_attn_b_conv_weight"].reshape(4, 4, P).transpose(2, 1, 0).reshape(P, 16)], axis=1),
        "ssm_heads": np.concatenate([i["L1_attn_b_A_log"], i["L1_attn_b_dt_bias"]]),
        "ssm_mats": np.stack([row <= col, row + 0 * col == P - 1]).astype(np.float32),
        "wqkv2": grouped(*qkv2), "wo2": i["L0_attn_b_W_out"].T,
        "wqkv3": grouped(i["L1_attn_a_Wq"], i["L1_attn_a_Wk"], i["L1_attn_a_Wv"]), "wo3": i["L1_attn_a_Wo"].T,
        "had": had.astype(np.float32), "wug": np.concatenate([i["L0_ffn_W_up"].T, i["L0_ffn_W_gate"].T], axis=1),
        "wdn": i["L0_ffn_W_down"].T, "su_ug": columns(i["L0_ffn_SU_ug"]), "su_dp": columns(i["L0_ffn_SU_dp"]),
        "scale_ug": i["L0_ffn_Wscale_ug"], "scale_dp": i["L0_ffn_Wscale_dp"],
    }
    return {k: np.ascontiguousarray(v) for k, v in d.items()}


def kernel(**inputs):
    import concourse.bacc as bacc
    from concourse.bass_utils import run_bass_kernel_spmd

    arrays = layouts({name: np.asarray(a) for name, a in inputs.items()})
    nc = bacc.Bacc("TRN2", target_bir_lowering=False, num_devices=1)
    a = {name: nc.dram_tensor(f"in_{name}", v.shape, mybir.dt.from_np(v.dtype), kind="ExternalInput").ap()
         for name, v in arrays.items()}
    out = nc.dram_tensor("out", (T, D), F32, kind="ExternalOutput").ap()
    program(nc, a, out)
    r = run_bass_kernel_spmd(nc, [{f"in_{name}": v for name, v in arrays.items()}], core_ids=[0])
    return r.results[0]["out"].reshape(B, S, D)
```
